# Optimizing a Trainium2 kernel written in Bass

```python
import numpy as np
import jax
import jax.numpy as jnp

def _softmax(x, axis=-1):
    return jax.nn.softmax(x, axis=axis)

def _gelu(x):
    return jax.nn.gelu(x, approximate=True)

def _silu(x):
    return jax.nn.silu(x)

def _sigmoid(x):
    return jax.nn.sigmoid(x)

def _layernorm(x, axis=-1, eps=1e-05):
    m = jnp.mean(x, axis=axis, keepdims=True)
    v = jnp.var(x, axis=axis, keepdims=True)
    return (x - m) / jnp.sqrt(v + eps)

def _scatter_add(tgt, idx, src, axis=0):
    return tgt.at[idx].add(src)

def _segment_sum(src, seg, n):
    return jax.ops.segment_sum(src, seg, n)
kernel_name = 'mk_gnn_resnorm_d4_gnn_r8_d2101b'

def setup_inputs(seed: int=0):
    np.random.seed(seed)
    _w = jnp.asarray

    def _rec_inputs():
        import jax
        import jax.numpy as jnp
        _gk = jax.random.key(seed)
        x = -0.0005121 + 1.001 * jax.random.normal(jax.random.fold_in(_gk, 1), (12500, 32), jnp.float32)
        src = jax.random.randint(jax.random.fold_in(_gk, 2), (400000,), 0, 12500, jnp.int32)
        dst = jnp.minimum((12500 * jax.random.uniform(jax.random.fold_in(_gk, 3), (400000,)) ** 2.0).astype(jnp.int32), 99999)
        _o = jnp.argsort(dst, stable=True)
        src = src[_o]
        dst = dst[_o]
        edge_attr_3 = 0.000549083 + 1.00031 * jax.random.normal(jax.random.fold_in(_gk, 11), (400000, 3), jnp.float32)
        edge_attr_32 = 0.000216709 + 1.00012 * jax.random.normal(jax.random.fold_in(_gk, 12), (400000, 32), jnp.float32)
        edge_attr_4 = 0.000714719 + 1.00021 * jax.random.normal(jax.random.fold_in(_gk, 13), (400000, 4), jnp.float32)
        edge_attr_5 = -0.000325185 + 1.00005 * jax.random.normal(jax.random.fold_in(_gk, 14), (400000, 5), jnp.float32)
        edge_attr_8 = jax.random.uniform(jax.random.fold_in(_gk, 15), (400000, 8), jnp.float32, 0.0, 1)
        edge_weight1 = 0.000452788 + 0.999756 * jax.random.normal(jax.random.fold_in(_gk, 17), (400000, 1), jnp.float32)
        return (x, src, dst, edge_attr_3, edge_attr_32, edge_attr_4, edge_attr_5, edge_attr_8, edge_weight1)
    x, src, dst, edge_attr_3, edge_attr_32, edge_attr_4, edge_attr_5, edge_attr_8, edge_weight1 = _rec_inputs()

    def _L0_gnn_setup():
        import jax, jax.numpy as jnp
        import numpy as np
        MUL = 8
        N_NODES = 12500
        N_EDGES = 100000
        EDGE_DIM = 32
        MLP_DIM = 64
        W_NUMEL = 4 * MUL * MUL
        ALPHA = 0.25
        C110 = 1.0 / np.sqrt(3.0)
        SI_SCALE = 1.0 / np.sqrt(MUL)
        key = jax.random.key(seed)
        ks = jax.random.split(key, 10)
        node_attr = jax.random.normal(ks[0], (N_NODES, 4 * MUL), dtype=jnp.float32)
        edge_index = jax.random.randint(ks[1], (2, N_EDGES), 0, N_NODES, dtype=jnp.int64)
        edge_sh = jax.random.normal(ks[2], (N_EDGES, 4), dtype=jnp.float32)
        edge_feat = jax.random.normal(ks[3], (N_EDGES, EDGE_DIM), dtype=jnp.float32)
        W1 = jax.random.normal(ks[4], (EDGE_DIM, MLP_DIM), dtype=jnp.float32) / np.sqrt(EDGE_DIM)
        b1 = jnp.zeros((MLP_DIM,), dtype=jnp.float32)
        W2 = jax.random.normal(ks[5], (MLP_DIM, W_NUMEL), dtype=jnp.float32) / np.sqrt(MLP_DIM)
        b2 = jnp.zeros((W_NUMEL,), dtype=jnp.float32)
        si_w0 = jax.random.normal(ks[6], (MUL, MUL), dtype=jnp.float32)
        si_w1 = jax.random.normal(ks[7], (MUL, MUL), dtype=jnp.float32)
        return {'node_attr': node_attr, 'edge_index': edge_index, 'edge_sh': edge_sh, 'edge_feat': edge_feat, 'W1': W1, 'b1': b1, 'W2': W2, 'b2': b2, 'si_w0': si_w0, 'si_w1': si_w1}
    _L0_gnn_all = _L0_gnn_setup()
    _L0_gnn_in = {k: v for k, v in _L0_gnn_all.items() if k in ('W1', 'b1', 'W2', 'b2', 'si_w0', 'si_w1')}
    del _L0_gnn_all

    def _L1_gnn_setup():
        import jax, jax.numpy as jnp
        import numpy as np
        import math
        M = 8
        COMBOS = [(0, 0, 0), (0, 1, 1), (1, 0, 1), (1, 1, 0), (1, 1, 1), (2, 1, 1)]

        def _cg_coeff(j1, m1, j2, m2, j3, m3):
            if m3 != m1 + m2:
                return 0.0
            f = math.factorial
            vmin = max(0, j2 - j3 - m1, j1 + m2 - j3)
            vmax = min(j1 + j2 - j3, j1 - m1, j2 + m2)
            pref = (2 * j3 + 1) * f(j3 + j1 - j2) * f(j3 - j1 + j2) * f(j1 + j2 - j3) / f(j1 + j2 + j3 + 1)
            pref *= f(j3 + m3) * f(j3 - m3) * f(j1 - m1) * f(j1 + m1) * f(j2 - m2) * f(j2 + m2)
            s = 0.0
            for v in range(vmin, vmax + 1):
                s += (-1) ** v / (f(v) * f(j1 + j2 - j3 - v) * f(j1 - m1 - v) * f(j2 + m2 - v) * f(j3 - j2 + m1 + v) * f(j3 - j1 - m2 + v))
            return math.sqrt(pref) * s

        def _su2_cg(l1, l2, l3):
            C = np.zeros((2 * l1 + 1, 2 * l2 + 1, 2 * l3 + 1), dtype=np.complex128)
            for m1 in range(-l1, l1 + 1):
                for m2 in range(-l2, l2 + 1):
                    m3 = m1 + m2
                    if -l3 <= m3 <= l3:
                        C[m1 + l1, m2 + l2, m3 + l3] = _cg_coeff(l1, m1, l2, m2, l3, m3)
            return C

        def _qmat(l):
            q = np.zeros((2 * l + 1, 2 * l + 1), dtype=np.complex128)
            for m in range(-l, 0):
                q[l + m, l + abs(m)] = 1 / np.sqrt(2)
                q[l + m, l - abs(m)] = -1j / np.sqrt(2)
            q[l, l] = 1.0
            for m in range(1, l + 1):
                q[l + m, l + abs(m)] = (-1) ** m / np.sqrt(2)
                q[l + m, l - abs(m)] = 1j * (-1) ** m / np.sqrt(2)
            return (-1j) ** l * q

        def _so3_cg(l1, l2, l3):
            C = np.einsum('ij,kl,mn,ikn->jlm', _qmat(l1), _qmat(l2), np.conj(_qmat(l3)).T, _su2_cg(l1, l2, l3))
            assert np.abs(C.imag).max() < 1e-06
            C = C.real
            return C / np.linalg.norm(C)
        CG = {c: jnp.asarray(_so3_cg(*c), dtype=jnp.float32) for c in COMBOS}
        N, E = (12500, 200000)
        ks = jax.random.split(jax.random.key(seed), 6)
        return {'node_irreps': jax.random.normal(ks[0], (N, 4 * M), jnp.float32), 'edge_index': jax.random.randint(ks[1], (2, E), 0, N, dtype=jnp.int32), 'sh0': jax.random.normal(ks[2], (E, 1), jnp.float32), 'sh1': jax.random.normal(ks[3], (E, 3), jnp.float32), 'sh2': jax.random.normal(ks[4], (E, 5), jnp.float32), 'W': jax.random.normal(ks[5], (len(COMBOS), M, M), jnp.float32)}
    _L1_gnn_all = _L1_gnn_setup()
    _L1_gnn_in = {k: v for k, v in _L1_gnn_all.items() if k in ('W',)}
    del _L1_gnn_all

    def _L2_gnn_setup():
        import jax, jax.numpy as jnp
        import numpy as np
        N_NODES = 12500
        N_EDGES = 200000
        EMB = 32
        HID = 64

        def gcn_conv(x, W, b, row, col, n_nodes):
            xw = x @ W
            ones = jnp.ones(row.shape[0], dtype=x.dtype)
            deg = jax.ops.segment_sum(ones, col, num_segments=n_nodes)
            dinv = jnp.where(deg > 0, jax.lax.rsqrt(deg), 0.0)
            norm = dinv[row] * dinv[col]
            msgs = norm[:, None] * xw[row]
            out = jax.ops.segment_sum(msgs, col, num_segments=n_nodes)
            return out + b
        key = jax.random.key(seed)
        k1, k2, k3, k4, k5, k6 = jax.random.split(key, 6)
        x = jax.random.normal(k1, (N_NODES, EMB), dtype=jnp.float32)
        edge_index = jax.random.randint(k2, (2, N_EDGES), 0, N_NODES, dtype=jnp.int64)
        W1 = jax.random.normal(k3, (EMB, HID), dtype=jnp.float32) / np.sqrt(EMB)
        b1 = jnp.zeros((HID,), dtype=jnp.float32)
        W2 = jax.random.normal(k4, (HID, EMB), dtype=jnp.float32) / np.sqrt(HID)
        b2 = jnp.zeros((EMB,), dtype=jnp.float32)
        return {'x': x, 'edge_index': edge_index, 'W1': W1, 'b1': b1, 'W2': W2, 'b2': b2}
    _L2_gnn_all = _L2_gnn_setup()
    _L2_gnn_in = {k: v for k, v in _L2_gnn_all.items() if k in ('W1', 'b1', 'W2', 'b2')}
    del _L2_gnn_all

    def _L3_gnn_setup():
        import jax, jax.numpy as jnp
        import numpy as np
        N = 4096
        E = 65536
        MUL = 8
        NB = 8
        HR = 64
        NTP = 4 * MUL * MUL
        AVG_NEI = 16.0
        INV_SQRT3 = 1.0 / np.sqrt(3.0)
        ALPHA = 1.0 / np.sqrt(2.0 * MUL)
        key = jax.random.key(seed)
        ks = jax.random.split(key, 12)
        h = jax.random.normal(ks[0], (N, 4 * MUL), jnp.float32)
        edge_index = jax.random.randint(ks[1], (2, E), 0, N)
        edge_sh = jax.random.normal(ks[2], (E, 4), jnp.float32)
        edge_radial = jax.random.uniform(ks[3], (E, NB), jnp.float32)

        def lin(k, fi, fo):
            return (jax.random.normal(k, (fi, fo), jnp.float32) / np.sqrt(fi)).astype(jnp.float32)
        W1 = lin(ks[4], NB, HR)
        b1 = jnp.zeros((HR,), jnp.float32)
        W2 = lin(ks[5], HR, HR)
        b2 = jnp.zeros((HR,), jnp.float32)
        W3 = lin(ks[6], HR, NTP)
        b3 = jnp.zeros((NTP,), jnp.float32)
        Ws = jax.random.normal(ks[7], (MUL, MUL), jnp.float32)
        Wv = jax.random.normal(ks[8], (MUL, MUL), jnp.float32)
        return dict(h=h, edge_index=edge_index, edge_sh=edge_sh, edge_radial=edge_radial, n_atoms=N, W1=W1, b1=b1, W2=W2, b2=b2, W3=W3, b3=b3, Ws=Ws, Wv=Wv)
    _L3_gnn_all = _L3_gnn_setup()
    _L3_gnn_in = {k: v for k, v in _L3_gnn_all.items() if k in ('W1', 'b1', 'W2', 'b2', 'W3', 'b3', 'Ws', 'Wv')}
    del _L3_gnn_all
    return {'x': x, 'src': src, 'dst': dst, 'edge_attr_3': edge_attr_3, 'edge_attr_32': edge_attr_32, 'edge_attr_4': edge_attr_4, 'edge_attr_5': edge_attr_5, 'edge_attr_8': edge_attr_8, 'edge_weight1': edge_weight1, 'L0_gnn_W1': _L0_gnn_in['W1'], 'L0_gnn_b1': _L0_gnn_in['b1'], 'L0_gnn_W2': _L0_gnn_in['W2'], 'L0_gnn_b2': _L0_gnn_in['b2'], 'L0_gnn_si_w0': _L0_gnn_in['si_w0'], 'L0_gnn_si_w1': _L0_gnn_in['si_w1'], 'L1_gnn_W': _L1_gnn_in['W'], 'L2_gnn_W1': _L2_gnn_in['W1'], 'L2_gnn_b1': _L2_gnn_in['b1'], 'L2_gnn_W2': _L2_gnn_in['W2'], 'L2_gnn_b2': _L2_gnn_in['b2'], 'L3_gnn_W1': _L3_gnn_in['W1'], 'L3_gnn_b1': _L3_gnn_in['b1'], 'L3_gnn_W2': _L3_gnn_in['W2'], 'L3_gnn_b2': _L3_gnn_in['b2'], 'L3_gnn_W3': _L3_gnn_in['W3'], 'L3_gnn_b3': _L3_gnn_in['b3'], 'L3_gnn_Ws': _L3_gnn_in['Ws'], 'L3_gnn_Wv': _L3_gnn_in['Wv']}

def reference(x, src, dst, edge_attr_3, edge_attr_32, edge_attr_4, edge_attr_5, edge_attr_8, edge_weight1, L0_gnn_W1, L0_gnn_b1, L0_gnn_W2, L0_gnn_b2, L0_gnn_si_w0, L0_gnn_si_w1, L1_gnn_W, L2_gnn_W1, L2_gnn_b1, L2_gnn_W2, L2_gnn_b2, L3_gnn_W1, L3_gnn_b1, L3_gnn_W2, L3_gnn_b2, L3_gnn_W3, L3_gnn_b3, L3_gnn_Ws, L3_gnn_Wv):
    import jax
    import jax.numpy as jnp

    def _L0_gnn_ref(node_attr, edge_index, edge_sh, edge_feat, W1, b1, W2, b2, si_w0, si_w1):
        import jax, jax.numpy as jnp
        import numpy as np
        MUL = 8
        N_NODES = 12500
        N_EDGES = 100000
        EDGE_DIM = 32
        MLP_DIM = 64
        W_NUMEL = 4 * MUL * MUL
        ALPHA = 0.25
        C110 = 1.0 / np.sqrt(3.0)
        SI_SCALE = 1.0 / np.sqrt(MUL)
        n = node_attr.shape[0]
        e = edge_sh.shape[0]
        h = jax.nn.relu(edge_feat @ W1 + b1)
        w = (h @ W2 + b2).reshape(e, 4, MUL, MUL)
        w_000, w_011, w_101, w_110 = (w[:, 0], w[:, 1], w[:, 2], w[:, 3])
        s = node_attr[:, :MUL]
        v = node_attr[:, MUL:].reshape(n, MUL, 3)
        src, dst = (edge_index[0], edge_index[1])
        s_e = s[src]
        v_e = v[src]
        sh0 = edge_sh[:, 0]
        sh1 = edge_sh[:, 1:4]
        m0 = ALPHA * (jnp.einsum('ei,eio->eo', s_e * sh0[:, None], w_000) + C110 * jnp.einsum('eim,em,eio->eo', v_e, sh1, w_110))
        m1 = ALPHA * (jnp.einsum('ei,em,eio->eom', s_e, sh1, w_011) + jnp.einsum('eim,eio->eom', v_e * sh0[:, None, None], w_101))
        out0 = jax.ops.segment_sum(m0, dst, num_segments=n)
        out1 = jax.ops.segment_sum(m1.reshape(e, MUL * 3), dst, num_segments=n).reshape(n, MUL, 3)
        out0 = out0 + SI_SCALE * (s @ si_w0)
        out1 = out1 + SI_SCALE * jnp.einsum('nim,io->nom', v, si_w1)
        return jnp.concatenate([out0, out1.reshape(n, MUL * 3)], axis=-1)

    def _L1_gnn_ref(node_irreps, edge_index, sh0, sh1, sh2, W):
        import jax, jax.numpy as jnp
        import numpy as np
        import math
        M = 8
        COMBOS = [(0, 0, 0), (0, 1, 1), (1, 0, 1), (1, 1, 0), (1, 1, 1), (2, 1, 1)]

        def _cg_coeff(j1, m1, j2, m2, j3, m3):
            if m3 != m1 + m2:
                return 0.0
            f = math.factorial
            vmin = max(0, j2 - j3 - m1, j1 + m2 - j3)
            vmax = min(j1 + j2 - j3, j1 - m1, j2 + m2)
            pref = (2 * j3 + 1) * f(j3 + j1 - j2) * f(j3 - j1 + j2) * f(j1 + j2 - j3) / f(j1 + j2 + j3 + 1)
            pref *= f(j3 + m3) * f(j3 - m3) * f(j1 - m1) * f(j1 + m1) * f(j2 - m2) * f(j2 + m2)
            s = 0.0
            for v in range(vmin, vmax + 1):
                s += (-1) ** v / (f(v) * f(j1 + j2 - j3 - v) * f(j1 - m1 - v) * f(j2 + m2 - v) * f(j3 - j2 + m1 + v) * f(j3 - j1 - m2 + v))
            return math.sqrt(pref) * s

        def _su2_cg(l1, l2, l3):
            C = np.zeros((2 * l1 + 1, 2 * l2 + 1, 2 * l3 + 1), dtype=np.complex128)
            for m1 in range(-l1, l1 + 1):
                for m2 in range(-l2, l2 + 1):
                    m3 = m1 + m2
                    if -l3 <= m3 <= l3:
                        C[m1 + l1, m2 + l2, m3 + l3] = _cg_coeff(l1, m1, l2, m2, l3, m3)
            return C

        def _qmat(l):
            q = np.zeros((2 * l + 1, 2 * l + 1), dtype=np.complex128)
            for m in range(-l, 0):
                q[l + m, l + abs(m)] = 1 / np.sqrt(2)
                q[l + m, l - abs(m)] = -1j / np.sqrt(2)
            q[l, l] = 1.0
            for m in range(1, l + 1):
                q[l + m, l + abs(m)] = (-1) ** m / np.sqrt(2)
                q[l + m, l - abs(m)] = 1j * (-1) ** m / np.sqrt(2)
            return (-1j) ** l * q

        def _so3_cg(l1, l2, l3):
            C = np.einsum('ij,kl,mn,ikn->jlm', _qmat(l1), _qmat(l2), np.conj(_qmat(l3)).T, _su2_cg(l1, l2, l3))
            assert np.abs(C.imag).max() < 1e-06
            C = C.real
            return C / np.linalg.norm(C)
        CG = {c: jnp.asarray(_so3_cg(*c), dtype=jnp.float32) for c in COMBOS}
        N, E = (node_irreps.shape[0], edge_index.shape[1])
        src = node_irreps[edge_index[0]]
        feats = {0: src[:, :M][:, :, None], 1: src[:, M:].reshape(E, M, 3)}
        sh = {0: sh0, 1: sh1, 2: sh2}
        msg = {0: jnp.zeros((E, M, 1), node_irreps.dtype), 1: jnp.zeros((E, M, 3), node_irreps.dtype)}
        for idx, (le, ln, lo) in enumerate(COMBOS):
            base = jnp.einsum('ijk,ei,emj->emk', CG[le, ln, lo], sh[le], feats[ln])
            msg[lo] = msg[lo] + jnp.einsum('io,eik->eok', W[idx], base)
        tgt = edge_index[1]
        agg0 = jax.ops.segment_sum(msg[0].reshape(E, M), tgt, num_segments=N)
        agg1 = jax.ops.segment_sum(msg[1].reshape(E, 3 * M), tgt, num_segments=N)
        return jnp.concatenate([agg0, agg1], axis=1)

    def _L2_gnn_ref(x, edge_index, W1, b1, W2, b2):
        import jax, jax.numpy as jnp
        import numpy as np
        N_NODES = 12500
        N_EDGES = 200000
        EMB = 32
        HID = 64

        def gcn_conv(x, W, b, row, col, n_nodes):
            xw = x @ W
            ones = jnp.ones(row.shape[0], dtype=x.dtype)
            deg = jax.ops.segment_sum(ones, col, num_segments=n_nodes)
            dinv = jnp.where(deg > 0, jax.lax.rsqrt(deg), 0.0)
            norm = dinv[row] * dinv[col]
            msgs = norm[:, None] * xw[row]
            out = jax.ops.segment_sum(msgs, col, num_segments=n_nodes)
            return out + b
        n = x.shape[0]
        loops = jnp.arange(n, dtype=edge_index.dtype)
        row = jnp.concatenate([edge_index[0], loops])
        col = jnp.concatenate([edge_index[1], loops])
        h = jax.nn.relu(gcn_conv(x, W1, b1, row, col, n))
        h = jax.nn.relu(gcn_conv(h, W2, b2, row, col, n))
        return h

    def _L3_gnn_ref(h, edge_index, edge_sh, edge_radial, n_atoms, W1, b1, W2, b2, W3, b3, Ws, Wv):
        import jax, jax.numpy as jnp
        import numpy as np
        N = 4096
        E = 65536
        MUL = 8
        NB = 8
        HR = 64
        NTP = 4 * MUL * MUL
        AVG_NEI = 16.0
        INV_SQRT3 = 1.0 / np.sqrt(3.0)
        ALPHA = 1.0 / np.sqrt(2.0 * MUL)
        src, dst = (edge_index[0], edge_index[1])
        x = jax.nn.silu(edge_radial @ W1 + b1)
        x = jax.nn.silu(x @ W2 + b2)
        tpw = x @ W3 + b3
        P = MUL * MUL
        W00 = tpw[:, 0 * P:1 * P].reshape(-1, MUL, MUL)
        W110 = tpw[:, 1 * P:2 * P].reshape(-1, MUL, MUL)
        W01 = tpw[:, 2 * P:3 * P].reshape(-1, MUL, MUL)
        W10 = tpw[:, 3 * P:4 * P].reshape(-1, MUL, MUL)
        hs = h[:, :MUL]
        hv = h[:, MUL:].reshape(-1, MUL, 3)
        hs_e = hs[src]
        hv_e = hv[src]
        sh0 = edge_sh[:, 0]
        sh1 = edge_sh[:, 1:4]
        m0 = ALPHA * (jnp.einsum('eu,euw->ew', hs_e * sh0[:, None], W00) + INV_SQRT3 * jnp.einsum('eui,ei,euw->ew', hv_e, sh1, W110))
        m1 = ALPHA * (jnp.einsum('eu,ei,euw->ewi', hs_e, sh1, W01) + jnp.einsum('eui,euw->ewi', hv_e * sh0[:, None, None], W10))
        messages = jnp.concatenate([m0, m1.reshape(-1, 3 * MUL)], axis=-1)
        agg = jax.ops.segment_sum(messages, dst, num_segments=n_atoms) / np.sqrt(AVG_NEI)
        self0 = hs @ Ws / np.sqrt(MUL)
        self1 = jnp.einsum('nui,uw->nwi', hv, Wv) / np.sqrt(MUL)
        h_self = jnp.concatenate([self0, self1.reshape(-1, 3 * MUL)], axis=-1)
        return h_self + agg
    edge_index = jnp.stack([src, dst])
    x = _layernorm(x + _L0_gnn_ref(x, edge_index, edge_attr_4, edge_attr_32, L0_gnn_W1, L0_gnn_b1, L0_gnn_W2, L0_gnn_b2, L0_gnn_si_w0, L0_gnn_si_w1), axis=-1)
    x = _layernorm(x + _L1_gnn_ref(x, edge_index, edge_weight1, edge_attr_3, edge_attr_5, L1_gnn_W), axis=-1)
    x = _layernorm(x + _L2_gnn_ref(x, edge_index, L2_gnn_W1, L2_gnn_b1, L2_gnn_W2, L2_gnn_b2), axis=-1)
    x = _layernorm(x + _L3_gnn_ref(x, edge_index, edge_attr_4, edge_attr_8, 12500, L3_gnn_W1, L3_gnn_b1, L3_gnn_W2, L3_gnn_b2, L3_gnn_W3, L3_gnn_b3, L3_gnn_Ws, L3_gnn_Wv), axis=-1)
    return x

_drawn_inputs = setup_inputs


def setup_inputs(seed=0):
    import zlib

    import numpy as np

    out = dict(_drawn_inputs(seed))
    spreads = {'L0_gnn_b1': (0.0, 0.1),
     'L0_gnn_b2': (0.0, 0.1),
     'L2_gnn_b1': (0.0, 0.293),
     'L2_gnn_b2': (0.0, 0.1),
     'L3_gnn_b1': (0.0, 0.298),
     'L3_gnn_b2': (0.0, 0.1),
     'L3_gnn_b3': (0.0, 0.1)}
    factors = {'L2_gnn_W1': 3.146}
    for name, (base, spread) in spreads.items():
        noise = np.random.default_rng([zlib.crc32(name.encode()), seed]).standard_normal(out[name].shape)
        drawn = base * np.exp(spread * noise) if base else spread * noise
        out[name] = jnp.asarray(drawn.astype(out[name].dtype))
    for name, factor in factors.items():
        out[name] = (out[name] * factor).astype(out[name].dtype)
    return out
```

```python
from contextlib import ExitStack

import concourse.bass as bass
import numpy as np
from concourse import mybir

F32 = mybir.dt.float32
I32 = mybir.dt.int32
U32 = mybir.dt.uint32
ALU = mybir.AluOpType
ACT = mybir.ActivationFunctionType
AX = mybir.AxisListType.X
DVE_ONLY = [mybir.EngineType.DVE]

NODES, EDGES, FEAT, MUL = 12500, 400000, 32, 8
P = 128
TILES = 5
BLOCK = TILES * P
SLOTS = 4
REAL_BLOCKS = EDGES // BLOCK
TURNS = -(-REAL_BLOCKS // SLOTS)
BLOCKS = TURNS * SLOTS
WINDOW = 64
ACC = NODES + WINDOW
HID = 64
WPATHS = 4 * MUL * MUL
HARM = 9
OUTER = 4 * FEAT + 5 * 3 * MUL
OCH = 125
NT = 125
GROUP = 4
GN = NT * GROUP
GROUPS = NODES // GN
EPS = 1e-5
HALF = BLOCK // 2
LO_SPLIT = REAL_BLOCKS // 125


def edge_order(a, fill=0):
    a = np.concatenate([a, np.full((BLOCKS * BLOCK - EDGES,) + a.shape[1:], fill, a.dtype)])
    a = a.reshape((BLOCKS, TILES, P) + a.shape[1:])
    a = np.moveaxis(a, 1, 2)
    return np.ascontiguousarray(np.concatenate([a, a[:SLOTS]]))


def edge_major(a):
    a = np.concatenate([a, np.zeros((BLOCKS * BLOCK - EDGES, a.shape[1]), a.dtype)])
    a = np.moveaxis(a.reshape(BLOCKS, BLOCK, -1), 1, 2)
    return np.ascontiguousarray(np.concatenate([a, a[:SLOTS]]))


def path_columns(w, order):
    w = w.reshape(-1, 4, MUL, MUL)
    vv_s, ss_s, s_v, v_v = (w[:, p] for p in order)
    scalars = np.stack([vv_s, ss_s], 1)
    return np.ascontiguousarray(np.concatenate([
        scalars.transpose(0, 3, 1, 2).reshape(len(w), 2 * MUL * MUL),
        s_v.transpose(0, 2, 1).reshape(len(w), MUL * MUL),
        v_v.transpose(0, 2, 1).reshape(len(w), MUL * MUL)], 1))


def irrep_blocks(w0, w1):
    m = np.zeros((FEAT, FEAT), w0.dtype)
    m[:MUL, :MUL] = w0
    for c in range(3):
        m[MUL + c::3, MUL + c::3] = w1
    return m


def coupling(l1, l2, l3):
    from math import factorial as f, sqrt

    def su2(j1, m1, j2, m2, j3, m3):
        if m3 != m1 + m2:
            return 0.0
        vmin = max(0, j2 - j3 - m1, j1 + m2 - j3)
        vmax = min(j1 + j2 - j3, j1 - m1, j2 + m2)
        pref = (2 * j3 + 1) * f(j3 + j1 - j2) * f(j3 - j1 + j2) * f(j1 + j2 - j3) / f(j1 + j2 + j3 + 1)
        pref *= f(j3 + m3) * f(j3 - m3) * f(j1 - m1) * f(j1 + m1) * f(j2 - m2) * f(j2 + m2)
        s = 0.0
        for v in range(vmin, vmax + 1):
            s += (-1) ** v / (f(v) * f(j1 + j2 - j3 - v) * f(j1 - m1 - v) * f(j2 + m2 - v)
                              * f(j3 - j2 + m1 + v) * f(j3 - j1 - m2 + v))
        return sqrt(pref) * s

    def q(l):
        m = np.zeros((2 * l + 1, 2 * l + 1), np.complex128)
        for k in range(-l, 0):
            m[l + k, l - k] = 1 / sqrt(2)
            m[l + k, l + k] = -1j / sqrt(2)
        m[l, l] = 1
        for k in range(1, l + 1):
            m[l + k, l + k] = (-1) ** k / sqrt(2)
            m[l + k, l - k] = 1j * (-1) ** k / sqrt(2)
        return (-1j) ** l * m

    c = np.zeros((2 * l1 + 1, 2 * l2 + 1, 2 * l3 + 1), np.complex128)
    for a in range(-l1, l1 + 1):
        for b in range(-l2, l2 + 1):
            if -l3 <= a + b <= l3:
                c[a + l1, b + l2, a + b + l3] = su2(l1, a, l2, b, l3, a + b)
    c = np.einsum("ij,kl,mn,ikn->jlm", q(l1), q(l2), np.conj(q(l3)).T, c).real
    return (c / np.linalg.norm(c)).astype(np.float32)


def coupling_layout(w):
    cg = {c: coupling(*c) for c in [(0, 0, 0), (0, 1, 1), (1, 0, 1), (1, 1, 0), (1, 1, 1), (2, 1, 1)]}
    coef = np.zeros((2 * OCH, FEAT + 1), np.float32)
    weight = np.zeros((2 * OCH, FEAT + 1), w.dtype)
    for path, (le, ln, lo) in enumerate(cg):
        c = cg[le, ln, lo]
        for a in range(2 * le + 1):
            for m in range(2 * ln + 1):
                for k in range(2 * lo + 1):
                    for i in range(MUL):
                        feat = i if ln == 0 else MUL + 3 * i + m
                        row = {0: 0, 1: FEAT * (1 + a)}[le] + feat if le < 2 else \
                            4 * FEAT + 3 * MUL * a + feat - MUL
                        for o in range(MUL):
                            col = o if lo == 0 else MUL + 3 * o + k
                            coef[row, col] = c[a, m, k]
                            weight[row, col] = w[path, i, o]
    coef[OUTER, FEAT] = 1
    weight[OUTER, FEAT] = 1
    return coef.reshape(2, OCH, FEAT + 1), weight.reshape(2, OCH, FEAT + 1)


def build(nc, a, out):
    with ExitStack() as ctx:
        dram = lambda name, shape, dt: nc.dram_tensor(name, shape, dt, kind="Internal").ap()
        sb = lambda name, shape, dt=F32: ctx.enter_context(nc.sbuf_tensor(name, shape, dt))
        x1, x2, x3 = (dram(f"x_after_{n}", [NODES, FEAT], F32) for n in ("weighted0", "coupled", "convolved"))
        u1, u2 = (dram(f"conv_rows_{n}", [NODES, FEAT], F32) for n in (1, 2))
        lo_row = dram("lowest_target", [1, BLOCKS], F32)
        span_row = dram("target_span", [1, 125], F32)
        k = {
            "nc": nc,
            "acc": sb("acc", [P, 2, ACC]),
            "local": sb("local", [P, BLOCKS, TILES]),
            "iota0": sb("iota0", [P, WINDOW]),
            "lo": sb("lo", [1, BLOCKS]),
            "passes": sb("passes", [1, 1], I32),
            "ident": sb("ident", [P, P]),
            "dinv": sb("dinv", [NT, GROUPS, GROUP]),
            "eps": sb("eps", [P, 1]),
        }
        setup(nc, a, k, lo_row, span_row)
        weighted_edges(nc, a, k, "weighted0", a["x"], "ef32", FEAT, ["L0_gnn_W1", "L0_gnn_W2"],
                       ["L0_gnn_b1", "L0_gnn_b2"], ACT.Relu)
        weighted_nodes(nc, a, k, "weighted0", a["x"], x1, "L0_self", 0.25, 1 / np.sqrt(MUL))
        coupled_edges(nc, a, k, x1)
        coupled_nodes(nc, a, k, x1, x2, u1)
        conv_edges(nc, a, k, "conv1", u1)
        conv1_nodes(nc, a, k, u1, u2)
        conv_edges(nc, a, k, "conv2", u2)
        conv2_nodes(nc, a, k, u2, x2, x3)
        weighted_edges(nc, a, k, "weighted3", x3, "ef8", MUL, ["L3_gnn_W1", "L3_gnn_W2", "L3_gnn_W3"],
                       ["L3_gnn_b1", "L3_gnn_b2", "L3_gnn_b3"], ACT.Silu)
        weighted_nodes(nc, a, k, "weighted3", x3, out, "L3_self", 0.25 / 4, 1 / np.sqrt(MUL))


def setup(nc, a, k, lo_row, span_row):
    with ExitStack() as ctx:
        sb = lambda name, shape, dt=F32: ctx.enter_context(nc.sbuf_tensor(name, shape, dt))
        sem = lambda name: ctx.enter_context(nc.semaphore(name))
        by_block = sb("by_block", [125, LO_SPLIT, BLOCK], I32)
        by_block_f = sb("by_block_f", [125, LO_SPLIT, BLOCK])
        by_lane = sb("by_lane", [P, BLOCKS * TILES], I32)
        lowest = sb("lowest", [125, LO_SPLIT])
        highest = sb("highest", [125, LO_SPLIT])
        span = sb("span", [125, LO_SPLIT])
        span_max = sb("span_max", [125, 1])
        none = sb("none", [1, BLOCKS - REAL_BLOCKS])
        lo_all = sb("lo_all", [P, BLOCKS])
        spans = sb("spans", [1, 125])
        widest = sb("widest", [1, 1])
        blocks_loaded, lanes_loaded = sem("blocks_loaded"), sem("lanes_loaded")
        found, lo_stored, lo_loaded, made = sem("found"), sem("lo_stored"), sem("lo_loaded"), sem("made")
        spans_loaded = sem("spans_loaded")
        with nc.Block() as block:
            @block.sync
            def _(sp):
                sp.dma_start(by_block[:, :, :], a["dst"].rearrange("(p b e) -> p b e", b=LO_SPLIT, e=BLOCK))\
                  .then_inc(blocks_loaded, 16)
                sp.dma_start(by_lane[:, :], a["dst_lanes"]).then_inc(lanes_loaded, 16)
                sp.wait_ge(found, 7)
                sp.dma_start(lo_row[0:1, 0:REAL_BLOCKS].rearrange("o (p b) -> (o p) b", b=LO_SPLIT), lowest[:, :])\
                  .then_inc(lo_stored, 16)
                sp.dma_start(lo_row[0:1, REAL_BLOCKS:BLOCKS], none[:, :]).then_inc(lo_stored, 16)
                sp.dma_start(span_row.rearrange("o p -> p o"), span_max[:, :]).then_inc(lo_stored, 16)
                sp.wait_ge(lo_stored, 48)
                sp.dma_start(k["lo"][:, :], lo_row).then_inc(lo_loaded, 16)
                sp.dma_start(lo_all[:, :], lo_row.broadcast_to([P, BLOCKS])).then_inc(lo_loaded, 16)
                sp.dma_start(spans[:, :], span_row).then_inc(spans_loaded, 16)

            @block.gpsimd
            def _(pool):
                pool.memset(k["ident"][:, :], 0.0).then_inc(made, 1)
                pool.wait_ge(made, 1)
                pool.affine_select(out=k["ident"][:, :], in_=k["ident"][:, :], compare_op=ALU.not_equal, fill=1.0,
                                   base=0, pattern=[[-1, P]], channel_multiplier=1).then_inc(made, 1)
                pool.iota(k["iota0"][:, :], pattern=[[1, WINDOW]], base=0, channel_multiplier=0,
                          allow_small_or_imprecise_dtypes=True).then_inc(made, 1)
                pool.wait_ge(made, 3)

            @block.vector
            def _(dve):
                dve.memset(k["eps"][:, :], EPS).then_inc(found, 1)
                dve.memset(none[:, :], 0.0).then_inc(found, 1)
                dve.wait_ge(blocks_loaded, 16)
                dve.tensor_copy(by_block_f[:, :, :], by_block[:, :, :]).then_inc(found, 1)
                dve.wait_ge(found, 3)
                dve.tensor_reduce(lowest[:, :], by_block_f[:, :, :], AX, ALU.min).then_inc(found, 1)
                dve.tensor_reduce(highest[:, :], by_block_f[:, :, :], AX, ALU.max).then_inc(found, 1)
                dve.wait_ge(found, 5)
                dve.tensor_tensor(span[:, :], highest[:, :], lowest[:, :], ALU.subtract).then_inc(found, 1)
                dve.wait_ge(found, 6)
                dve.tensor_reduce(span_max[:, :], span[:, :], AX, ALU.max).then_inc(found, 1)
                dve.wait_ge(lanes_loaded, 16)
                dve.tensor_copy(k["local"][:, :, :], by_lane[:, :].rearrange("p (b t) -> p b t", t=TILES))\
                   .then_inc(found, 1)
                dve.wait_ge(found, 8)
                dve.wait_ge(lo_loaded, 32)
                dve.tensor_tensor(k["local"][:, :, :], k["local"][:, :, :],
                                  lo_all[:, :, None].broadcast_to([P, BLOCKS, TILES]), ALU.subtract)\
                   .then_inc(found, 1)
                dve.wait_ge(spans_loaded, 16)
                dve.tensor_reduce(widest[:, :], spans[:, :], AX, ALU.max).then_inc(found, 1)
                dve.wait_ge(found, 10)
                dve.tensor_copy(k["passes"][:, :], widest[:, :]).then_inc(found, 1)
                dve.wait_ge(found, 11)


def hold(engine, sem, value, passed):
    engine.wait_ge(sem, value)
    engine.sem_inc(passed, 1)


class Turns:

    def __init__(self, engine, k):
        self.engine = engine
        self.passes = engine.value_load(k["passes"][0:1, 0:1], min_val=0, max_val=NODES) // WINDOW + 1

    def flat(self):
        return self.engine.Fori(0, self.passes * TURNS, 1)


def load_blocks(sp, k, loads, used, loaded, ended):
    def fill(slot, block):
        for dst, src in loads:
            sp.dma_start(dst[slot], src(block)).then_inc(loaded[slot], 16)

    turns = Turns(sp, k)
    for s in range(SLOTS):
        fill(s, 0 * SLOTS + s)
    with sp.Fori(0, turns.passes, 1) as p:
        with sp.Fori(0, TURNS, 1) as i:
            for s in range(SLOTS):
                sp.wait_ge(used, (p * TURNS + i) * SLOTS + s + 1)
                fill(s, i * SLOTS + (SLOTS + s))
    for s in range(SLOTS):
        hold(sp, loaded[s], (turns.passes * TURNS + 1) * (16 * len(loads)), ended)


def gather_rows(pool, k, table, idx, rows, loaded, per_load, gathered, started):
    turns = Turns(pool, k)
    with turns.flat() as g:
        for s in range(SLOTS):
            hold(pool, loaded[s], (g + 1) * per_load, started)
            for t in range(TILES):
                pool.indirect_dma_start(rows[s][:, t, :], None, table,
                                        bass.IndirectOffsetOnAxis(ap=idx[s][:, t:t + 1].bitcast(U32), axis=0))\
                    .then_inc(gathered[s], 16)


class Windows:

    def __init__(self, dve, k, iota, base_f, base, stepped, parts):
        self.dve, self.k, self.iota, self.base_f, self.base, self.stepped = dve, k, iota, base_f, base, stepped
        dve.memset(k["acc"][0:parts[0], 0:parts[1], :], 0.0).then_inc(stepped, 1)
        dve.tensor_copy(iota[:, :], k["iota0"][:, :]).then_inc(stepped, 1)
        dve.tensor_copy(base_f[:, :], k["lo"][:, :]).then_inc(stepped, 1)
        dve.tensor_copy(base[:, :, :].rearrange("o i s -> o (i s)"), k["lo"][:, :]).then_inc(stepped, 1)
        dve.wait_ge(stepped, 4)

    def next_window(self, p):
        dve = self.dve
        dve.tensor_scalar(self.iota[:, :], self.iota[:, :], float(WINDOW), None, ALU.add).then_inc(self.stepped, 1)
        dve.tensor_scalar(self.base_f[:, :], self.base_f[:, :], float(WINDOW), float(NODES), ALU.add, ALU.min)\
           .then_inc(self.stepped, 1)
        dve.wait_ge(self.stepped, p * 3 + 6)
        dve.tensor_copy(self.base[:, :, :].rearrange("o i s -> o (i s)"), self.base_f[:, :]).then_inc(self.stepped, 1)
        dve.wait_ge(self.stepped, p * 3 + 7)

    def bases(self, i):
        return nc_values(self.k["nc"], self.base[0:1, bass.ds(i, 1), :].rearrange("o i s -> o (i s)"))

    def one_hot(self, dst, block):
        return self.dve.tensor_tensor(
            dst[:, :, :], self.iota[:, None, :].broadcast_to([P, TILES, WINDOW]),
            self.k["local"][:, bass.ds(block, 1), :].rearrange("p b t -> p (b t)")[:, :, None]
            .broadcast_to([P, TILES, WINDOW]), ALU.is_equal)


def nc_values(nc, row):
    return nc.values_load_multi_w_load_instructions(row, engines=DVE_ONLY, min_val=0, max_val=NODES)[1]


def weighted_edges(nc, a, k, name, table, feats, fan_in, weights, biases, func):
    deep = len(weights) == 3
    layers = len(weights) - 1
    with ExitStack() as ctx:
        sb = lambda n, shape, dt=F32: ctx.enter_context(nc.sbuf_tensor(f"{name}_{n}", shape, dt))
        sem = lambda n: ctx.enter_context(nc.semaphore(f"{name}_{n}"))
        ring = lambda n, shape, dt=F32: [sb(f"{n}{s}", shape, dt) for s in range(SLOTS)]
        psum = lambda n, shape: ctx.enter_context(nc.psum_tensor(f"{name}_{n}_ps", shape, F32))
        idx, feat, sh = ring("idx", [P, TILES], I32), ring("feat", [fan_in, BLOCK]), ring("sh", [P, TILES, 4])
        rows, onehot, msg = ring("rows", [P, TILES, FEAT]), ring("onehot", [P, TILES, WINDOW]), ring("msg", [P, TILES, FEAT])
        hidden = ring("hidden", [HID + 1, BLOCK])
        first = sb("first", [HID, HALF])
        w_in, w_mid, w_out = sb("w_in", [fan_in, HID]), sb("w_mid", [HID, HID]), sb("w_out", [HID + 1, WPATHS])
        b_in, b_mid = sb("b_in", [HID, 1]), sb("b_mid", [HID, 1])
        iota, base_f, base = sb("iota", [P, WINDOW]), sb("base_f", [1, BLOCKS]), sb("base", [1, TURNS, SLOTS], I32)
        vsh = sb("vsh", [P, TILES, MUL, 3])
        scaled = sb("scaled", [P, TILES, MUL + FEAT])
        to_s = sb("to_s", [P, TILES, MUL, 2 * MUL])
        to_v = sb("to_v", [P, TILES, 4 * MUL, MUL])
        sums = sb("sums", [P, TILES, 4 * MUL])
        s_sh = sb("s_sh", [P, TILES, MUL, 3])
        banks = [psum("weights0", [P, 3 * 512]), psum("weights1", [P, 3 * 512])]
        hid_ps = psum("hid", [P, 512])
        win_ps = psum("win", [P, 512])
        loaded, gathered = [sem(f"loaded{s}") for s in range(SLOTS)], [sem(f"gathered{s}") for s in range(SLOTS)]
        params, ones = sem("params"), sem("ones")
        pre_ready, hidden_ready = sem("pre_ready"), sem("hidden_ready")
        w_ready, w_used = sem("w_ready"), sem("w_used")
        vec, crossed, summed, msg_ready = sem("vec"), sem("crossed"), sem("summed"), sem("msg_ready")
        spread, stepped = sem("spread"), sem("stepped")
        started, ended, held = sem("started"), sem("ended"), sem("held")
        PARAMS = 16 * 2 * len(weights)
        PER_BLOCK = 2 * layers
        VEC = 6

        with nc.Block() as block:
            @block.sync
            def _(sp):
                sp.dma_start(w_in[:, :], a[weights[0]]).then_inc(params, 16)
                sp.dma_start(b_in[:, :], a[biases[0]].rearrange("(h o) -> h o", o=1)).then_inc(params, 16)
                if deep:
                    sp.dma_start(w_mid[:, :], a[weights[1]]).then_inc(params, 16)
                    sp.dma_start(b_mid[:, :], a[biases[1]].rearrange("(h o) -> h o", o=1)).then_inc(params, 16)
                sp.dma_start(w_out[0:HID, :], a[weights[-1]]).then_inc(params, 16)
                sp.dma_start(w_out[HID:HID + 1, :], a[biases[-1]].rearrange("(o n) -> o n", o=1)).then_inc(params, 16)
                load_blocks(sp, k, [
                    ([x[:, :] for x in idx], lambda b: one(a["src_blocks"], b)),
                    ([x[:, :, :].rearrange("p t c -> p (t c)") for x in sh],
                     lambda b: one(a["sh4"], b, "b p t c -> p (b t c)")),
                    ([x[:, :] for x in feat], lambda b: one(a[feats], b)),
                ], msg_ready, loaded, ended)

            @block.gpsimd
            def _(pool):
                gather_rows(pool, k, table, idx, rows, loaded, 48, gathered, started)

            @block.tensor
            def _(pe):
                def hidden_mm(b, slot, half, layer):
                    n = b * PER_BLOCK + layers * half + layer
                    cols = slice(half * HALF, half * HALF + HALF)
                    if layer == 0:
                        if isinstance(n, int) and n == 0:
                            pe.wait_ge(params, PARAMS)
                        else:
                            pe.wait_ge(hidden_ready, n + 1 - layers)
                        pe.matmul(hid_ps[0:HID, 0:HALF], w_in[:, :], feat[slot][:, cols], start=True, stop=True)\
                          .then_inc(pre_ready, 1)
                    else:
                        hold(pe, hidden_ready, n, held)
                        pe.matmul(hid_ps[HID:2 * HID, 0:HALF], w_mid[:, :], first[:, :], start=True, stop=True)\
                          .then_inc(pre_ready, 1)

                def weight_mm(b, slot, bank, tiles):
                    for t in tiles:
                        if t == 0:
                            pe.wait_ge(hidden_ready, (b + 1) * PER_BLOCK)
                            if not (isinstance(b, int) and b == 0):
                                pe.wait_ge(w_used, b - 1)
                        mm = pe.matmul(banks[bank][:, t * WPATHS:(t + 1) * WPATHS],
                                       hidden[slot][:, t * P:(t + 1) * P], w_out[:, :], start=True, stop=True)
                        if t == TILES - 1:
                            mm.then_inc(w_ready, 1)

                def both(b_h, slot_h, turn_h, b_w, slot_w, bank_w):
                    pe.wait_ge(loaded[slot_h], turn_h * 48 + 48)
                    hidden_mm(b_h, slot_h, 0, 0)
                    weight_mm(b_w, slot_w, bank_w, [0, 1])
                    if deep:
                        hidden_mm(b_h, slot_h, 0, 1)
                    hidden_mm(b_h, slot_h, 1, 0)
                    weight_mm(b_w, slot_w, bank_w, [2, 3])
                    if deep:
                        hidden_mm(b_h, slot_h, 1, 1)
                    weight_mm(b_w, slot_w, bank_w, [4])

                turns = Turns(pe, k)
                pe.wait_ge(ones, SLOTS + 1)
                pe.wait_ge(loaded[0], 48)
                for half in range(2):
                    for layer in range(layers):
                        hidden_mm(0, 0, half, layer)
                both(1, 1, 0, 0, 0, 0)
                with turns.flat() as g:
                    for s in range(SLOTS):
                        n = g * SLOTS + s
                        both(n + 2, (s + 2) % SLOTS, g + (s + 2) // SLOTS, n + 1, (s + 1) % SLOTS, (s + 1) % 2)
                        pe.wait_ge(summed, n)
                        pe.wait_ge(msg_ready, n + 1)
                        for t in range(TILES):
                            mm = pe.matmul(win_ps[0:FEAT, 0:WINDOW], msg[s][:, t, :], onehot[s][:, t, :],
                                           start=(t == 0), stop=(t == TILES - 1))
                        mm.then_inc(spread, 1)

            @block.scalar
            def _(act):
                def hidden_act(b, slot, half, layer):
                    n = b * PER_BLOCK + layers * half + layer
                    last = layer == layers - 1
                    act.wait_ge(pre_ready, n + 1)
                    dst = hidden[slot][0:HID, half * HALF:half * HALF + HALF] if last else first[:, :]
                    nc.scalar.activation(dst, hid_ps[HID * layer:HID * layer + HID, 0:HALF], func,
                                         bias=(b_mid if layer else b_in)[:, 0:1]).then_inc(hidden_ready, 1)

                def block_act(b, slot):
                    for half in range(2):
                        for layer in range(layers):
                            hidden_act(b, slot, half, layer)

                turns = Turns(act, k)
                act.wait_ge(params, PARAMS)
                block_act(0, 0)
                block_act(1, 1)
                with turns.flat() as g:
                    for s in range(SLOTS):
                        block_act(g * SLOTS + s + 2, (s + 2) % SLOTS)

            @block.vector
            def _(dve):
                for s in range(SLOTS):
                    dve.memset(hidden[s][HID:HID + 1, :], 1.0).then_inc(ones, 1)
                dve.wait_ge(params, PARAMS)
                dots = w_out[:, 0:2 * MUL * MUL].rearrange("h (o q i) -> h o q i", q=2, i=MUL)[:, :, 0, :]
                dve.tensor_scalar(dots, dots, float(1 / np.sqrt(3.0)), None, ALU.mult).then_inc(ones, 1)
                win = Windows(dve, k, iota, base_f, base, stepped, (FEAT, 1))
                turns = Turns(dve, k)

                def add_window(n, at):
                    dve.wait_ge(spread, n + 1)
                    dst = k["acc"][0:FEAT, 0, bass.ds(at, WINDOW)]
                    dve.tensor_tensor(dst, dst, win_ps[0:FEAT, 0:WINDOW], ALU.add).then_inc(summed, 1)

                with dve.Fori(0, turns.passes, 1) as p:
                    with dve.Fori(0, TURNS, 1) as i:
                        g = p * TURNS + i
                        bases = win.bases(i)
                        for s in range(SLOTS):
                            n = g * SLOTS + s
                            x, h = rows[s], sh[s]
                            harm = h[:, :, 1:4][:, :, None, :].broadcast_to([P, TILES, MUL, 3])
                            vecs = x[:, :, MUL:].rearrange("p t (i m) -> p t i m", m=3)
                            win.one_hot(onehot[s], i * SLOTS + s).then_inc(vec, 1)
                            dve.wait_ge(gathered[s], g * (16 * TILES) + 16 * TILES)
                            dve.wait_ge(loaded[s], g * 48 + 48)
                            dve.tensor_tensor(vsh[:, :, :, :], vecs, harm, ALU.mult).then_inc(vec, 1)
                            dve.tensor_tensor(scaled[:, :, MUL:], x[:, :, :],
                                              h[:, :, 0:1].broadcast_to([P, TILES, FEAT]), ALU.mult).then_inc(vec, 1)
                            dve.wait_ge(vec, n * VEC + 2)
                            dve.tensor_reduce(scaled[:, :, 0:MUL], vsh[:, :, :, :], AX, ALU.add).then_inc(vec, 1)
                            dve.wait_ge(w_ready, n + 1)
                            w = banks[s % 2][:, 0:TILES * WPATHS].rearrange("p (t n) -> p t n", t=TILES)
                            w_s = w[:, :, 0:2 * MUL * MUL].rearrange("p t (o i) -> p t o i", o=MUL)
                            w_sv = w[:, :, 2 * MUL * MUL:3 * MUL * MUL].rearrange("p t (o i) -> p t o i", o=MUL)
                            w_vv = w[:, :, 3 * MUL * MUL:].rearrange("p t (o i) -> p t o i", o=MUL)
                            dve.tensor_tensor(to_v[:, :, 0:MUL, :], w_sv,
                                              x[:, :, None, 0:MUL].broadcast_to([P, TILES, MUL, MUL]), ALU.mult)
                            dve.wait_ge(vec, n * VEC + 4)
                            for m in range(3):
                                v_m = scaled[:, :, 2 * MUL:].rearrange("p t (i m) -> p t m i", m=3)[:, :, m]
                                last = dve.tensor_tensor(
                                    to_v[:, :, MUL:, :].rearrange("p t (o m) i -> p t m o i", m=3)[:, :, m],
                                    w_vv, v_m[:, :, None, :].broadcast_to([P, TILES, MUL, MUL]), ALU.mult)
                            last.then_inc(vec, 1)
                            dve.tensor_tensor(to_s[:, :, :, :], w_s,
                                              scaled[:, :, None, 0:2 * MUL].broadcast_to([P, TILES, MUL, 2 * MUL]),
                                              ALU.mult).then_inc(w_used, 1)
                            if s > 0:
                                add_window(n - 1, bases[s - 1])
                            dve.wait_ge(w_used, n + 1)
                            dve.tensor_reduce(sums[:, :, :], to_v[:, :, :, :], AX, ALU.add).then_inc(vec, 1)
                            dve.tensor_reduce(msg[s][:, :, 0:MUL], to_s[:, :, :, :], AX, ALU.add)
                            dve.wait_ge(vec, n * VEC + 6)
                            dve.tensor_tensor(s_sh[:, :, :, :], sums[:, :, 0:MUL][:, :, :, None]
                                              .broadcast_to([P, TILES, MUL, 3]), harm, ALU.mult).then_inc(crossed, 1)
                            dve.wait_ge(crossed, n + 1)
                            dve.tensor_tensor(msg[s][:, :, MUL:], s_sh[:, :, :, :].rearrange("p t o m -> p t (o m)"),
                                              sums[:, :, MUL:], ALU.add).then_inc(msg_ready, 1)
                        add_window(g * SLOTS + (SLOTS - 1), bases[SLOTS - 1])
                    win.next_window(p)


def one(src, b, to="b p t -> p (b t)"):
    return src[bass.ds(b, 1)].rearrange(to)


def coupled_edges(nc, a, k, table):
    with ExitStack() as ctx:
        sb = lambda n, shape, dt=F32: ctx.enter_context(nc.sbuf_tensor(f"coupled_{n}", shape, dt))
        sem = lambda n: ctx.enter_context(nc.semaphore(f"coupled_{n}"))
        ring = lambda n, shape, dt=F32: [sb(f"{n}{s}", shape, dt) for s in range(SLOTS)]
        idx, sh = ring("idx", [P, TILES], I32), ring("sh", [P, TILES, HARM])
        rows, onehot = ring("rows", [P, TILES, FEAT]), ring("onehot", [P, TILES, WINDOW])
        prod = ring("prod", [P, TILES, 2 * OCH])
        iota, base_f, base = sb("iota", [P, WINDOW]), sb("base_f", [1, BLOCKS]), sb("base", [1, TURNS, SLOTS], I32)
        win_ps = [ctx.enter_context(nc.psum_tensor(f"coupled_win{b}", [P, 512], F32)) for b in range(2)]
        loaded, gathered = [sem(f"loaded{s}") for s in range(SLOTS)], [sem(f"gathered{s}") for s in range(SLOTS)]
        msg_ready, spread, summed, stepped, ones = sem("msg_ready"), sem("spread"), sem("summed"), sem("stepped"), sem("ones")
        started, ended = sem("started"), sem("ended")

        with nc.Block() as block:
            @block.sync
            def _(sp):
                load_blocks(sp, k, [
                    ([x[:, :] for x in idx], lambda b: one(a["src_blocks"], b)),
                    ([x[:, :, :].rearrange("p t c -> p (t c)") for x in sh],
                     lambda b: one(a["sh9"], b, "b p t c -> p (b t c)")),
                ], msg_ready, loaded, ended)

            @block.gpsimd
            def _(pool):
                gather_rows(pool, k, table, idx, rows, loaded, 32, gathered, started)

            @block.tensor
            def _(pe):
                turns = Turns(pe, k)
                pe.wait_ge(ones, 2 * SLOTS)
                with turns.flat() as g:
                    for s in range(SLOTS):
                        n = g * SLOTS + s
                        if s == 0:
                            pe.wait_ge(summed, n)
                        else:
                            pe.wait_ge(summed, n - 1)
                        pe.wait_ge(msg_ready, n + 1)
                        for c in range(2):
                            for t in range(TILES):
                                mm = pe.matmul(win_ps[s % 2][0:OCH, c * WINDOW:(c + 1) * WINDOW],
                                               prod[s][:, t, c * OCH:(c + 1) * OCH], onehot[s][:, t, :],
                                               start=(t == 0), stop=(t == TILES - 1))
                        mm.then_inc(spread, 1)

            @block.vector
            def _(dve):
                for s in range(SLOTS):
                    dve.memset(prod[s][:, :, OUTER:OUTER + 1], 1.0).then_inc(ones, 1)
                    dve.memset(prod[s][:, :, OUTER + 1:], 0.0).then_inc(ones, 1)
                win = Windows(dve, k, iota, base_f, base, stepped, (P, 2))
                turns = Turns(dve, k)

                def add_window(n, s, at):
                    dve.wait_ge(summed, n)
                    dve.wait_ge(spread, n + 1)
                    dst = k["acc"][0:OCH, :, bass.ds(at, WINDOW)]
                    dve.tensor_tensor(dst, dst, win_ps[s % 2][0:OCH, 0:2 * WINDOW].rearrange("p (c w) -> p c w", c=2),
                                      ALU.add).then_inc(summed, 1)

                with dve.Fori(0, turns.passes, 1) as p:
                    with dve.Fori(0, TURNS, 1) as i:
                        g = p * TURNS + i
                        bases = win.bases(i)
                        for s in range(SLOTS):
                            n = g * SLOTS + s
                            x, h = rows[s], sh[s]
                            win.one_hot(onehot[s], i * SLOTS + s)
                            dve.wait_ge(gathered[s], g * (16 * TILES) + 16 * TILES)
                            dve.wait_ge(loaded[s], g * 32 + 32)
                            dve.tensor_tensor(
                                prod[s][:, :, 0:4 * FEAT].rearrange("p t (c f) -> p t c f", c=4),
                                h[:, :, 0:4][:, :, :, None].broadcast_to([P, TILES, 4, FEAT]),
                                x[:, :, None, :].broadcast_to([P, TILES, 4, FEAT]), ALU.mult)
                            dve.tensor_tensor(
                                prod[s][:, :, 4 * FEAT:OUTER].rearrange("p t (c f) -> p t c f", c=5),
                                h[:, :, 4:9][:, :, :, None].broadcast_to([P, TILES, 5, 3 * MUL]),
                                x[:, :, None, MUL:].broadcast_to([P, TILES, 5, 3 * MUL]), ALU.mult)\
                                .then_inc(msg_ready, 1)
                            if s > 0:
                                add_window(n - 1, s - 1, bases[s - 1])
                        add_window(g * SLOTS + (SLOTS - 1), SLOTS - 1, bases[SLOTS - 1])
                    win.next_window(p)


def conv_edges(nc, a, k, name, table):
    with ExitStack() as ctx:
        sb = lambda n, shape, dt=F32: ctx.enter_context(nc.sbuf_tensor(f"{name}_{n}", shape, dt))
        sem = lambda n: ctx.enter_context(nc.semaphore(f"{name}_{n}"))
        ring = lambda n, shape, dt=F32: [sb(f"{n}{s}", shape, dt) for s in range(SLOTS)]
        idx = ring("idx", [P, TILES], I32)
        rows, onehot = ring("rows", [P, TILES, FEAT]), ring("onehot", [P, TILES, WINDOW])
        iota, base_f, base = sb("iota", [P, WINDOW]), sb("base_f", [1, BLOCKS]), sb("base", [1, TURNS, SLOTS], I32)
        win_ps = [ctx.enter_context(nc.psum_tensor(f"{name}_win{b}", [P, 512], F32)) for b in range(2)]
        loaded, gathered = [sem(f"loaded{s}") for s in range(SLOTS)], [sem(f"gathered{s}") for s in range(SLOTS)]
        msg_ready, spread, summed, stepped = sem("msg_ready"), sem("spread"), sem("summed"), sem("stepped")
        started, ended = sem("started"), sem("ended")

        with nc.Block() as block:
            @block.sync
            def _(sp):
                load_blocks(sp, k, [([x[:, :] for x in idx], lambda b: one(a["src_blocks"], b))],
                            spread, loaded, ended)

            @block.gpsimd
            def _(pool):
                gather_rows(pool, k, table, idx, rows, loaded, 16, gathered, started)

            @block.tensor
            def _(pe):
                turns = Turns(pe, k)
                with turns.flat() as g:
                    for s in range(SLOTS):
                        n = g * SLOTS + s
                        if s == 0:
                            pe.wait_ge(summed, n)
                        else:
                            pe.wait_ge(summed, n - 1)
                        pe.wait_ge(msg_ready, n + 1)
                        pe.wait_ge(gathered[s], g * (16 * TILES) + 16 * TILES)
                        for t in range(TILES):
                            mm = pe.matmul(win_ps[s % 2][0:FEAT, 0:WINDOW], rows[s][:, t, :], onehot[s][:, t, :],
                                           start=(t == 0), stop=(t == TILES - 1))
                        mm.then_inc(spread, 1)

            @block.vector
            def _(dve):
                win = Windows(dve, k, iota, base_f, base, stepped, (FEAT, 1))
                turns = Turns(dve, k)

                def add_window(n, s, at):
                    dve.wait_ge(summed, n)
                    dve.wait_ge(spread, n + 1)
                    dst = k["acc"][0:FEAT, 0, bass.ds(at, WINDOW)]
                    dve.tensor_tensor(dst, dst, win_ps[s % 2][0:FEAT, 0:WINDOW], ALU.add).then_inc(summed, 1)

                with dve.Fori(0, turns.passes, 1) as p:
                    with dve.Fori(0, TURNS, 1) as i:
                        g = p * TURNS + i
                        bases = win.bases(i)
                        for s in range(SLOTS):
                            n = g * SLOTS + s
                            win.one_hot(onehot[s], i * SLOTS + s).then_inc(msg_ready, 1)
                            if s > 0:
                                add_window(n - 1, s - 1, bases[s - 1])
                        add_window(g * SLOTS + (SLOTS - 1), SLOTS - 1, bases[SLOTS - 1])
                    win.next_window(p)


def node_rows(t, g):
    return t.rearrange("(g q p) f -> g p q f", q=GROUP, p=NT)[bass.ds(g, 1)].rearrange("g p q f -> p (g q) f")


class Steps:

    def __init__(self, dve, done, per_group, g, before=0):
        self.dve, self.done, self.base, self.n = dve, done, g * per_group + before, 0

    def __call__(self, instruction):
        instruction.then_inc(self.done, 1)
        self.n += 1
        return self.n

    def wait(self, n):
        self.dve.wait_ge(self.done, self.base + n)


NORM_DVE = 9


def normalise(nc, step, dve, b, root_ready, g):
    wide = [NT, GROUP, FEAT]
    over = lambda t: t[:, :, None].broadcast_to(wide)
    step.wait(step(dve.tensor_reduce(b["mean"][:, :], b["y"][:, :, :], AX, ALU.add)))
    step.wait(step(dve.tensor_scalar(b["mean"][:, :], b["mean"][:, :], 1.0 / FEAT, None, ALU.mult)))
    step.wait(step(dve.tensor_tensor(b["y"][:, :, :], b["y"][:, :, :], over(b["mean"]), ALU.subtract)))
    step.wait(step(dve.tensor_tensor(b["sq"][:, :, :], b["y"][:, :, :], b["y"][:, :, :], ALU.mult)))
    n = step(dve.tensor_reduce(b["var"][:, :], b["sq"][:, :, :], AX, ALU.add))
    dve.wait_ge(root_ready, g + 1)
    step.wait(step(dve.reciprocal(b["rstd"][:, :], b["root"][:, :])))
    step(dve.tensor_tensor(b["xn"][:, :, :], b["y"][:, :, :], over(b["rstd"]), ALU.mult))
    return n


def norm_buffers(sb):
    b = {n: sb(n, [NT, GROUP, FEAT]) for n in ("y", "sq", "xn")}
    return b | {n: sb(n, [NT, GROUP]) for n in ("mean", "var", "root", "rstd")}


def node_phase(nc, name):
    ctx = ExitStack()
    sb = lambda n, shape, dt=F32: ctx.enter_context(nc.sbuf_tensor(f"{name}_{n}", shape, dt))
    sem = lambda n: ctx.enter_context(nc.semaphore(f"{name}_{n}"))
    psum = lambda n, shape: ctx.enter_context(nc.psum_tensor(f"{name}_{n}_ps", shape, F32))
    return ctx, sb, sem, psum


def weighted_nodes(nc, a, k, name, x_in, x_out, self_w, agg_scale, self_scale):
    ctx, sb, sem, psum = node_phase(nc, f"{name}_nodes")
    with ctx:
        x, xt = sb("x", [NT, GROUP, FEAT]), sb("xt", [FEAT, GN])
        sums = sb("sums", [FEAT, GN])
        own = sb("own", [FEAT, FEAT])
        b = norm_buffers(sb)
        xt_ps, y_ps = psum("xt", [FEAT, 512]), psum("y", [NT, 512])
        own_loaded, x_loaded, xt_ready, mixed, own_ready = (sem(n) for n in ("own_loaded", "x_loaded", "xt_ready", "mixed", "own_ready"))
        copied, done, root_ready, stored = sem("copied"), sem("done"), sem("root_ready"), sem("stored")
        STEPS = 8
        with nc.Block() as block:
            @block.sync
            def _(sp):
                sp.dma_start(own[:, :], a[self_w]).then_inc(own_loaded, 16)
                sp.dma_start(x[:, :, :], node_rows(x_in, 0)).then_inc(x_loaded, 16)
                with sp.Fori(0, GROUPS, 1) as g:
                    sp.wait_ge(done, g * STEPS + STEPS)
                    sp.dma_start(node_rows(x_out, g), b["xn"][:, :, :]).then_inc(stored, 16)
                    sp.wait_ge(stored, g * 16 + 16)
                    sp.dma_start(x[:, :, :], node_rows(x_in, next_group(g))).then_inc(x_loaded, 16)
                sp.wait_ge(x_loaded, 16 * (GROUPS + 1))
                sp.wait_ge(stored, 16 * GROUPS)

            @block.tensor
            def _(pe):
                with pe.Fori(0, GROUPS, 1) as g:
                    pe.wait_ge(x_loaded, g * 16 + 16)
                    pe.wait_ge(copied, g * 2)
                    for q in range(GROUP):
                        mm = pe.transpose(xt_ps[:, q * NT:(q + 1) * NT], x[:, q, :], k["ident"][0:NT, 0:NT])
                    mm.then_inc(xt_ready, 1)
                    pe.wait_ge(copied, g * 2 + 2)
                    pe.wait_ge(done, g * STEPS)
                    pe.wait_ge(own_ready, 1)
                    for q in range(GROUP):
                        cols = slice(q * NT, (q + 1) * NT)
                        pe.matmul(y_ps[:, q * FEAT:(q + 1) * FEAT], sums[:, cols], k["ident"][0:FEAT, 0:FEAT],
                                  start=True, stop=False)
                        mm = pe.matmul(y_ps[:, q * FEAT:(q + 1) * FEAT], xt[:, cols], own[:, :], start=False, stop=True)
                    mm.then_inc(mixed, 1)

            @block.scalar
            def _(act):
                with act.Fori(0, GROUPS, 1) as g:
                    act.wait_ge(mixed, g)
                    nc.scalar.activation(sums[:, :], k["acc"][0:FEAT, 0, bass.ds(g * GN, GN)], ACT.Copy,
                                         scale=float(agg_scale)).then_inc(copied, 1)
                    act.wait_ge(xt_ready, g + 1)
                    nc.scalar.activation(xt[:, :], xt_ps[:, 0:GN], ACT.Copy).then_inc(copied, 1)
                    act.wait_ge(done, g * STEPS + 6)
                    nc.scalar.activation(b["root"][:, :], b["var"][:, :], ACT.Sqrt, scale=1.0 / FEAT,
                                         bias=k["eps"][0:NT, 0:1]).then_inc(root_ready, 1)

            @block.vector
            def _(dve):
                dve.wait_ge(own_loaded, 16)
                dve.tensor_scalar(own[:, :], own[:, :], float(self_scale), None, ALU.mult).then_inc(own_ready, 1)
                with dve.Fori(0, GROUPS, 1) as g:
                    step = Steps(dve, done, STEPS, g)
                    dve.wait_ge(mixed, g + 1)
                    dve.wait_ge(stored, g * 16)
                    step.wait(step(dve.tensor_tensor(
                        b["y"][:, :, :], y_ps[:, 0:GROUP * FEAT].rearrange("p (q f) -> p q f", q=GROUP),
                        x[:, :, :], ALU.add)))
                    normalise(nc, step, dve, b, root_ready, g)


def next_group(g):
    return (g + 1) % GROUPS


def coupled_nodes(nc, a, k, x_in, x_out, u_out):
    ctx, sb, sem, psum = node_phase(nc, "coupled_nodes")
    with ctx:
        x, sums = sb("x", [NT, GROUP, FEAT]), sb("sums", [OCH, 2, GN])
        mix, coef = sb("mix", [OCH, 2, FEAT + 1]), sb("coef", [OCH, 2, FEAT + 1])
        deg, root_d, u = sb("deg", [NT, GROUP]), sb("root_d", [NT, GROUP]), sb("u", [NT, GROUP, FEAT])
        b = norm_buffers(sb)
        y_ps = psum("y", [NT, 512])
        mix_loaded, mix_ready, x_loaded, mixed = sem("mix_loaded"), sem("mix_ready"), sem("x_loaded"), sem("mixed")
        copied, done, root_ready, stored, rootd_ready = sem("copied"), sem("done"), sem("root_ready"), sem("stored"), sem("rootd_ready")
        STEPS = 11
        with nc.Block() as block:
            @block.sync
            def _(sp):
                sp.dma_start(mix[:, :, :], a["L1_mix"].rearrange("c p f -> p c f")).then_inc(mix_loaded, 16)
                sp.dma_start(coef[:, :, :], a["L1_coef"].rearrange("c p f -> p c f")).then_inc(mix_loaded, 16)
                sp.dma_start(x[:, :, :], node_rows(x_in, 0)).then_inc(x_loaded, 16)
                with sp.Fori(0, GROUPS, 1) as g:
                    sp.wait_ge(done, g * STEPS + STEPS)
                    sp.dma_start(node_rows(x_out, g), b["xn"][:, :, :]).then_inc(stored, 16)
                    sp.dma_start(node_rows(u_out, g), u[:, :, :]).then_inc(stored, 16)
                    sp.wait_ge(stored, g * 32 + 32)
                    sp.dma_start(x[:, :, :], node_rows(x_in, next_group(g))).then_inc(x_loaded, 16)
                sp.wait_ge(x_loaded, 16 * (GROUPS + 1))
                sp.wait_ge(stored, 32 * GROUPS)

            @block.tensor
            def _(pe):
                pe.wait_ge(mix_ready, 1)
                with pe.Fori(0, GROUPS, 1) as g:
                    pe.wait_ge(copied, g * 2 + 2)
                    pe.wait_ge(done, g * STEPS)
                    for q in range(GROUP):
                        for c in range(2):
                            mm = pe.matmul(y_ps[:, q * (FEAT + 1):(q + 1) * (FEAT + 1)], sums[:, c, q * NT:(q + 1) * NT],
                                           mix[:, c, :], start=(c == 0), stop=(c == 1))
                    mm.then_inc(mixed, 1)

            @block.scalar
            def _(act):
                with act.Fori(0, GROUPS, 1) as g:
                    act.wait_ge(mixed, g)
                    for c in range(2):
                        nc.scalar.activation(sums[:, c, :], k["acc"][0:OCH, c, bass.ds(g * GN, GN)], ACT.Copy)\
                          .then_inc(copied, 1)
                    act.wait_ge(done, g * STEPS + 2)
                    nc.scalar.activation(root_d[:, :], deg[:, :], ACT.Sqrt).then_inc(rootd_ready, 1)
                    act.wait_ge(done, g * STEPS + 7)
                    nc.scalar.activation(b["root"][:, :], b["var"][:, :], ACT.Sqrt, scale=1.0 / FEAT,
                                         bias=k["eps"][0:NT, 0:1]).then_inc(root_ready, 1)

            @block.vector
            def _(dve):
                dve.wait_ge(mix_loaded, 32)
                dve.tensor_tensor(mix[:, :, :], mix[:, :, :], coef[:, :, :], ALU.mult).then_inc(mix_ready, 1)
                with dve.Fori(0, GROUPS, 1) as g:
                    step = Steps(dve, done, STEPS, g)
                    dve.wait_ge(mixed, g + 1)
                    dve.wait_ge(x_loaded, g * 16 + 16)
                    dve.wait_ge(stored, g * 32)
                    y = y_ps[:, 0:GROUP * (FEAT + 1)].rearrange("p (q f) -> p q f", q=GROUP)
                    step(dve.tensor_tensor(b["y"][:, :, :], y[:, :, 0:FEAT], x[:, :, :], ALU.add))
                    step.wait(step(dve.tensor_scalar(deg[:, :], y[:, :, FEAT], 1.0, None, ALU.add)))
                    normalise(nc, step, dve, b, root_ready, g)
                    dve.wait_ge(rootd_ready, g + 1)
                    dinv = k["dinv"][:, bass.ds(g, 1), :].rearrange("p g q -> p (g q)")
                    step.wait(step(dve.reciprocal(dinv, root_d[:, :])))
                    step(dve.tensor_tensor(u[:, :, :], b["xn"][:, :, :],
                                           dinv[:, :, None].broadcast_to([NT, GROUP, FEAT]), ALU.mult))


def conv1_nodes(nc, a, k, u_in, u_out):
    ctx, sb, sem, psum = node_phase(nc, "conv1_nodes")
    with ctx:
        u, sums = sb("u", [NT, GROUP, FEAT]), sb("sums", [FEAT, GN])
        z, zt, h, o = sb("z", [NT, GROUP, FEAT]), sb("zt", [FEAT, GN]), sb("h", [HID, GN]), sb("o", [NT, GROUP, FEAT])
        w1, b1, w2 = sb("w1", [FEAT, HID]), sb("b1", [HID, 1]), sb("w2", [HID, FEAT])
        agg_ps, zt_ps, h_ps, o_ps = psum("agg", [NT, 512]), psum("zt", [FEAT, 512]), psum("h", [HID, 512]), psum("o", [NT, 512])
        params, u_loaded, copied, turned, done, stored = (sem(n) for n in ("params", "u_loaded", "copied", "turned", "done", "stored"))
        STEPS, TURNED, COPIED = 3, 4, 3
        with nc.Block() as block:
            @block.sync
            def _(sp):
                sp.dma_start(w1[:, :], a["L2_gnn_W1"]).then_inc(params, 16)
                sp.dma_start(b1[:, :], a["L2_gnn_b1"].rearrange("(h o) -> h o", o=1)).then_inc(params, 16)
                sp.dma_start(w2[:, :], a["L2_gnn_W2"]).then_inc(params, 16)
                sp.dma_start(u[:, :, :], node_rows(u_in, 0)).then_inc(u_loaded, 16)
                with sp.Fori(0, GROUPS, 1) as g:
                    sp.wait_ge(done, g * STEPS + STEPS)
                    sp.dma_start(node_rows(u_out, g), o[:, :, :]).then_inc(stored, 16)
                    sp.wait_ge(stored, g * 16 + 16)
                    sp.dma_start(u[:, :, :], node_rows(u_in, next_group(g))).then_inc(u_loaded, 16)
                sp.wait_ge(u_loaded, 16 * (GROUPS + 1))
                sp.wait_ge(stored, 16 * GROUPS)

            @block.tensor
            def _(pe):
                pe.wait_ge(params, 48)
                with pe.Fori(0, GROUPS, 1) as g:
                    pe.wait_ge(copied, g * COPIED + 1)
                    for q in range(GROUP):
                        mm = pe.matmul(agg_ps[:, q * FEAT:(q + 1) * FEAT], sums[:, q * NT:(q + 1) * NT],
                                       k["ident"][0:FEAT, 0:FEAT], start=True, stop=True)
                    mm.then_inc(turned, 1)
                    pe.wait_ge(done, g * STEPS + 2)
                    for q in range(GROUP):
                        mm = pe.transpose(zt_ps[:, q * NT:(q + 1) * NT], z[:, q, :], k["ident"][0:NT, 0:NT])
                    mm.then_inc(turned, 1)
                    pe.wait_ge(copied, g * COPIED + 2)
                    pe.matmul(h_ps[:, 0:GN], w1[:, :], zt[:, :], start=True, stop=True).then_inc(turned, 1)
                    pe.wait_ge(copied, g * COPIED + 3)
                    for q in range(GROUP):
                        mm = pe.matmul(o_ps[:, q * FEAT:(q + 1) * FEAT], h[:, q * NT:(q + 1) * NT], w2[:, :],
                                       start=True, stop=True)
                    mm.then_inc(turned, 1)

            @block.scalar
            def _(act):
                act.wait_ge(params, 48)
                with act.Fori(0, GROUPS, 1) as g:
                    act.wait_ge(turned, g * TURNED)
                    nc.scalar.activation(sums[:, :], k["acc"][0:FEAT, 0, bass.ds(g * GN, GN)], ACT.Copy).then_inc(copied, 1)
                    act.wait_ge(turned, g * TURNED + 2)
                    nc.scalar.activation(zt[:, :], zt_ps[:, 0:GN], ACT.Copy).then_inc(copied, 1)
                    act.wait_ge(turned, g * TURNED + 3)
                    nc.scalar.activation(h[:, :], h_ps[:, 0:GN], ACT.Relu, bias=b1[:, 0:1]).then_inc(copied, 1)

            @block.vector
            def _(dve):
                with dve.Fori(0, GROUPS, 1) as g:
                    step = Steps(dve, done, STEPS, g)
                    dinv = k["dinv"][:, bass.ds(g, 1), :].rearrange("p g q -> p (g q)")[:, :, None]\
                        .broadcast_to([NT, GROUP, FEAT])
                    as_rows = lambda ps: ps[:, 0:GROUP * FEAT].rearrange("p (q f) -> p q f", q=GROUP)
                    dve.wait_ge(turned, g * TURNED + 1)
                    dve.wait_ge(u_loaded, g * 16 + 16)
                    step.wait(step(dve.tensor_tensor(z[:, :, :], as_rows(agg_ps), u[:, :, :], ALU.add)))
                    step(dve.tensor_tensor(z[:, :, :], z[:, :, :], dinv, ALU.mult))
                    dve.wait_ge(stored, g * 16)
                    dve.wait_ge(turned, g * TURNED + 4)
                    step(dve.tensor_tensor(o[:, :, :], as_rows(o_ps), dinv, ALU.mult))


def conv2_nodes(nc, a, k, u_in, x_in, x_out):
    ctx, sb, sem, psum = node_phase(nc, "conv2_nodes")
    with ctx:
        u, x, sums = sb("u", [NT, GROUP, FEAT]), sb("x", [NT, GROUP, FEAT]), sb("sums", [FEAT, GN])
        z, bias = sb("z", [NT, GROUP, FEAT]), sb("bias", [NT, FEAT])
        b = norm_buffers(sb)
        agg_ps = psum("agg", [NT, 512])
        params, loaded, copied, turned, done, root_ready, stored = (
            sem(n) for n in ("params", "loaded", "copied", "turned", "done", "root_ready", "stored"))
        STEPS = 12
        with nc.Block() as block:
            @block.sync
            def _(sp):
                sp.dma_start(bias[:, :], a["L2_gnn_b2"].rearrange("(o n) -> o n", o=1).broadcast_to([NT, FEAT]))\
                  .then_inc(params, 16)
                sp.dma_start(u[:, :, :], node_rows(u_in, 0)).then_inc(loaded, 16)
                sp.dma_start(x[:, :, :], node_rows(x_in, 0)).then_inc(loaded, 16)
                with sp.Fori(0, GROUPS, 1) as g:
                    sp.wait_ge(done, g * STEPS + STEPS)
                    sp.dma_start(node_rows(x_out, g), b["xn"][:, :, :]).then_inc(stored, 16)
                    sp.wait_ge(stored, g * 16 + 16)
                    sp.dma_start(u[:, :, :], node_rows(u_in, next_group(g))).then_inc(loaded, 16)
                    sp.dma_start(x[:, :, :], node_rows(x_in, next_group(g))).then_inc(loaded, 16)
                sp.wait_ge(loaded, 32 * (GROUPS + 1))
                sp.wait_ge(stored, 16 * GROUPS)

            @block.tensor
            def _(pe):
                pe.wait_ge(params, 16)
                with pe.Fori(0, GROUPS, 1) as g:
                    pe.wait_ge(done, g * STEPS)
                    pe.wait_ge(copied, g + 1)
                    for q in range(GROUP):
                        mm = pe.matmul(agg_ps[:, q * FEAT:(q + 1) * FEAT], sums[:, q * NT:(q + 1) * NT],
                                       k["ident"][0:FEAT, 0:FEAT], start=True, stop=True)
                    mm.then_inc(turned, 1)

            @block.scalar
            def _(act):
                with act.Fori(0, GROUPS, 1) as g:
                    act.wait_ge(turned, g)
                    nc.scalar.activation(sums[:, :], k["acc"][0:FEAT, 0, bass.ds(g * GN, GN)], ACT.Copy).then_inc(copied, 1)
                    act.wait_ge(done, g * STEPS + 10)
                    nc.scalar.activation(b["root"][:, :], b["var"][:, :], ACT.Sqrt, scale=1.0 / FEAT,
                                         bias=k["eps"][0:NT, 0:1]).then_inc(root_ready, 1)

            @block.vector
            def _(dve):
                dve.wait_ge(params, 16)
                with dve.Fori(0, GROUPS, 1) as g:
                    step = Steps(dve, done, STEPS, g)
                    wide = [NT, GROUP, FEAT]
                    dinv = k["dinv"][:, bass.ds(g, 1), :].rearrange("p g q -> p (g q)")[:, :, None].broadcast_to(wide)
                    dve.wait_ge(turned, g + 1)
                    dve.wait_ge(loaded, g * 32 + 32)
                    dve.wait_ge(stored, g * 16)
                    step.wait(step(dve.tensor_tensor(
                        z[:, :, :], agg_ps[:, 0:GROUP * FEAT].rearrange("p (q f) -> p q f", q=GROUP), u[:, :, :], ALU.add)))
                    step.wait(step(dve.tensor_tensor(z[:, :, :], z[:, :, :], dinv, ALU.mult)))
                    step.wait(step(dve.tensor_tensor(z[:, :, :], z[:, :, :], bias[:, None, :].broadcast_to(wide), ALU.add)))
                    step.wait(step(dve.tensor_scalar(z[:, :, :], z[:, :, :], 0.0, None, ALU.max)))
                    step.wait(step(dve.tensor_tensor(b["y"][:, :, :], z[:, :, :], x[:, :, :], ALU.add)))
                    normalise(nc, step, dve, b, root_ready, g)


def kernel(**inputs):
    import concourse.bacc as bacc
    from concourse.bass_utils import run_bass_kernel_spmd

    v = {n: np.asarray(x) for n, x in inputs.items()}
    coef, mix = coupling_layout(v["L1_gnn_W"])
    dst = np.concatenate([v["dst"], np.full(BLOCKS * BLOCK - EDGES, -1, v["dst"].dtype)])
    arrays = {
        "x": v["x"], "dst": v["dst"],
        "dst_lanes": np.ascontiguousarray(dst.reshape(BLOCKS * TILES, P).T),
        "src_blocks": edge_order(v["src"]),
        "sh4": edge_order(v["edge_attr_4"]),
        "sh9": edge_order(np.concatenate([v["edge_weight1"], v["edge_attr_3"], v["edge_attr_5"]], 1)),
        "ef32": edge_major(v["edge_attr_32"]), "ef8": edge_major(v["edge_attr_8"]),
        "L0_self": irrep_blocks(v["L0_gnn_si_w0"], v["L0_gnn_si_w1"]),
        "L3_self": irrep_blocks(v["L3_gnn_Ws"], v["L3_gnn_Wv"]),
        "L1_mix": mix, "L1_coef": coef,
        "L0_gnn_W2": path_columns(v["L0_gnn_W2"], (3, 0, 1, 2)),
        "L0_gnn_b2": path_columns(v["L0_gnn_b2"][None], (3, 0, 1, 2))[0],
        "L3_gnn_W3": path_columns(v["L3_gnn_W3"], (1, 0, 2, 3)),
        "L3_gnn_b3": path_columns(v["L3_gnn_b3"][None], (1, 0, 2, 3))[0],
    }
    for n in ("L0_gnn_W1", "L0_gnn_b1", "L2_gnn_W1", "L2_gnn_b1", "L2_gnn_W2", "L2_gnn_b2",
              "L3_gnn_W1", "L3_gnn_b1", "L3_gnn_W2", "L3_gnn_b2"):
        arrays[n] = v[n]
    nc = bacc.Bacc("TRN2", target_bir_lowering=False, num_devices=1)
    aps = {n: nc.dram_tensor(f"in_{n}", x.shape, mybir.dt.from_np(x.dtype), kind="ExternalInput").ap()
           for n, x in arrays.items()}
    out = nc.dram_tensor("out", [NODES, FEAT], F32, kind="ExternalOutput").ap()
    build(nc, aps, out)
    r = run_bass_kernel_spmd(nc, [{f"in_{n}": x for n, x in arrays.items()}], core_ids=[0])
    return r.results[0]["out"]
```

```python
from contextlib import ExitStack

import concourse.bass as bass
import numpy as np
from concourse import mybir

F32 = mybir.dt.float32
I32 = mybir.dt.int32
U32 = mybir.dt.uint32
ALU = mybir.AluOpType
ACT = mybir.ActivationFunctionType
AX = mybir.AxisListType.X
DVE_ONLY = [mybir.EngineType.DVE]

NODES, EDGES, FEAT, MUL = 12500, 400000, 32, 8
P = 128
TILES = 5
BLOCK = TILES * P
SLOTS = 4
REAL_BLOCKS = EDGES // BLOCK
TURNS = -(-REAL_BLOCKS // SLOTS)
BLOCKS = TURNS * SLOTS
WINDOW = 64
ACC = NODES + WINDOW
HID = 64
WPATHS = 4 * MUL * MUL
HARM = 9
OUTER = 4 * FEAT + 5 * 3 * MUL
OCH = 125
NT = 125
GROUP = 4
GN = NT * GROUP
GROUPS = NODES // GN
EPS = 1e-5
HALF = BLOCK // 2
TO_S, V_V = 2 * MUL * MUL, 3 * MUL * MUL // 2
WCH = (TO_S + V_V + 3 * MUL) // 2
LO_SPLIT = REAL_BLOCKS // 125


def edge_order(a, fill=0):
    a = np.concatenate([a, np.full((BLOCKS * BLOCK - EDGES,) + a.shape[1:], fill, a.dtype)])
    a = a.reshape((BLOCKS, TILES, P) + a.shape[1:])
    a = np.moveaxis(a, 1, 2)
    return np.ascontiguousarray(np.concatenate([a, a[:SLOTS]]))


def edge_major(a):
    a = np.concatenate([a, np.zeros((BLOCKS * BLOCK - EDGES, a.shape[1]), a.dtype)])
    a = np.moveaxis(a.reshape(BLOCKS, BLOCK, -1), 1, 2)
    return np.ascontiguousarray(np.concatenate([a, a[:SLOTS]]))


def path_columns(w, order):
    w = w.reshape(-1, 4, MUL, MUL)
    vv_s, ss_s, s_v, v_v = (w[:, p] for p in order)
    scalars = np.stack([vv_s, ss_s], 1)
    return np.ascontiguousarray(np.concatenate([
        scalars.transpose(0, 3, 1, 2).reshape(len(w), 2 * MUL * MUL),
        s_v.transpose(0, 2, 1).reshape(len(w), MUL * MUL),
        v_v.transpose(0, 2, 1).reshape(len(w), MUL * MUL)], 1))


def half_rows(blocks):
    b, n, _ = blocks.shape
    return np.ascontiguousarray(blocks.reshape(b, n, 2, HALF).transpose(0, 2, 1, 3)).reshape(b, 2 * n, HALF)


def message_sums():
    m = np.zeros((2 * WCH, FEAT), np.float32)
    vector = np.arange(3 * MUL).reshape(MUL, 3) + MUL
    m[np.arange(TO_S), np.repeat(np.arange(MUL), 2 * MUL)] = 1
    m[TO_S + np.arange(V_V), np.repeat(vector.T.reshape(-1), MUL // 2)] = 1
    m[TO_S + V_V + np.arange(3 * MUL), vector.reshape(-1)] = 1
    return m.reshape(2, WCH, FEAT)


def irrep_blocks(w0, w1):
    m = np.zeros((FEAT, FEAT), w0.dtype)
    m[:MUL, :MUL] = w0
    for c in range(3):
        m[MUL + c::3, MUL + c::3] = w1
    return m


def coupling(l1, l2, l3):
    from math import factorial as f, sqrt

    def su2(j1, m1, j2, m2, j3, m3):
        if m3 != m1 + m2:
            return 0.0
        vmin = max(0, j2 - j3 - m1, j1 + m2 - j3)
        vmax = min(j1 + j2 - j3, j1 - m1, j2 + m2)
        pref = (2 * j3 + 1) * f(j3 + j1 - j2) * f(j3 - j1 + j2) * f(j1 + j2 - j3) / f(j1 + j2 + j3 + 1)
        pref *= f(j3 + m3) * f(j3 - m3) * f(j1 - m1) * f(j1 + m1) * f(j2 - m2) * f(j2 + m2)
        s = 0.0
        for v in range(vmin, vmax + 1):
            s += (-1) ** v / (f(v) * f(j1 + j2 - j3 - v) * f(j1 - m1 - v) * f(j2 + m2 - v)
                              * f(j3 - j2 + m1 + v) * f(j3 - j1 - m2 + v))
        return sqrt(pref) * s

    def q(l):
        m = np.zeros((2 * l + 1, 2 * l + 1), np.complex128)
        for k in range(-l, 0):
            m[l + k, l - k] = 1 / sqrt(2)
            m[l + k, l + k] = -1j / sqrt(2)
        m[l, l] = 1
        for k in range(1, l + 1):
            m[l + k, l + k] = (-1) ** k / sqrt(2)
            m[l + k, l - k] = 1j * (-1) ** k / sqrt(2)
        return (-1j) ** l * m

    c = np.zeros((2 * l1 + 1, 2 * l2 + 1, 2 * l3 + 1), np.complex128)
    for a in range(-l1, l1 + 1):
        for b in range(-l2, l2 + 1):
            if -l3 <= a + b <= l3:
                c[a + l1, b + l2, a + b + l3] = su2(l1, a, l2, b, l3, a + b)
    c = np.einsum("ij,kl,mn,ikn->jlm", q(l1), q(l2), np.conj(q(l3)).T, c).real
    return (c / np.linalg.norm(c)).astype(np.float32)


def coupling_layout(w):
    cg = {c: coupling(*c) for c in [(0, 0, 0), (0, 1, 1), (1, 0, 1), (1, 1, 0), (1, 1, 1), (2, 1, 1)]}
    coef = np.zeros((2 * OCH, FEAT + 1), np.float32)
    weight = np.zeros((2 * OCH, FEAT + 1), w.dtype)
    for path, (le, ln, lo) in enumerate(cg):
        c = cg[le, ln, lo]
        for a in range(2 * le + 1):
            for m in range(2 * ln + 1):
                for k in range(2 * lo + 1):
                    for i in range(MUL):
                        feat = i if ln == 0 else MUL + 3 * i + m
                        row = {0: 0, 1: FEAT * (1 + a)}[le] + feat if le < 2 else \
                            4 * FEAT + 3 * MUL * a + feat - MUL
                        for o in range(MUL):
                            col = o if lo == 0 else MUL + 3 * o + k
                            coef[row, col] = c[a, m, k]
                            weight[row, col] = w[path, i, o]
    coef[OUTER, FEAT] = 1
    weight[OUTER, FEAT] = 1
    return coef.reshape(2, OCH, FEAT + 1), weight.reshape(2, OCH, FEAT + 1)


def build(nc, a, out):
    with ExitStack() as ctx:
        dram = lambda name, shape, dt: nc.dram_tensor(name, shape, dt, kind="Internal").ap()
        sb = lambda name, shape, dt=F32: ctx.enter_context(nc.sbuf_tensor(name, shape, dt))
        x1, x2, x3 = (dram(f"x_after_{n}", [NODES, FEAT], F32) for n in ("weighted0", "coupled", "convolved"))
        u1, u2 = (dram(f"conv_rows_{n}", [NODES, FEAT], F32) for n in (1, 2))
        lo_row = dram("lowest_target", [1, BLOCKS], F32)
        span_row = dram("target_span", [1, 125], F32)
        k = {
            "nc": nc,
            "acc": sb("acc", [P, 2, ACC]),
            "local": sb("local", [P, BLOCKS, TILES]),
            "iota0": sb("iota0", [P, WINDOW]),
            "lo": sb("lo", [1, BLOCKS]),
            "passes": sb("passes", [1, 1], I32),
            "ident": sb("ident", [P, P]),
            "dinv": sb("dinv", [NT, GROUPS, GROUP]),
            "eps": sb("eps", [P, 1]),
        }
        setup(nc, a, k, lo_row, span_row)
        weighted_edges(nc, a, k, "weighted0", a["x"], "ef32", FEAT, ["L0_gnn_W1", "L0_gnn_W2"],
                       ["L0_gnn_b1", "L0_gnn_b2"], ACT.Relu)
        weighted_nodes(nc, a, k, "weighted0", a["x"], x1, "L0_self", 0.25, 1 / np.sqrt(MUL))
        coupled_edges(nc, a, k, x1)
        coupled_nodes(nc, a, k, x1, x2, u1)
        conv_edges(nc, a, k, "conv1", u1)
        conv1_nodes(nc, a, k, u1, u2)
        conv_edges(nc, a, k, "conv2", u2)
        conv2_nodes(nc, a, k, u2, x2, x3)
        weighted_edges(nc, a, k, "weighted3", x3, "ef8", MUL, ["L3_gnn_W1", "L3_gnn_W2", "L3_gnn_W3"],
                       ["L3_gnn_b1", "L3_gnn_b2", "L3_gnn_b3"], ACT.Silu)
        weighted_nodes(nc, a, k, "weighted3", x3, out, "L3_self", 0.25 / 4, 1 / np.sqrt(MUL))


def setup(nc, a, k, lo_row, span_row):
    with ExitStack() as ctx:
        sb = lambda name, shape, dt=F32: ctx.enter_context(nc.sbuf_tensor(name, shape, dt))
        sem = lambda name: ctx.enter_context(nc.semaphore(name))
        by_block = sb("by_block", [125, LO_SPLIT, BLOCK], I32)
        by_block_f = sb("by_block_f", [125, LO_SPLIT, BLOCK])
        by_lane = sb("by_lane", [P, BLOCKS * TILES], I32)
        lowest = sb("lowest", [125, LO_SPLIT])
        highest = sb("highest", [125, LO_SPLIT])
        span = sb("span", [125, LO_SPLIT])
        span_max = sb("span_max", [125, 1])
        none = sb("none", [1, BLOCKS - REAL_BLOCKS])
        lo_all = sb("lo_all", [P, BLOCKS])
        spans = sb("spans", [1, 125])
        widest = sb("widest", [1, 1])
        blocks_loaded, lanes_loaded = sem("blocks_loaded"), sem("lanes_loaded")
        found, lo_stored, lo_loaded, made = sem("found"), sem("lo_stored"), sem("lo_loaded"), sem("made")
        spans_loaded = sem("spans_loaded")
        with nc.Block() as block:
            @block.sync
            def _(sp):
                sp.dma_start(by_block[:, :, :], a["dst"].rearrange("(p b e) -> p b e", b=LO_SPLIT, e=BLOCK))\
                  .then_inc(blocks_loaded, 16)
                sp.dma_start(by_lane[:, :], a["dst_lanes"]).then_inc(lanes_loaded, 16)
                sp.wait_ge(found, 7)
                sp.dma_start(lo_row[0:1, 0:REAL_BLOCKS].rearrange("o (p b) -> (o p) b", b=LO_SPLIT), lowest[:, :])\
                  .then_inc(lo_stored, 16)
                sp.dma_start(lo_row[0:1, REAL_BLOCKS:BLOCKS], none[:, :]).then_inc(lo_stored, 16)
                sp.dma_start(span_row.rearrange("o p -> p o"), span_max[:, :]).then_inc(lo_stored, 16)
                sp.wait_ge(lo_stored, 48)
                sp.dma_start(k["lo"][:, :], lo_row).then_inc(lo_loaded, 16)
                sp.dma_start(lo_all[:, :], lo_row.broadcast_to([P, BLOCKS])).then_inc(lo_loaded, 16)
                sp.dma_start(spans[:, :], span_row).then_inc(spans_loaded, 16)

            @block.gpsimd
            def _(pool):
                pool.memset(k["ident"][:, :], 0.0).then_inc(made, 1)
                pool.wait_ge(made, 1)
                pool.affine_select(out=k["ident"][:, :], in_=k["ident"][:, :], compare_op=ALU.not_equal, fill=1.0,
                                   base=0, pattern=[[-1, P]], channel_multiplier=1).then_inc(made, 1)
                pool.iota(k["iota0"][:, :], pattern=[[1, WINDOW]], base=0, channel_multiplier=0,
                          allow_small_or_imprecise_dtypes=True).then_inc(made, 1)
                pool.wait_ge(made, 3)

            @block.vector
            def _(dve):
                dve.memset(k["eps"][:, :], EPS).then_inc(found, 1)
                dve.memset(none[:, :], 0.0).then_inc(found, 1)
                dve.wait_ge(blocks_loaded, 16)
                dve.tensor_copy(by_block_f[:, :, :], by_block[:, :, :]).then_inc(found, 1)
                dve.wait_ge(found, 3)
                dve.tensor_reduce(lowest[:, :], by_block_f[:, :, :], AX, ALU.min).then_inc(found, 1)
                dve.tensor_reduce(highest[:, :], by_block_f[:, :, :], AX, ALU.max).then_inc(found, 1)
                dve.wait_ge(found, 5)
                dve.tensor_tensor(span[:, :], highest[:, :], lowest[:, :], ALU.subtract).then_inc(found, 1)
                dve.wait_ge(found, 6)
                dve.tensor_reduce(span_max[:, :], span[:, :], AX, ALU.max).then_inc(found, 1)
                dve.wait_ge(lanes_loaded, 16)
                dve.tensor_copy(k["local"][:, :, :], by_lane[:, :].rearrange("p (b t) -> p b t", t=TILES))\
                   .then_inc(found, 1)
                dve.wait_ge(found, 8)
                dve.wait_ge(lo_loaded, 32)
                dve.tensor_tensor(k["local"][:, :, :], k["local"][:, :, :],
                                  lo_all[:, :, None].broadcast_to([P, BLOCKS, TILES]), ALU.subtract)\
                   .then_inc(found, 1)
                dve.wait_ge(spans_loaded, 16)
                dve.tensor_reduce(widest[:, :], spans[:, :], AX, ALU.max).then_inc(found, 1)
                dve.wait_ge(found, 10)
                dve.tensor_copy(k["passes"][:, :], widest[:, :]).then_inc(found, 1)
                dve.wait_ge(found, 11)


def hold(engine, sem, value, passed):
    engine.wait_ge(sem, value)
    engine.sem_inc(passed, 1)


class Turns:

    def __init__(self, engine, k):
        self.engine = engine
        self.passes = engine.value_load(k["passes"][0:1, 0:1], min_val=0, max_val=NODES) // WINDOW + 1

    def flat(self):
        return self.engine.Fori(0, self.passes * TURNS, 1)


def load_blocks(sp, k, loads, used, loaded, ended):
    def fill(slot, block):
        for dst, src in loads:
            sp.dma_start(dst[slot], src(block)).then_inc(loaded[slot], 16)

    turns = Turns(sp, k)
    for s in range(SLOTS):
        fill(s, 0 * SLOTS + s)
    with sp.Fori(0, turns.passes, 1) as p:
        with sp.Fori(0, TURNS, 1) as i:
            for s in range(SLOTS):
                sp.wait_ge(used, (p * TURNS + i) * SLOTS + s + 1)
                fill(s, i * SLOTS + (SLOTS + s))
    for s in range(SLOTS):
        hold(sp, loaded[s], (turns.passes * TURNS + 1) * (16 * len(loads)), ended)


def gather_rows(pool, k, table, idx, rows, loaded, per_load, gathered, started):
    turns = Turns(pool, k)
    with turns.flat() as g:
        for s in range(SLOTS):
            hold(pool, loaded[s], (g + 1) * per_load, started)
            for t in range(TILES):
                pool.indirect_dma_start(rows[s][:, t, :], None, table,
                                        bass.IndirectOffsetOnAxis(ap=idx[s][:, t:t + 1].bitcast(U32), axis=0))\
                    .then_inc(gathered[s], 16)


class Windows:

    def __init__(self, dve, k, iota, base_f, base, stepped, parts):
        self.dve, self.k, self.iota, self.base_f, self.base, self.stepped = dve, k, iota, base_f, base, stepped
        dve.memset(k["acc"][0:parts[0], 0:parts[1], :], 0.0).then_inc(stepped, 1)
        dve.tensor_copy(iota[:, :], k["iota0"][:, :]).then_inc(stepped, 1)
        dve.memset(base_f[:, :], float(NODES)).then_inc(stepped, 1)
        dve.wait_ge(stepped, 3)
        dve.tensor_copy(base_f[:, 1:BLOCKS + 1], k["lo"][:, :]).then_inc(stepped, 1)
        dve.wait_ge(stepped, 4)
        dve.tensor_copy(base[:, :], base_f[:, :]).then_inc(stepped, 1)
        dve.wait_ge(stepped, 5)

    def next_window(self, p):
        dve = self.dve
        dve.tensor_scalar(self.iota[:, :], self.iota[:, :], float(WINDOW), None, ALU.add).then_inc(self.stepped, 1)
        dve.tensor_scalar(self.base_f[:, :], self.base_f[:, :], float(WINDOW), float(NODES), ALU.add, ALU.min)\
           .then_inc(self.stepped, 1)
        dve.wait_ge(self.stepped, p * 3 + 7)
        dve.tensor_copy(self.base[:, :], self.base_f[:, :]).then_inc(self.stepped, 1)
        dve.wait_ge(self.stepped, p * 3 + 8)

    def bases(self, block, count=SLOTS):
        return nc_values(self.k["nc"], self.base[0:1, bass.ds(block + 1, count)])

    def one_hot(self, dst, block):
        return self.dve.tensor_tensor(
            dst[:, :, :], self.iota[:, None, :].broadcast_to([P, TILES, WINDOW]),
            self.k["local"][:, bass.ds(block, 1), :].rearrange("p b t -> p (b t)")[:, :, None]
            .broadcast_to([P, TILES, WINDOW]), ALU.is_equal)


def nc_values(nc, row):
    return nc.values_load_multi_w_load_instructions(row, engines=DVE_ONLY, min_val=0, max_val=NODES)[1]


def weighted_edges(nc, a, k, name, table, feats, fan_in, weights, biases, func):
    deep = len(weights) == 3
    halves = 2 if deep else 1
    fan_rows = halves * fan_in
    with ExitStack() as ctx:
        sb = lambda n, shape, dt=F32: ctx.enter_context(nc.sbuf_tensor(f"{name}_{n}", shape, dt))
        sem = lambda n: ctx.enter_context(nc.semaphore(f"{name}_{n}"))
        ring = lambda n, shape, dt=F32: [sb(f"{n}{s}", shape, dt) for s in range(SLOTS)]
        psum = lambda n, shape: ctx.enter_context(nc.psum_tensor(f"{name}_{n}_ps", shape, F32))
        idx, feat, sh = ring("idx", [P, TILES], I32), ring("feat", [fan_rows, BLOCK // halves]), ring("sh", [P, TILES, 4])
        rows, onehot, prod = ring("rows", [P, TILES, FEAT]), ring("onehot", [P, TILES, WINDOW]), ring("prod", [P, TILES, 2 * WCH])
        hidden = ring("hidden", [P, BLOCK])
        first = sb("first", [P, HALF])
        w_in, w_mid, w_out = sb("w_in", [fan_rows, halves * HID]), sb("w_mid", [P, 2, HID]), sb("w_out", [P, WPATHS])
        b_in, b_mid = sb("b_in", [halves * HID, 1]), sb("b_mid", [HID, 1])
        iota, base_f, base = sb("iota", [P, WINDOW]), sb("base_f", [1, BLOCKS + SLOTS]), sb("base", [1, BLOCKS + SLOTS], I32)
        vsh = sb("vsh", [P, TILES, MUL, 3])
        scaled = sb("scaled", [P, TILES, MUL + FEAT])
        s_v = sb("s_v", [P, TILES, MUL, MUL])
        v_v = sb("v_v", [P, TILES, 3 * MUL, MUL])
        sums = sb("sums", [P, TILES, MUL])
        banks = [psum("weights0", [P, 3 * 512]), psum("weights1", [P, 3 * 512])]
        hid_ps = psum("hid", [P, 512])
        win_ps = psum("win", [P, 512])
        loaded, gathered = [sem(f"loaded{s}") for s in range(SLOTS)], [sem(f"gathered{s}") for s in range(SLOTS)]
        params, ones = sem("params"), sem("ones")
        pre_ready, hidden_ready = sem("pre_ready"), sem("hidden_ready")
        w_ready, w_used = sem("w_ready"), sem("w_used")
        vec, summed, msg_ready = sem("vec"), sem("summed"), sem("msg_ready")
        spread, stepped = sem("spread"), sem("stepped")
        started, ended, held, zeroed = sem("started"), sem("ended"), sem("held"), sem("zeroed")
        PARAMS = 16 * (4 if not deep else 9)
        PER_BLOCK = 3 if deep else 2
        VEC = 6
        ZEROED = SLOTS + 3

        with nc.Block() as block:
            @block.sync
            def _(sp):
                sp.wait_ge(ones, ZEROED)
                for h in range(halves):
                    sp.dma_start(w_in[h * fan_in:(h + 1) * fan_in, h * HID:(h + 1) * HID], a[weights[0]]).then_inc(params, 16)
                    sp.dma_start(b_in[h * HID:(h + 1) * HID, :], a[biases[0]].rearrange("(h o) -> h o", o=1))\
                      .then_inc(params, 16)
                if deep:
                    for h in range(2):
                        sp.dma_start(w_mid[h * HID:(h + 1) * HID, h, :], a[weights[1]]).then_inc(params, 16)
                    sp.dma_start(b_mid[:, :], a[biases[1]].rearrange("(h o) -> h o", o=1)).then_inc(params, 16)
                sp.dma_start(w_out[0:HID, :], a[weights[-1]]).then_inc(params, 16)
                sp.dma_start(w_out[HID:HID + 1, :], a[biases[-1]].rearrange("(o n) -> o n", o=1)).then_inc(params, 16)
                load_blocks(sp, k, [
                    ([x[:, :] for x in idx], lambda b: one(a["src_blocks"], b)),
                    ([x[:, :, :].rearrange("p t c -> p (t c)") for x in sh],
                     lambda b: one(a["sh4"], b, "b p t c -> p (b t c)")),
                    ([x[:, :] for x in feat], lambda b: one(a[feats], b)),
                ], msg_ready, loaded, ended)

            @block.gpsimd
            def _(pool):
                gather_rows(pool, k, table, idx, rows, loaded, 48, gathered, started)

            @block.tensor
            def _(pe):
                def hidden_mm(b, slot, u):
                    if isinstance(b, int) and b * PER_BLOCK + u == 0:
                        pe.wait_ge(params, PARAMS)
                    else:
                        hold(pe, hidden_ready, b * PER_BLOCK + u, held)
                    if deep and u > 0:
                        mm = pe.matmul(hid_ps[0:HID, 0:HALF], w_mid[:, u - 1, :], first[:, :], start=True, stop=True)
                    else:
                        mm = pe.matmul(hid_ps[0:halves * HID, 0:HALF], w_in[:, :], feat[slot][:, u * HALF:(u + 1) * HALF],
                                       start=True, stop=True)
                    mm.then_inc(pre_ready, 1)

                def weight_mm(b, slot, bank, tiles):
                    for t in tiles:
                        if t == 0:
                            pe.wait_ge(hidden_ready, (b + 1) * PER_BLOCK)
                            if not (isinstance(b, int) and b == 0):
                                pe.wait_ge(w_used, b - 1)
                        mm = pe.matmul(banks[bank][:, t * WPATHS:(t + 1) * WPATHS],
                                       hidden[slot][:, t * P:(t + 1) * P], w_out[:, :], start=True, stop=True)
                        if t == TILES - 1:
                            mm.then_inc(w_ready, 1)

                def both(b_h, slot_h, turn_h, b_w, slot_w, bank_w):
                    pe.wait_ge(loaded[slot_h], turn_h * 48 + 48)
                    hidden_mm(b_h, slot_h, 0)
                    weight_mm(b_w, slot_w, bank_w, [0, 1])
                    hidden_mm(b_h, slot_h, 1)
                    weight_mm(b_w, slot_w, bank_w, [2, 3])
                    if deep:
                        hidden_mm(b_h, slot_h, 2)
                    weight_mm(b_w, slot_w, bank_w, [4])

                turns = Turns(pe, k)
                pe.wait_ge(ones, ZEROED + SLOTS + 1)
                pe.wait_ge(loaded[0], 48)
                for u in range(PER_BLOCK):
                    hidden_mm(0, 0, u)
                both(1, 1, 0, 0, 0, 0)
                with pe.Fori(0, turns.passes, 1) as p:
                    with pe.Fori(0, TURNS, 1) as i:
                        g = p * TURNS + i
                        for s in range(SLOTS):
                            n = g * SLOTS + s
                            both(n + 2, (s + 2) % SLOTS, g + (s + 2) // SLOTS, n + 1, (s + 1) % SLOTS, (s + 1) % 2)
                            pe.wait_ge(summed, n + p + 1)
                            pe.wait_ge(msg_ready, n + 1)
                            for c in range(2):
                                for t in range(TILES):
                                    mm = pe.matmul(win_ps[0:WCH, c * WINDOW:(c + 1) * WINDOW],
                                                   prod[s][:, t, c * WCH:(c + 1) * WCH], onehot[s][:, t, :],
                                                   start=(t == 0), stop=(t == TILES - 1))
                            mm.then_inc(spread, 1)

            @block.scalar
            def _(act):
                def block_act(b, slot):
                    for u in range(PER_BLOCK):
                        act.wait_ge(pre_ready, b * PER_BLOCK + u + 1)
                        if deep and u == 0:
                            step = nc.scalar.activation(first[:, :], hid_ps[:, 0:HALF], func, bias=b_in[:, 0:1])
                        else:
                            half = u - 1 if deep else u
                            step = nc.scalar.activation(
                                hidden[slot][0:HID, half * HALF:(half + 1) * HALF], hid_ps[0:HID, 0:HALF], func,
                                bias=(b_mid if deep else b_in)[:, 0:1])
                        step.then_inc(hidden_ready, 1)

                turns = Turns(act, k)
                act.wait_ge(params, PARAMS)
                block_act(0, 0)
                block_act(1, 1)
                with turns.flat() as g:
                    for s in range(SLOTS):
                        block_act(g * SLOTS + s + 2, (s + 2) % SLOTS)

            @block.vector
            def _(dve):
                for s in range(SLOTS):
                    dve.memset(hidden[s][HID:, :], 0.0).then_inc(ones, 1)
                dve.memset(w_out[HID:, :], 0.0).then_inc(ones, 1)
                dve.memset(w_in[:, :], 0.0).then_inc(ones, 1)
                dve.memset(w_mid[:, :, :], 0.0).then_inc(ones, 1)
                dve.wait_ge(ones, ZEROED)
                for s in range(SLOTS):
                    dve.memset(hidden[s][HID:HID + 1, :], 1.0).then_inc(ones, 1)
                dve.wait_ge(params, PARAMS)
                dots = w_out[0:HID + 1, 0:2 * MUL * MUL].rearrange("h (o q i) -> h o q i", q=2, i=MUL)[:, :, 0, :]
                dve.tensor_scalar(dots, dots, float(1 / np.sqrt(3.0)), None, ALU.mult).then_inc(ones, 1)
                win = Windows(dve, k, iota, base_f, base, stepped, (WCH, 2))
                dve.memset(win_ps[0:WCH, 0:2 * WINDOW], 0.0).then_inc(zeroed, 1)
                dve.wait_ge(zeroed, 1)
                turns = Turns(dve, k)

                def add_window(count, at):
                    dve.wait_ge(summed, count)
                    dst = k["acc"][0:WCH, :, bass.ds(at, WINDOW)]
                    dve.tensor_tensor(dst, dst, win_ps[0:WCH, 0:2 * WINDOW].rearrange("p (c w) -> p c w", c=2),
                                      ALU.add).then_inc(summed, 1)

                with dve.Fori(0, turns.passes, 1) as p:
                    with dve.Fori(0, TURNS, 1) as i:
                        g = p * TURNS + i
                        before = win.bases(i * SLOTS - 1)
                        for s in range(SLOTS):
                            n = g * SLOTS + s
                            x, h = rows[s], sh[s]
                            harm = h[:, :, 1:4][:, :, None, :].broadcast_to([P, TILES, MUL, 3])
                            vecs = x[:, :, MUL:].rearrange("p t (i m) -> p t i m", m=3)
                            win.one_hot(onehot[s], i * SLOTS + s).then_inc(vec, 1)
                            dve.wait_ge(gathered[s], g * (16 * TILES) + 16 * TILES)
                            dve.wait_ge(loaded[s], g * 48 + 48)
                            dve.tensor_tensor(vsh[:, :, :, :], vecs, harm, ALU.mult).then_inc(vec, 1)
                            dve.tensor_tensor(scaled[:, :, MUL:], x[:, :, :],
                                              h[:, :, 0:1].broadcast_to([P, TILES, FEAT]), ALU.mult).then_inc(vec, 1)
                            dve.wait_ge(vec, n * VEC + 2)
                            dve.tensor_reduce(scaled[:, :, 0:MUL], vsh[:, :, :, :], AX, ALU.add).then_inc(vec, 1)
                            dve.wait_ge(w_ready, n + 1)
                            w = banks[s % 2][:, 0:TILES * WPATHS].rearrange("p (t n) -> p t n", t=TILES)
                            w_s = w[:, :, 0:2 * MUL * MUL].rearrange("p t (o i) -> p t o i", o=MUL)
                            w_sv = w[:, :, 2 * MUL * MUL:3 * MUL * MUL].rearrange("p t (o i) -> p t o i", o=MUL)
                            w_vv = w[:, :, 3 * MUL * MUL:].rearrange("p t (o i) -> p t o i", o=MUL)
                            dve.tensor_tensor(s_v[:, :, :, :], w_sv,
                                              x[:, :, None, 0:MUL].broadcast_to([P, TILES, MUL, MUL]), ALU.mult)
                            dve.wait_ge(vec, n * VEC + 4)
                            for m in range(3):
                                v_m = scaled[:, :, 2 * MUL:].rearrange("p t (i m) -> p t m i", m=3)[:, :, m]
                                last = dve.tensor_tensor(
                                    v_v[:, :, m * MUL:(m + 1) * MUL, :], w_vv,
                                    v_m[:, :, None, :].broadcast_to([P, TILES, MUL, MUL]), ALU.mult)
                            last.then_inc(vec, 1)
                            dve.tensor_tensor(prod[s][:, :, 0:TO_S].rearrange("p t (o i) -> p t o i", o=MUL), w_s,
                                              scaled[:, :, None, 0:2 * MUL].broadcast_to([P, TILES, MUL, 2 * MUL]),
                                              ALU.mult).then_inc(w_used, 1)
                            dve.wait_ge(spread, n)
                            add_window(n + p, before[s])
                            dve.wait_ge(vec, n * VEC + 5)
                            dve.tensor_reduce(sums[:, :, :], s_v[:, :, :, :], AX, ALU.add).then_inc(vec, 1)
                            dve.tensor_tensor(
                                prod[s][:, :, TO_S:TO_S + V_V].rearrange("p t (o i) -> p t o i", i=MUL // 2),
                                v_v[:, :, :, 0:MUL // 2], v_v[:, :, :, MUL // 2:], ALU.add)
                            dve.wait_ge(vec, n * VEC + 6)
                            dve.tensor_tensor(prod[s][:, :, TO_S + V_V:].rearrange("p t (o m) -> p t o m", m=3),
                                              sums[:, :, :, None].broadcast_to([P, TILES, MUL, 3]), harm,
                                              ALU.mult).then_inc(msg_ready, 1)
                    last_base = win.bases(BLOCKS - 1, 1)[0]
                    dve.wait_ge(spread, (p + 1) * BLOCKS)
                    add_window((p + 1) * BLOCKS + p, last_base)
                    win.next_window(p)


def one(src, b, to="b p t -> p (b t)"):
    return src[bass.ds(b, 1)].rearrange(to)


def coupled_edges(nc, a, k, table):
    with ExitStack() as ctx:
        sb = lambda n, shape, dt=F32: ctx.enter_context(nc.sbuf_tensor(f"coupled_{n}", shape, dt))
        sem = lambda n: ctx.enter_context(nc.semaphore(f"coupled_{n}"))
        ring = lambda n, shape, dt=F32: [sb(f"{n}{s}", shape, dt) for s in range(SLOTS)]
        idx, sh = ring("idx", [P, TILES], I32), ring("sh", [P, TILES, HARM])
        rows, onehot = ring("rows", [P, TILES, FEAT]), ring("onehot", [P, TILES, WINDOW])
        prod = ring("prod", [P, TILES, 2 * OCH])
        iota, base_f, base = sb("iota", [P, WINDOW]), sb("base_f", [1, BLOCKS + SLOTS]), sb("base", [1, BLOCKS + SLOTS], I32)
        win_ps = [ctx.enter_context(nc.psum_tensor(f"coupled_win{b}", [P, 512], F32)) for b in range(2)]
        loaded, gathered = [sem(f"loaded{s}") for s in range(SLOTS)], [sem(f"gathered{s}") for s in range(SLOTS)]
        msg_ready, spread, summed, stepped, ones = sem("msg_ready"), sem("spread"), sem("summed"), sem("stepped"), sem("ones")
        started, ended = sem("started"), sem("ended")

        with nc.Block() as block:
            @block.sync
            def _(sp):
                load_blocks(sp, k, [
                    ([x[:, :] for x in idx], lambda b: one(a["src_blocks"], b)),
                    ([x[:, :, :].rearrange("p t c -> p (t c)") for x in sh],
                     lambda b: one(a["sh9"], b, "b p t c -> p (b t c)")),
                ], msg_ready, loaded, ended)

            @block.gpsimd
            def _(pool):
                gather_rows(pool, k, table, idx, rows, loaded, 32, gathered, started)

            @block.tensor
            def _(pe):
                turns = Turns(pe, k)
                pe.wait_ge(ones, 2 * SLOTS)
                with turns.flat() as g:
                    for s in range(SLOTS):
                        n = g * SLOTS + s
                        if s == 0:
                            pe.wait_ge(summed, n)
                        else:
                            pe.wait_ge(summed, n - 1)
                        pe.wait_ge(msg_ready, n + 1)
                        for c in range(2):
                            for t in range(TILES):
                                mm = pe.matmul(win_ps[s % 2][0:OCH, c * WINDOW:(c + 1) * WINDOW],
                                               prod[s][:, t, c * OCH:(c + 1) * OCH], onehot[s][:, t, :],
                                               start=(t == 0), stop=(t == TILES - 1))
                        mm.then_inc(spread, 1)

            @block.vector
            def _(dve):
                for s in range(SLOTS):
                    dve.memset(prod[s][:, :, OUTER:OUTER + 1], 1.0).then_inc(ones, 1)
                    dve.memset(prod[s][:, :, OUTER + 1:], 0.0).then_inc(ones, 1)
                win = Windows(dve, k, iota, base_f, base, stepped, (P, 2))
                turns = Turns(dve, k)

                def add_window(n, s, at):
                    dve.wait_ge(summed, n)
                    dve.wait_ge(spread, n + 1)
                    dst = k["acc"][0:OCH, :, bass.ds(at, WINDOW)]
                    dve.tensor_tensor(dst, dst, win_ps[s % 2][0:OCH, 0:2 * WINDOW].rearrange("p (c w) -> p c w", c=2),
                                      ALU.add).then_inc(summed, 1)

                with dve.Fori(0, turns.passes, 1) as p:
                    with dve.Fori(0, TURNS, 1) as i:
                        g = p * TURNS + i
                        bases = win.bases(i * SLOTS)
                        for s in range(SLOTS):
                            n = g * SLOTS + s
                            x, h = rows[s], sh[s]
                            win.one_hot(onehot[s], i * SLOTS + s)
                            dve.wait_ge(gathered[s], g * (16 * TILES) + 16 * TILES)
                            dve.wait_ge(loaded[s], g * 32 + 32)
                            dve.tensor_tensor(
                                prod[s][:, :, 0:4 * FEAT].rearrange("p t (c f) -> p t c f", c=4),
                                h[:, :, 0:4][:, :, :, None].broadcast_to([P, TILES, 4, FEAT]),
                                x[:, :, None, :].broadcast_to([P, TILES, 4, FEAT]), ALU.mult)
                            dve.tensor_tensor(
                                prod[s][:, :, 4 * FEAT:OUTER].rearrange("p t (c f) -> p t c f", c=5),
                                h[:, :, 4:9][:, :, :, None].broadcast_to([P, TILES, 5, 3 * MUL]),
                                x[:, :, None, MUL:].broadcast_to([P, TILES, 5, 3 * MUL]), ALU.mult)\
                                .then_inc(msg_ready, 1)
                            if s > 0:
                                add_window(n - 1, s - 1, bases[s - 1])
                        add_window(g * SLOTS + (SLOTS - 1), SLOTS - 1, bases[SLOTS - 1])
                    win.next_window(p)


def conv_edges(nc, a, k, name, table):
    with ExitStack() as ctx:
        sb = lambda n, shape, dt=F32: ctx.enter_context(nc.sbuf_tensor(f"{name}_{n}", shape, dt))
        sem = lambda n: ctx.enter_context(nc.semaphore(f"{name}_{n}"))
        ring = lambda n, shape, dt=F32: [sb(f"{n}{s}", shape, dt) for s in range(SLOTS)]
        idx = ring("idx", [P, TILES], I32)
        rows, onehot = ring("rows", [P, TILES, FEAT]), ring("onehot", [P, TILES, WINDOW])
        iota, base_f, base = sb("iota", [P, WINDOW]), sb("base_f", [1, BLOCKS + SLOTS]), sb("base", [1, BLOCKS + SLOTS], I32)
        win_ps = [ctx.enter_context(nc.psum_tensor(f"{name}_win{b}", [P, 512], F32)) for b in range(2)]
        loaded, gathered = [sem(f"loaded{s}") for s in range(SLOTS)], [sem(f"gathered{s}") for s in range(SLOTS)]
        msg_ready, spread, summed, stepped = sem("msg_ready"), sem("spread"), sem("summed"), sem("stepped")
        started, ended = sem("started"), sem("ended")

        with nc.Block() as block:
            @block.sync
            def _(sp):
                load_blocks(sp, k, [([x[:, :] for x in idx], lambda b: one(a["src_blocks"], b))],
                            spread, loaded, ended)

            @block.gpsimd
            def _(pool):
                gather_rows(pool, k, table, idx, rows, loaded, 16, gathered, started)

            @block.tensor
            def _(pe):
                turns = Turns(pe, k)
                with turns.flat() as g:
                    for s in range(SLOTS):
                        n = g * SLOTS + s
                        if s == 0:
                            pe.wait_ge(summed, n)
                        else:
                            pe.wait_ge(summed, n - 1)
                        pe.wait_ge(msg_ready, n + 1)
                        pe.wait_ge(gathered[s], g * (16 * TILES) + 16 * TILES)
                        for t in range(TILES):
                            mm = pe.matmul(win_ps[s % 2][0:FEAT, 0:WINDOW], rows[s][:, t, :], onehot[s][:, t, :],
                                           start=(t == 0), stop=(t == TILES - 1))
                        mm.then_inc(spread, 1)

            @block.vector
            def _(dve):
                win = Windows(dve, k, iota, base_f, base, stepped, (FEAT, 1))
                turns = Turns(dve, k)

                def add_window(n, s, at):
                    dve.wait_ge(summed, n)
                    dve.wait_ge(spread, n + 1)
                    dst = k["acc"][0:FEAT, 0, bass.ds(at, WINDOW)]
                    dve.tensor_tensor(dst, dst, win_ps[s % 2][0:FEAT, 0:WINDOW], ALU.add).then_inc(summed, 1)

                with dve.Fori(0, turns.passes, 1) as p:
                    with dve.Fori(0, TURNS, 1) as i:
                        g = p * TURNS + i
                        bases = win.bases(i * SLOTS)
                        for s in range(SLOTS):
                            n = g * SLOTS + s
                            win.one_hot(onehot[s], i * SLOTS + s).then_inc(msg_ready, 1)
                            if s > 0:
                                add_window(n - 1, s - 1, bases[s - 1])
                        add_window(g * SLOTS + (SLOTS - 1), SLOTS - 1, bases[SLOTS - 1])
                    win.next_window(p)


def node_rows(t, g):
    return t.rearrange("(g q p) f -> g p q f", q=GROUP, p=NT)[bass.ds(g, 1)].rearrange("g p q f -> p (g q) f")


class Steps:

    def __init__(self, dve, done, per_group, g, before=0):
        self.dve, self.done, self.base, self.n = dve, done, g * per_group + before, 0

    def __call__(self, instruction):
        instruction.then_inc(self.done, 1)
        self.n += 1
        return self.n

    def wait(self, n):
        self.dve.wait_ge(self.done, self.base + n)


NORM_DVE = 9


def normalise(nc, step, dve, b, root_ready, g):
    wide = [NT, GROUP, FEAT]
    over = lambda t: t[:, :, None].broadcast_to(wide)
    step.wait(step(dve.tensor_reduce(b["mean"][:, :], b["y"][:, :, :], AX, ALU.add)))
    step.wait(step(dve.tensor_scalar(b["mean"][:, :], b["mean"][:, :], 1.0 / FEAT, None, ALU.mult)))
    step.wait(step(dve.tensor_tensor(b["y"][:, :, :], b["y"][:, :, :], over(b["mean"]), ALU.subtract)))
    step.wait(step(dve.tensor_tensor(b["sq"][:, :, :], b["y"][:, :, :], b["y"][:, :, :], ALU.mult)))
    n = step(dve.tensor_reduce(b["var"][:, :], b["sq"][:, :, :], AX, ALU.add))
    dve.wait_ge(root_ready, g + 1)
    step.wait(step(dve.reciprocal(b["rstd"][:, :], b["root"][:, :])))
    step(dve.tensor_tensor(b["xn"][:, :, :], b["y"][:, :, :], over(b["rstd"]), ALU.mult))
    return n


def norm_buffers(sb):
    b = {n: sb(n, [NT, GROUP, FEAT]) for n in ("y", "sq", "xn")}
    return b | {n: sb(n, [NT, GROUP]) for n in ("mean", "var", "root", "rstd")}


def node_phase(nc, name):
    ctx = ExitStack()
    sb = lambda n, shape, dt=F32: ctx.enter_context(nc.sbuf_tensor(f"{name}_{n}", shape, dt))
    sem = lambda n: ctx.enter_context(nc.semaphore(f"{name}_{n}"))
    psum = lambda n, shape: ctx.enter_context(nc.psum_tensor(f"{name}_{n}_ps", shape, F32))
    return ctx, sb, sem, psum


def weighted_nodes(nc, a, k, name, x_in, x_out, self_w, agg_scale, self_scale):
    ctx, sb, sem, psum = node_phase(nc, f"{name}_nodes")
    with ctx:
        x, xt = sb("x", [NT, GROUP, FEAT]), sb("xt", [FEAT, GN])
        sums, ends = sb("sums", [WCH, 2, GN]), sb("ends", [WCH, 2, FEAT])
        own = sb("own", [FEAT, FEAT])
        b = norm_buffers(sb)
        xt_ps, y_ps = psum("xt", [FEAT, 512]), psum("y", [NT, 512])
        own_loaded, x_loaded, xt_ready, mixed, own_ready = (sem(n) for n in ("own_loaded", "x_loaded", "xt_ready", "mixed", "own_ready"))
        copied, done, root_ready, stored = sem("copied"), sem("done"), sem("root_ready"), sem("stored")
        STEPS = 8
        with nc.Block() as block:
            @block.sync
            def _(sp):
                sp.dma_start(own[:, :], a[self_w]).then_inc(own_loaded, 16)
                sp.dma_start(ends[:, :, :], a["sum_columns"].rearrange("c p f -> p c f")).then_inc(own_loaded, 16)
                sp.dma_start(x[:, :, :], node_rows(x_in, 0)).then_inc(x_loaded, 16)
                with sp.Fori(0, GROUPS, 1) as g:
                    sp.wait_ge(done, g * STEPS + STEPS)
                    sp.dma_start(node_rows(x_out, g), b["xn"][:, :, :]).then_inc(stored, 16)
                    sp.wait_ge(stored, g * 16 + 16)
                    sp.dma_start(x[:, :, :], node_rows(x_in, next_group(g))).then_inc(x_loaded, 16)
                sp.wait_ge(x_loaded, 16 * (GROUPS + 1))
                sp.wait_ge(stored, 16 * GROUPS)

            @block.tensor
            def _(pe):
                with pe.Fori(0, GROUPS, 1) as g:
                    pe.wait_ge(x_loaded, g * 16 + 16)
                    pe.wait_ge(copied, g * 3)
                    for q in range(GROUP):
                        mm = pe.transpose(xt_ps[:, q * NT:(q + 1) * NT], x[:, q, :], k["ident"][0:NT, 0:NT])
                    mm.then_inc(xt_ready, 1)
                    pe.wait_ge(copied, g * 3 + 3)
                    pe.wait_ge(done, g * STEPS)
                    pe.wait_ge(own_ready, 1)
                    for q in range(GROUP):
                        cols = slice(q * NT, (q + 1) * NT)
                        for c in range(2):
                            pe.matmul(y_ps[:, q * FEAT:(q + 1) * FEAT], sums[:, c, cols], ends[:, c, :],
                                      start=(c == 0), stop=False)
                        mm = pe.matmul(y_ps[:, q * FEAT:(q + 1) * FEAT], xt[:, cols], own[:, :], start=False, stop=True)
                    mm.then_inc(mixed, 1)

            @block.scalar
            def _(act):
                with act.Fori(0, GROUPS, 1) as g:
                    act.wait_ge(mixed, g)
                    for c in range(2):
                        nc.scalar.activation(sums[:, c, :], k["acc"][0:WCH, c, bass.ds(g * GN, GN)], ACT.Copy,
                                             scale=float(agg_scale)).then_inc(copied, 1)
                    act.wait_ge(xt_ready, g + 1)
                    nc.scalar.activation(xt[:, :], xt_ps[:, 0:GN], ACT.Copy).then_inc(copied, 1)
                    act.wait_ge(done, g * STEPS + 6)
                    nc.scalar.activation(b["root"][:, :], b["var"][:, :], ACT.Sqrt, scale=1.0 / FEAT,
                                         bias=k["eps"][0:NT, 0:1]).then_inc(root_ready, 1)

            @block.vector
            def _(dve):
                dve.wait_ge(own_loaded, 32)
                dve.tensor_scalar(own[:, :], own[:, :], float(self_scale), None, ALU.mult).then_inc(own_ready, 1)
                with dve.Fori(0, GROUPS, 1) as g:
                    step = Steps(dve, done, STEPS, g)
                    dve.wait_ge(mixed, g + 1)
                    dve.wait_ge(stored, g * 16)
                    step.wait(step(dve.tensor_tensor(
                        b["y"][:, :, :], y_ps[:, 0:GROUP * FEAT].rearrange("p (q f) -> p q f", q=GROUP),
                        x[:, :, :], ALU.add)))
                    normalise(nc, step, dve, b, root_ready, g)


def next_group(g):
    return (g + 1) % GROUPS


def coupled_nodes(nc, a, k, x_in, x_out, u_out):
    ctx, sb, sem, psum = node_phase(nc, "coupled_nodes")
    with ctx:
        x, sums = sb("x", [NT, GROUP, FEAT]), sb("sums", [OCH, 2, GN])
        mix, coef = sb("mix", [OCH, 2, FEAT + 1]), sb("coef", [OCH, 2, FEAT + 1])
        deg, root_d, u = sb("deg", [NT, GROUP]), sb("root_d", [NT, GROUP]), sb("u", [NT, GROUP, FEAT])
        b = norm_buffers(sb)
        y_ps = psum("y", [NT, 512])
        mix_loaded, mix_ready, x_loaded, mixed = sem("mix_loaded"), sem("mix_ready"), sem("x_loaded"), sem("mixed")
        copied, done, root_ready, stored, rootd_ready = sem("copied"), sem("done"), sem("root_ready"), sem("stored"), sem("rootd_ready")
        STEPS = 11
        with nc.Block() as block:
            @block.sync
            def _(sp):
                sp.dma_start(mix[:, :, :], a["L1_mix"].rearrange("c p f -> p c f")).then_inc(mix_loaded, 16)
                sp.dma_start(coef[:, :, :], a["L1_coef"].rearrange("c p f -> p c f")).then_inc(mix_loaded, 16)
                sp.dma_start(x[:, :, :], node_rows(x_in, 0)).then_inc(x_loaded, 16)
                with sp.Fori(0, GROUPS, 1) as g:
                    sp.wait_ge(done, g * STEPS + STEPS)
                    sp.dma_start(node_rows(x_out, g), b["xn"][:, :, :]).then_inc(stored, 16)
                    sp.dma_start(node_rows(u_out, g), u[:, :, :]).then_inc(stored, 16)
                    sp.wait_ge(stored, g * 32 + 32)
                    sp.dma_start(x[:, :, :], node_rows(x_in, next_group(g))).then_inc(x_loaded, 16)
                sp.wait_ge(x_loaded, 16 * (GROUPS + 1))
                sp.wait_ge(stored, 32 * GROUPS)

            @block.tensor
            def _(pe):
                pe.wait_ge(mix_ready, 1)
                with pe.Fori(0, GROUPS, 1) as g:
                    pe.wait_ge(copied, g * 2 + 2)
                    pe.wait_ge(done, g * STEPS)
                    for q in range(GROUP):
                        for c in range(2):
                            mm = pe.matmul(y_ps[:, q * (FEAT + 1):(q + 1) * (FEAT + 1)], sums[:, c, q * NT:(q + 1) * NT],
                                           mix[:, c, :], start=(c == 0), stop=(c == 1))
                    mm.then_inc(mixed, 1)

            @block.scalar
            def _(act):
                with act.Fori(0, GROUPS, 1) as g:
                    act.wait_ge(mixed, g)
                    for c in range(2):
                        nc.scalar.activation(sums[:, c, :], k["acc"][0:OCH, c, bass.ds(g * GN, GN)], ACT.Copy)\
                          .then_inc(copied, 1)
                    act.wait_ge(done, g * STEPS + 2)
                    nc.scalar.activation(root_d[:, :], deg[:, :], ACT.Sqrt).then_inc(rootd_ready, 1)
                    act.wait_ge(done, g * STEPS + 7)
                    nc.scalar.activation(b["root"][:, :], b["var"][:, :], ACT.Sqrt, scale=1.0 / FEAT,
                                         bias=k["eps"][0:NT, 0:1]).then_inc(root_ready, 1)

            @block.vector
            def _(dve):
                dve.wait_ge(mix_loaded, 32)
                dve.tensor_tensor(mix[:, :, :], mix[:, :, :], coef[:, :, :], ALU.mult).then_inc(mix_ready, 1)
                with dve.Fori(0, GROUPS, 1) as g:
                    step = Steps(dve, done, STEPS, g)
                    dve.wait_ge(mixed, g + 1)
                    dve.wait_ge(x_loaded, g * 16 + 16)
                    dve.wait_ge(stored, g * 32)
                    y = y_ps[:, 0:GROUP * (FEAT + 1)].rearrange("p (q f) -> p q f", q=GROUP)
                    step(dve.tensor_tensor(b["y"][:, :, :], y[:, :, 0:FEAT], x[:, :, :], ALU.add))
                    step.wait(step(dve.tensor_scalar(deg[:, :], y[:, :, FEAT], 1.0, None, ALU.add)))
                    normalise(nc, step, dve, b, root_ready, g)
                    dve.wait_ge(rootd_ready, g + 1)
                    dinv = k["dinv"][:, bass.ds(g, 1), :].rearrange("p g q -> p (g q)")
                    step.wait(step(dve.reciprocal(dinv, root_d[:, :])))
                    step(dve.tensor_tensor(u[:, :, :], b["xn"][:, :, :],
                                           dinv[:, :, None].broadcast_to([NT, GROUP, FEAT]), ALU.mult))


def conv1_nodes(nc, a, k, u_in, u_out):
    ctx, sb, sem, psum = node_phase(nc, "conv1_nodes")
    with ctx:
        u, sums = sb("u", [NT, GROUP, FEAT]), sb("sums", [FEAT, GN])
        z, zt, h, o = sb("z", [NT, GROUP, FEAT]), sb("zt", [FEAT, GN]), sb("h", [HID, GN]), sb("o", [NT, GROUP, FEAT])
        w1, b1, w2 = sb("w1", [FEAT, HID]), sb("b1", [HID, 1]), sb("w2", [HID, FEAT])
        agg_ps, zt_ps, h_ps, o_ps = psum("agg", [NT, 512]), psum("zt", [FEAT, 512]), psum("h", [HID, 512]), psum("o", [NT, 512])
        params, u_loaded, copied, turned, done, stored = (sem(n) for n in ("params", "u_loaded", "copied", "turned", "done", "stored"))
        STEPS, TURNED, COPIED = 3, 4, 3
        with nc.Block() as block:
            @block.sync
            def _(sp):
                sp.dma_start(w1[:, :], a["L2_gnn_W1"]).then_inc(params, 16)
                sp.dma_start(b1[:, :], a["L2_gnn_b1"].rearrange("(h o) -> h o", o=1)).then_inc(params, 16)
                sp.dma_start(w2[:, :], a["L2_gnn_W2"]).then_inc(params, 16)
                sp.dma_start(u[:, :, :], node_rows(u_in, 0)).then_inc(u_loaded, 16)
                with sp.Fori(0, GROUPS, 1) as g:
                    sp.wait_ge(done, g * STEPS + STEPS)
                    sp.dma_start(node_rows(u_out, g), o[:, :, :]).then_inc(stored, 16)
                    sp.wait_ge(stored, g * 16 + 16)
                    sp.dma_start(u[:, :, :], node_rows(u_in, next_group(g))).then_inc(u_loaded, 16)
                sp.wait_ge(u_loaded, 16 * (GROUPS + 1))
                sp.wait_ge(stored, 16 * GROUPS)

            @block.tensor
            def _(pe):
                pe.wait_ge(params, 48)
                with pe.Fori(0, GROUPS, 1) as g:
                    pe.wait_ge(copied, g * COPIED + 1)
                    for q in range(GROUP):
                        mm = pe.matmul(agg_ps[:, q * FEAT:(q + 1) * FEAT], sums[:, q * NT:(q + 1) * NT],
                                       k["ident"][0:FEAT, 0:FEAT], start=True, stop=True)
                    mm.then_inc(turned, 1)
                    pe.wait_ge(done, g * STEPS + 2)
                    for q in range(GROUP):
                        mm = pe.transpose(zt_ps[:, q * NT:(q + 1) * NT], z[:, q, :], k["ident"][0:NT, 0:NT])
                    mm.then_inc(turned, 1)
                    pe.wait_ge(copied, g * COPIED + 2)
                    pe.matmul(h_ps[:, 0:GN], w1[:, :], zt[:, :], start=True, stop=True).then_inc(turned, 1)
                    pe.wait_ge(copied, g * COPIED + 3)
                    for q in range(GROUP):
                        mm = pe.matmul(o_ps[:, q * FEAT:(q + 1) * FEAT], h[:, q * NT:(q + 1) * NT], w2[:, :],
                                       start=True, stop=True)
                    mm.then_inc(turned, 1)

            @block.scalar
            def _(act):
                act.wait_ge(params, 48)
                with act.Fori(0, GROUPS, 1) as g:
                    act.wait_ge(turned, g * TURNED)
                    nc.scalar.activation(sums[:, :], k["acc"][0:FEAT, 0, bass.ds(g * GN, GN)], ACT.Copy).then_inc(copied, 1)
                    act.wait_ge(turned, g * TURNED + 2)
                    nc.scalar.activation(zt[:, :], zt_ps[:, 0:GN], ACT.Copy).then_inc(copied, 1)
                    act.wait_ge(turned, g * TURNED + 3)
                    nc.scalar.activation(h[:, :], h_ps[:, 0:GN], ACT.Relu, bias=b1[:, 0:1]).then_inc(copied, 1)

            @block.vector
            def _(dve):
                with dve.Fori(0, GROUPS, 1) as g:
                    step = Steps(dve, done, STEPS, g)
                    dinv = k["dinv"][:, bass.ds(g, 1), :].rearrange("p g q -> p (g q)")[:, :, None]\
                        .broadcast_to([NT, GROUP, FEAT])
                    as_rows = lambda ps: ps[:, 0:GROUP * FEAT].rearrange("p (q f) -> p q f", q=GROUP)
                    dve.wait_ge(turned, g * TURNED + 1)
                    dve.wait_ge(u_loaded, g * 16 + 16)
                    step.wait(step(dve.tensor_tensor(z[:, :, :], as_rows(agg_ps), u[:, :, :], ALU.add)))
                    step(dve.tensor_tensor(z[:, :, :], z[:, :, :], dinv, ALU.mult))
                    dve.wait_ge(stored, g * 16)
                    dve.wait_ge(turned, g * TURNED + 4)
                    step(dve.tensor_tensor(o[:, :, :], as_rows(o_ps), dinv, ALU.mult))


def conv2_nodes(nc, a, k, u_in, x_in, x_out):
    ctx, sb, sem, psum = node_phase(nc, "conv2_nodes")
    with ctx:
        u, x, sums = sb("u", [NT, GROUP, FEAT]), sb("x", [NT, GROUP, FEAT]), sb("sums", [FEAT, GN])
        z, bias = sb("z", [NT, GROUP, FEAT]), sb("bias", [NT, FEAT])
        b = norm_buffers(sb)
        agg_ps = psum("agg", [NT, 512])
        params, loaded, copied, turned, done, root_ready, stored = (
            sem(n) for n in ("params", "loaded", "copied", "turned", "done", "root_ready", "stored"))
        STEPS = 12
        with nc.Block() as block:
            @block.sync
            def _(sp):
                sp.dma_start(bias[:, :], a["L2_gnn_b2"].rearrange("(o n) -> o n", o=1).broadcast_to([NT, FEAT]))\
                  .then_inc(params, 16)
                sp.dma_start(u[:, :, :], node_rows(u_in, 0)).then_inc(loaded, 16)
                sp.dma_start(x[:, :, :], node_rows(x_in, 0)).then_inc(loaded, 16)
                with sp.Fori(0, GROUPS, 1) as g:
                    sp.wait_ge(done, g * STEPS + STEPS)
                    sp.dma_start(node_rows(x_out, g), b["xn"][:, :, :]).then_inc(stored, 16)
                    sp.wait_ge(stored, g * 16 + 16)
                    sp.dma_start(u[:, :, :], node_rows(u_in, next_group(g))).then_inc(loaded, 16)
                    sp.dma_start(x[:, :, :], node_rows(x_in, next_group(g))).then_inc(loaded, 16)
                sp.wait_ge(loaded, 32 * (GROUPS + 1))
                sp.wait_ge(stored, 16 * GROUPS)

            @block.tensor
            def _(pe):
                pe.wait_ge(params, 16)
                with pe.Fori(0, GROUPS, 1) as g:
                    pe.wait_ge(done, g * STEPS)
                    pe.wait_ge(copied, g + 1)
                    for q in range(GROUP):
                        mm = pe.matmul(agg_ps[:, q * FEAT:(q + 1) * FEAT], sums[:, q * NT:(q + 1) * NT],
                                       k["ident"][0:FEAT, 0:FEAT], start=True, stop=True)
                    mm.then_inc(turned, 1)

            @block.scalar
            def _(act):
                with act.Fori(0, GROUPS, 1) as g:
                    act.wait_ge(turned, g)
                    nc.scalar.activation(sums[:, :], k["acc"][0:FEAT, 0, bass.ds(g * GN, GN)], ACT.Copy).then_inc(copied, 1)
                    act.wait_ge(done, g * STEPS + 10)
                    nc.scalar.activation(b["root"][:, :], b["var"][:, :], ACT.Sqrt, scale=1.0 / FEAT,
                                         bias=k["eps"][0:NT, 0:1]).then_inc(root_ready, 1)

            @block.vector
            def _(dve):
                dve.wait_ge(params, 16)
                with dve.Fori(0, GROUPS, 1) as g:
                    step = Steps(dve, done, STEPS, g)
                    wide = [NT, GROUP, FEAT]
                    dinv = k["dinv"][:, bass.ds(g, 1), :].rearrange("p g q -> p (g q)")[:, :, None].broadcast_to(wide)
                    dve.wait_ge(turned, g + 1)
                    dve.wait_ge(loaded, g * 32 + 32)
                    dve.wait_ge(stored, g * 16)
                    step.wait(step(dve.tensor_tensor(
                        z[:, :, :], agg_ps[:, 0:GROUP * FEAT].rearrange("p (q f) -> p q f", q=GROUP), u[:, :, :], ALU.add)))
                    step.wait(step(dve.tensor_tensor(z[:, :, :], z[:, :, :], dinv, ALU.mult)))
                    step.wait(step(dve.tensor_tensor(z[:, :, :], z[:, :, :], bias[:, None, :].broadcast_to(wide), ALU.add)))
                    step.wait(step(dve.tensor_scalar(z[:, :, :], z[:, :, :], 0.0, None, ALU.max)))
                    step.wait(step(dve.tensor_tensor(b["y"][:, :, :], z[:, :, :], x[:, :, :], ALU.add)))
                    normalise(nc, step, dve, b, root_ready, g)


def kernel(**inputs):
    import concourse.bacc as bacc
    from concourse.bass_utils import run_bass_kernel_spmd

    v = {n: np.asarray(x) for n, x in inputs.items()}
    coef, mix = coupling_layout(v["L1_gnn_W"])
    dst = np.concatenate([v["dst"], np.full(BLOCKS * BLOCK - EDGES, -1, v["dst"].dtype)])
    arrays = {
        "x": v["x"], "dst": v["dst"],
        "dst_lanes": np.ascontiguousarray(dst.reshape(BLOCKS * TILES, P).T),
        "src_blocks": edge_order(v["src"]),
        "sh4": edge_order(v["edge_attr_4"]),
        "sh9": edge_order(np.concatenate([v["edge_weight1"], v["edge_attr_3"], v["edge_attr_5"]], 1)),
        "ef32": edge_major(v["edge_attr_32"]), "ef8": half_rows(edge_major(v["edge_attr_8"])),
        "L0_self": irrep_blocks(v["L0_gnn_si_w0"], v["L0_gnn_si_w1"]),
        "L3_self": irrep_blocks(v["L3_gnn_Ws"], v["L3_gnn_Wv"]),
        "sum_columns": message_sums(),
        "L1_mix": mix, "L1_coef": coef,
        "L0_gnn_W2": path_columns(v["L0_gnn_W2"], (3, 0, 1, 2)),
        "L0_gnn_b2": path_columns(v["L0_gnn_b2"][None], (3, 0, 1, 2))[0],
        "L3_gnn_W3": path_columns(v["L3_gnn_W3"], (1, 0, 2, 3)),
        "L3_gnn_b3": path_columns(v["L3_gnn_b3"][None], (1, 0, 2, 3))[0],
    }
    for n in ("L0_gnn_W1", "L0_gnn_b1", "L2_gnn_W1", "L2_gnn_b1", "L2_gnn_W2", "L2_gnn_b2",
              "L3_gnn_W1", "L3_gnn_b1", "L3_gnn_W2", "L3_gnn_b2"):
        arrays[n] = v[n]
    nc = bacc.Bacc("TRN2", target_bir_lowering=False, num_devices=1)
    aps = {n: nc.dram_tensor(f"in_{n}", x.shape, mybir.dt.from_np(x.dtype), kind="ExternalInput").ap()
           for n, x in arrays.items()}
    out = nc.dram_tensor("out", [NODES, FEAT], F32, kind="ExternalOutput").ap()
    build(nc, aps, out)
    r = run_bass_kernel_spmd(nc, [{f"in_{n}": x for n, x in arrays.items()}], core_ids=[0])
    return r.results[0]["out"]
```

```python
from contextlib import ExitStack

import concourse.bass as bass
import numpy as np
from concourse import mybir

F32 = mybir.dt.float32
I32 = mybir.dt.int32
U32 = mybir.dt.uint32
ALU = mybir.AluOpType
ACT = mybir.ActivationFunctionType
AX = mybir.AxisListType.X
DVE_ONLY = [mybir.EngineType.DVE]

NODES, EDGES, FEAT, MUL = 12500, 400000, 32, 8
P = 128
TILES = 5
BLOCK = TILES * P
SLOTS = 4
REAL_BLOCKS = EDGES // BLOCK
TURNS = -(-REAL_BLOCKS // SLOTS)
BLOCKS = TURNS * SLOTS
WINDOW = 64
ACC = NODES + WINDOW
HID = 64
WPATHS = 4 * MUL * MUL
HARM = 9
OUTER = 4 * FEAT + 5 * 3 * MUL
OCH = 125
NT = 125
NODE_TILES = NODES // NT
GROUP = 10
GROUPS = NODE_TILES // GROUP
EPS = 1e-5
HALF = BLOCK // 2
TO_S, V_V = MUL * MUL, 3 * MUL * MUL // 2
MSG = TO_S + V_V + 3 * MUL
LO_SPLIT = REAL_BLOCKS // 125


def edge_order(a, fill=0):
    a = np.concatenate([a, np.full((BLOCKS * BLOCK - EDGES,) + a.shape[1:], fill, a.dtype)])
    a = a.reshape((BLOCKS, TILES, P) + a.shape[1:])
    a = np.moveaxis(a, 1, 2)
    return np.ascontiguousarray(np.concatenate([a, a[:SLOTS]]))


def edge_major(a):
    a = np.concatenate([a, np.zeros((BLOCKS * BLOCK - EDGES, a.shape[1]), a.dtype)])
    a = np.moveaxis(a.reshape(BLOCKS, BLOCK, -1), 1, 2)
    return np.ascontiguousarray(np.concatenate([a, a[:SLOTS]]))


def path_columns(w, order):
    w = w.reshape(-1, 4, MUL, MUL)
    vv_s, ss_s, s_v, v_v = (w[:, p] for p in order)
    scalars = np.stack([vv_s, ss_s], 1)
    return np.ascontiguousarray(np.concatenate([
        scalars.transpose(0, 3, 1, 2).reshape(len(w), 2 * MUL * MUL),
        s_v.transpose(0, 2, 1).reshape(len(w), MUL * MUL),
        v_v.transpose(0, 2, 1).reshape(len(w), MUL * MUL)], 1))


def half_rows(blocks):
    b, n, _ = blocks.shape
    return np.ascontiguousarray(blocks.reshape(b, n, 2, HALF).transpose(0, 2, 1, 3)).reshape(b, 2 * n, HALF)


def message_sums():
    m = np.zeros((2 * P, FEAT), np.float32)
    vector = np.arange(3 * MUL).reshape(MUL, 3) + MUL
    m[np.arange(TO_S), np.repeat(np.arange(MUL), MUL)] = 1
    m[TO_S + np.arange(V_V), np.repeat(vector.T.reshape(-1), MUL // 2)] = 1
    m[TO_S + V_V + np.arange(3 * MUL), vector.reshape(-1)] = 1
    return m.reshape(2, P, FEAT)


def irrep_blocks(w0, w1):
    m = np.zeros((FEAT, FEAT), w0.dtype)
    m[:MUL, :MUL] = w0
    for c in range(3):
        m[MUL + c::3, MUL + c::3] = w1
    return m


def coupling(l1, l2, l3):
    from math import factorial as f, sqrt

    def su2(j1, m1, j2, m2, j3, m3):
        if m3 != m1 + m2:
            return 0.0
        vmin = max(0, j2 - j3 - m1, j1 + m2 - j3)
        vmax = min(j1 + j2 - j3, j1 - m1, j2 + m2)
        pref = (2 * j3 + 1) * f(j3 + j1 - j2) * f(j3 - j1 + j2) * f(j1 + j2 - j3) / f(j1 + j2 + j3 + 1)
        pref *= f(j3 + m3) * f(j3 - m3) * f(j1 - m1) * f(j1 + m1) * f(j2 - m2) * f(j2 + m2)
        s = 0.0
        for v in range(vmin, vmax + 1):
            s += (-1) ** v / (f(v) * f(j1 + j2 - j3 - v) * f(j1 - m1 - v) * f(j2 + m2 - v)
                              * f(j3 - j2 + m1 + v) * f(j3 - j1 - m2 + v))
        return sqrt(pref) * s

    def q(l):
        m = np.zeros((2 * l + 1, 2 * l + 1), np.complex128)
        for k in range(-l, 0):
            m[l + k, l - k] = 1 / sqrt(2)
            m[l + k, l + k] = -1j / sqrt(2)
        m[l, l] = 1
        for k in range(1, l + 1):
            m[l + k, l + k] = (-1) ** k / sqrt(2)
            m[l + k, l - k] = 1j * (-1) ** k / sqrt(2)
        return (-1j) ** l * m

    c = np.zeros((2 * l1 + 1, 2 * l2 + 1, 2 * l3 + 1), np.complex128)
    for a in range(-l1, l1 + 1):
        for b in range(-l2, l2 + 1):
            if -l3 <= a + b <= l3:
                c[a + l1, b + l2, a + b + l3] = su2(l1, a, l2, b, l3, a + b)
    c = np.einsum("ij,kl,mn,ikn->jlm", q(l1), q(l2), np.conj(q(l3)).T, c).real
    return (c / np.linalg.norm(c)).astype(np.float32)


def coupling_layout(w):
    cg = {c: coupling(*c) for c in [(0, 0, 0), (0, 1, 1), (1, 0, 1), (1, 1, 0), (1, 1, 1), (2, 1, 1)]}
    coef = np.zeros((2 * OCH, FEAT + 1), np.float32)
    weight = np.zeros((2 * OCH, FEAT + 1), w.dtype)
    for path, (le, ln, lo) in enumerate(cg):
        c = cg[le, ln, lo]
        for a in range(2 * le + 1):
            for m in range(2 * ln + 1):
                for k in range(2 * lo + 1):
                    for i in range(MUL):
                        feat = i if ln == 0 else MUL + 3 * i + m
                        row = {0: 0, 1: FEAT * (1 + a)}[le] + feat if le < 2 else \
                            4 * FEAT + 3 * MUL * a + feat - MUL
                        for o in range(MUL):
                            col = o if lo == 0 else MUL + 3 * o + k
                            coef[row, col] = c[a, m, k]
                            weight[row, col] = w[path, i, o]
    coef[OUTER, FEAT] = 1
    weight[OUTER, FEAT] = 1
    return coef.reshape(2, OCH, FEAT + 1), weight.reshape(2, OCH, FEAT + 1)


def build(nc, a, out):
    with ExitStack() as ctx:
        dram = lambda name, shape, dt: nc.dram_tensor(name, shape, dt, kind="Internal").ap()
        sb = lambda name, shape, dt=F32: ctx.enter_context(nc.sbuf_tensor(name, shape, dt))
        x1, x3 = (dram(f"x_after_{n}", [NODES, FEAT], F32) for n in ("weighted0", "convolved"))
        u1, u2 = (dram(f"conv_rows_{n}", [NODES, FEAT], F32) for n in (1, 2))
        lo_row = dram("lowest_target", [1, BLOCKS], F32)
        span_row = dram("target_span", [1, 125], F32)
        k = {
            "nc": nc,
            "acc": sb("acc", [P, 2, ACC]),
            "local": sb("local", [P, BLOCKS, TILES]),
            "iota0": sb("iota0", [P, WINDOW]),
            "lo": sb("lo", [1, BLOCKS]),
            "passes": sb("passes", [1, 1], I32),
            "ident": sb("ident", [P, P]),
            "x": sb("x", [NT, NODE_TILES, FEAT]),
            "dinv": sb("dinv", [NT, NODE_TILES]),
            "eps": sb("eps", [P, 1]),
        }
        setup(nc, a, k, lo_row, span_row)
        weighted_edges(nc, a, k, "weighted0", a["x"], "ef32", FEAT, ["L0_gnn_W1", "L0_gnn_W2"],
                       ["L0_gnn_b1", "L0_gnn_b2"], ACT.Relu)
        weighted_nodes(nc, a, k, "weighted0", x1, "L0_self", 0.25, 1 / np.sqrt(MUL))
        coupled_edges(nc, a, k, x1)
        with nc.sbuf_tensor("u", [NT, NODE_TILES, FEAT], F32) as k["u"]:
            coupled_nodes(nc, a, k, u1)
            conv_edges(nc, a, k, "conv1", u1)
            conv1_nodes(nc, a, k, u2)
            conv_edges(nc, a, k, "conv2", u2)
            conv2_nodes(nc, a, k, x3)
        weighted_edges(nc, a, k, "weighted3", x3, "ef8", MUL, ["L3_gnn_W1", "L3_gnn_W2", "L3_gnn_W3"],
                       ["L3_gnn_b1", "L3_gnn_b2", "L3_gnn_b3"], ACT.Silu)
        weighted_nodes(nc, a, k, "weighted3", out, "L3_self", 0.25 / 4, 1 / np.sqrt(MUL))


def setup(nc, a, k, lo_row, span_row):
    with ExitStack() as ctx:
        sb = lambda name, shape, dt=F32: ctx.enter_context(nc.sbuf_tensor(name, shape, dt))
        sem = lambda name: ctx.enter_context(nc.semaphore(name))
        by_block = sb("by_block", [125, LO_SPLIT, BLOCK], I32)
        by_block_f = sb("by_block_f", [125, LO_SPLIT, BLOCK])
        by_lane = sb("by_lane", [P, BLOCKS * TILES], I32)
        lowest = sb("lowest", [125, LO_SPLIT])
        highest = sb("highest", [125, LO_SPLIT])
        span = sb("span", [125, LO_SPLIT])
        span_max = sb("span_max", [125, 1])
        none = sb("none", [1, BLOCKS - REAL_BLOCKS])
        lo_all = sb("lo_all", [P, BLOCKS])
        spans = sb("spans", [1, 125])
        widest = sb("widest", [1, 1])
        blocks_loaded, lanes_loaded = sem("blocks_loaded"), sem("lanes_loaded")
        found, lo_stored, lo_loaded, made = sem("found"), sem("lo_stored"), sem("lo_loaded"), sem("made")
        spans_loaded, x_loaded = sem("spans_loaded"), sem("x_loaded")
        with nc.Block() as block:
            @block.sync
            def _(sp):
                sp.dma_start(by_block[:, :, :], a["dst"].rearrange("(p b e) -> p b e", b=LO_SPLIT, e=BLOCK))\
                  .then_inc(blocks_loaded, 16)
                sp.dma_start(by_lane[:, :], a["dst_lanes"]).then_inc(lanes_loaded, 16)
                sp.dma_start(k["x"][:, :, :], a["x"].rearrange("(p j) f -> p j f", j=NODE_TILES)).then_inc(x_loaded, 16)
                sp.wait_ge(found, 7)
                sp.dma_start(lo_row[0:1, 0:REAL_BLOCKS].rearrange("o (p b) -> (o p) b", b=LO_SPLIT), lowest[:, :])\
                  .then_inc(lo_stored, 16)
                sp.dma_start(lo_row[0:1, REAL_BLOCKS:BLOCKS], none[:, :]).then_inc(lo_stored, 16)
                sp.dma_start(span_row.rearrange("o p -> p o"), span_max[:, :]).then_inc(lo_stored, 16)
                sp.wait_ge(lo_stored, 48)
                sp.dma_start(k["lo"][:, :], lo_row).then_inc(lo_loaded, 16)
                sp.dma_start(lo_all[:, :], lo_row.broadcast_to([P, BLOCKS])).then_inc(lo_loaded, 16)
                sp.dma_start(spans[:, :], span_row).then_inc(spans_loaded, 16)
                sp.wait_ge(x_loaded, 16)

            @block.gpsimd
            def _(pool):
                pool.memset(k["ident"][:, :], 0.0).then_inc(made, 1)
                pool.wait_ge(made, 1)
                pool.affine_select(out=k["ident"][:, :], in_=k["ident"][:, :], compare_op=ALU.not_equal, fill=1.0,
                                   base=0, pattern=[[-1, P]], channel_multiplier=1).then_inc(made, 1)
                pool.iota(k["iota0"][:, :], pattern=[[1, WINDOW]], base=0, channel_multiplier=0,
                          allow_small_or_imprecise_dtypes=True).then_inc(made, 1)
                pool.wait_ge(made, 3)

            @block.vector
            def _(dve):
                dve.memset(k["eps"][:, :], EPS).then_inc(found, 1)
                dve.memset(none[:, :], 0.0).then_inc(found, 1)
                dve.wait_ge(blocks_loaded, 16)
                dve.tensor_copy(by_block_f[:, :, :], by_block[:, :, :]).then_inc(found, 1)
                dve.wait_ge(found, 3)
                dve.tensor_reduce(lowest[:, :], by_block_f[:, :, :], AX, ALU.min).then_inc(found, 1)
                dve.tensor_reduce(highest[:, :], by_block_f[:, :, :], AX, ALU.max).then_inc(found, 1)
                dve.wait_ge(found, 5)
                dve.tensor_tensor(span[:, :], highest[:, :], lowest[:, :], ALU.subtract).then_inc(found, 1)
                dve.wait_ge(found, 6)
                dve.tensor_reduce(span_max[:, :], span[:, :], AX, ALU.max).then_inc(found, 1)
                dve.wait_ge(lanes_loaded, 16)
                dve.tensor_copy(k["local"][:, :, :], by_lane[:, :].rearrange("p (b t) -> p b t", t=TILES))\
                   .then_inc(found, 1)
                dve.wait_ge(found, 8)
                dve.wait_ge(lo_loaded, 32)
                dve.tensor_tensor(k["local"][:, :, :], k["local"][:, :, :],
                                  lo_all[:, :, None].broadcast_to([P, BLOCKS, TILES]), ALU.subtract)\
                   .then_inc(found, 1)
                dve.wait_ge(spans_loaded, 16)
                dve.tensor_reduce(widest[:, :], spans[:, :], AX, ALU.max).then_inc(found, 1)
                dve.wait_ge(found, 10)
                dve.tensor_copy(k["passes"][:, :], widest[:, :]).then_inc(found, 1)
                dve.wait_ge(found, 11)


def hold(engine, sem, value, passed):
    engine.wait_ge(sem, value)
    engine.sem_inc(passed, 1)


class Turns:

    def __init__(self, engine, k):
        self.engine = engine
        self.passes = engine.value_load(k["passes"][0:1, 0:1], min_val=0, max_val=NODES) // WINDOW + 1

    def flat(self):
        return self.engine.Fori(0, self.passes * TURNS, 1)


def load_blocks(sp, k, loads, used, loaded, ended):
    def fill(slot, block):
        for dst, src in loads:
            sp.dma_start(dst[slot], src(block)).then_inc(loaded[slot], 16)

    turns = Turns(sp, k)
    for s in range(SLOTS):
        fill(s, 0 * SLOTS + s)
    with sp.Fori(0, turns.passes, 1) as p:
        with sp.Fori(0, TURNS, 1) as i:
            for s in range(SLOTS):
                sp.wait_ge(used, (p * TURNS + i) * SLOTS + s + 1)
                fill(s, i * SLOTS + (SLOTS + s))
    for s in range(SLOTS):
        hold(sp, loaded[s], (turns.passes * TURNS + 1) * (16 * len(loads)), ended)


def gather_rows(pool, k, table, idx, rows, loaded, per_load, gathered, started):
    turns = Turns(pool, k)
    with turns.flat() as g:
        for s in range(SLOTS):
            hold(pool, loaded[s], (g + 1) * per_load, started)
            for t in range(TILES):
                pool.indirect_dma_start(rows[s][:, t, :], None, table,
                                        bass.IndirectOffsetOnAxis(ap=idx[s][:, t:t + 1].bitcast(U32), axis=0))\
                    .then_inc(gathered[s], 16)


class Windows:

    def __init__(self, dve, k, iota, base_f, base, stepped, parts):
        self.dve, self.k, self.iota, self.base_f, self.base, self.stepped = dve, k, iota, base_f, base, stepped
        dve.memset(k["acc"][0:parts[0], 0:parts[1], :], 0.0).then_inc(stepped, 1)
        dve.tensor_copy(iota[:, :], k["iota0"][:, :]).then_inc(stepped, 1)
        dve.memset(base_f[:, :], float(NODES)).then_inc(stepped, 1)
        dve.wait_ge(stepped, 3)
        dve.tensor_copy(base_f[:, 1:BLOCKS + 1], k["lo"][:, :]).then_inc(stepped, 1)
        dve.wait_ge(stepped, 4)
        dve.tensor_copy(base[:, :], base_f[:, :]).then_inc(stepped, 1)
        dve.wait_ge(stepped, 5)

    def next_window(self, p):
        dve = self.dve
        dve.tensor_scalar(self.iota[:, :], self.iota[:, :], float(WINDOW), None, ALU.add).then_inc(self.stepped, 1)
        dve.tensor_scalar(self.base_f[:, :], self.base_f[:, :], float(WINDOW), float(NODES), ALU.add, ALU.min)\
           .then_inc(self.stepped, 1)
        dve.wait_ge(self.stepped, p * 3 + 7)
        dve.tensor_copy(self.base[:, :], self.base_f[:, :]).then_inc(self.stepped, 1)
        dve.wait_ge(self.stepped, p * 3 + 8)

    def bases(self, block, count=SLOTS):
        return nc_values(self.k["nc"], self.base[0:1, bass.ds(block + 1, count)])

    def one_hot(self, dst, block):
        return self.dve.tensor_tensor(
            dst[:, :, :], self.iota[:, None, :].broadcast_to([P, TILES, WINDOW]),
            self.k["local"][:, bass.ds(block, 1), :].rearrange("p b t -> p (b t)")[:, :, None]
            .broadcast_to([P, TILES, WINDOW]), ALU.is_equal)


def nc_values(nc, row):
    return nc.values_load_multi_w_load_instructions(row, engines=DVE_ONLY, min_val=0, max_val=NODES)[1]


def weighted_edges(nc, a, k, name, table, feats, fan_in, weights, biases, func):
    deep = len(weights) == 3
    halves = 2 if deep else 1
    fan_rows = halves * fan_in
    with ExitStack() as ctx:
        sb = lambda n, shape, dt=F32: ctx.enter_context(nc.sbuf_tensor(f"{name}_{n}", shape, dt))
        sem = lambda n: ctx.enter_context(nc.semaphore(f"{name}_{n}"))
        ring = lambda n, shape, dt=F32: [sb(f"{n}{s}", shape, dt) for s in range(SLOTS)]
        psum = lambda n, shape: ctx.enter_context(nc.psum_tensor(f"{name}_{n}_ps", shape, F32))
        idx, feat, sh = ring("idx", [P, TILES], I32), ring("feat", [fan_rows, BLOCK // halves]), ring("sh", [P, TILES, 4])
        rows, onehot, prod = ring("rows", [P, TILES, FEAT]), ring("onehot", [P, TILES, WINDOW]), ring("prod", [P, TILES, MSG])
        hidden = ring("hidden", [P, BLOCK])
        first = sb("first", [P, HALF])
        w_in, w_mid, w_out = sb("w_in", [fan_rows, halves * HID]), sb("w_mid", [P, 2, HID]), sb("w_out", [P, WPATHS])
        b_in, b_mid = sb("b_in", [halves * HID, 1]), sb("b_mid", [HID, 1])
        iota, base_f, base = sb("iota", [P, WINDOW]), sb("base_f", [1, BLOCKS + SLOTS]), sb("base", [1, BLOCKS + SLOTS], I32)
        vsh = sb("vsh", [P, TILES, MUL, 3])
        scaled_pair = [sb(f"scaled{s}", [P, TILES, MUL + FEAT]) for s in range(2)]
        to_s = sb("to_s", [P, TILES, MUL, 2 * MUL])
        s_v = sb("s_v", [P, TILES, MUL, MUL])
        v_v = sb("v_v", [P, TILES, 3 * MUL, MUL])
        sums = sb("sums", [P, TILES, MUL])
        banks = [psum("weights0", [P, 3 * 512]), psum("weights1", [P, 3 * 512])]
        hid_ps = psum("hid", [P, 512])
        win_ps = psum("win", [P, 512])
        loaded, gathered = [sem(f"loaded{s}") for s in range(SLOTS)], [sem(f"gathered{s}") for s in range(SLOTS)]
        params, ones = sem("params"), sem("ones")
        pre_ready, hidden_ready = sem("pre_ready"), sem("hidden_ready")
        w_ready, w_used = sem("w_ready"), sem("w_used")
        vec, summed, msg_ready, rows_scaled = sem("vec"), sem("summed"), sem("msg_ready"), sem("rows_scaled")
        spread, stepped = sem("spread"), sem("stepped")
        started, ended, held, zeroed = sem("started"), sem("ended"), sem("held"), sem("zeroed")
        PARAMS = 16 * (4 if not deep else 9)
        PER_BLOCK = 3 if deep else 2
        VEC = 5
        ZEROED = SLOTS + 3

        with nc.Block() as block:
            @block.sync
            def _(sp):
                sp.wait_ge(ones, ZEROED)
                for h in range(halves):
                    sp.dma_start(w_in[h * fan_in:(h + 1) * fan_in, h * HID:(h + 1) * HID], a[weights[0]]).then_inc(params, 16)
                    sp.dma_start(b_in[h * HID:(h + 1) * HID, :], a[biases[0]].rearrange("(h o) -> h o", o=1))\
                      .then_inc(params, 16)
                if deep:
                    for h in range(2):
                        sp.dma_start(w_mid[h * HID:(h + 1) * HID, h, :], a[weights[1]]).then_inc(params, 16)
                    sp.dma_start(b_mid[:, :], a[biases[1]].rearrange("(h o) -> h o", o=1)).then_inc(params, 16)
                sp.dma_start(w_out[0:HID, :], a[weights[-1]]).then_inc(params, 16)
                sp.dma_start(w_out[HID:HID + 1, :], a[biases[-1]].rearrange("(o n) -> o n", o=1)).then_inc(params, 16)
                load_blocks(sp, k, [
                    ([x[:, :] for x in idx], lambda b: one(a["src_blocks"], b)),
                    ([x[:, :, :].rearrange("p t c -> p (t c)") for x in sh],
                     lambda b: one(a["sh4"], b, "b p t c -> p (b t c)")),
                    ([x[:, :] for x in feat], lambda b: one(a[feats], b)),
                ], msg_ready, loaded, ended)

            @block.gpsimd
            def _(pool):
                gather_rows(pool, k, table, idx, rows, loaded, 48, gathered, started)

            @block.tensor
            def _(pe):
                def hidden_mm(b, slot, u):
                    if isinstance(b, int) and b * PER_BLOCK + u == 0:
                        pe.wait_ge(params, PARAMS)
                    else:
                        hold(pe, hidden_ready, b * PER_BLOCK + u, held)
                    if deep and u > 0:
                        mm = pe.matmul(hid_ps[0:HID, 0:HALF], w_mid[:, u - 1, :], first[:, :], start=True, stop=True)
                    else:
                        mm = pe.matmul(hid_ps[0:halves * HID, 0:HALF], w_in[:, :], feat[slot][:, u * HALF:(u + 1) * HALF],
                                       start=True, stop=True)
                    mm.then_inc(pre_ready, 1)

                def weight_mm(b, slot, bank, tiles):
                    for t in tiles:
                        if t == 0:
                            pe.wait_ge(hidden_ready, (b + 1) * PER_BLOCK)
                            if not isinstance(b, int):
                                pe.wait_ge(w_used, b + 1)
                        mm = pe.matmul(banks[bank][:, t * WPATHS:(t + 1) * WPATHS],
                                       hidden[slot][:, t * P:(t + 1) * P], w_out[:, :], start=True, stop=True)
                        if t == TILES - 1:
                            mm.then_inc(w_ready, 1)

                def both(b_h, slot_h, turn_h, b_w, slot_w, bank_w):
                    pe.wait_ge(loaded[slot_h], turn_h * 48 + 48)
                    hidden_mm(b_h, slot_h, 0)
                    weight_mm(b_w, slot_w, bank_w, [0, 1])
                    hidden_mm(b_h, slot_h, 1)
                    weight_mm(b_w, slot_w, bank_w, [2, 3])
                    if deep:
                        hidden_mm(b_h, slot_h, 2)
                    weight_mm(b_w, slot_w, bank_w, [4])

                turns = Turns(pe, k)
                pe.sem_inc(spread, 1)
                pe.wait_ge(ones, ZEROED + SLOTS + 1)
                pe.wait_ge(loaded[0], 48)
                for u in range(PER_BLOCK):
                    hidden_mm(0, 0, u)
                both(1, 1, 0, 0, 0, 0)
                with pe.Fori(0, turns.passes, 1) as p:
                    with pe.Fori(0, TURNS, 1) as i:
                        g = p * TURNS + i
                        for s in range(SLOTS):
                            n = g * SLOTS + s
                            both(n + 2, (s + 2) % SLOTS, g + (s + 2) // SLOTS, n + 1, (s + 1) % SLOTS, (s + 1) % 2)
                            pe.wait_ge(summed, n + p + 2)
                            pe.wait_ge(msg_ready, n + 1)
                            for c in range(2):
                                for t in range(TILES):
                                    columns = prod[s][:, t, c * P:min((c + 1) * P, MSG)]
                                    mm = pe.matmul(win_ps[0:min(P, MSG - c * P), c * WINDOW:(c + 1) * WINDOW],
                                                   columns, onehot[s][:, t, :],
                                                   start=(t == 0), stop=(t == TILES - 1))
                            mm.then_inc(spread, 1)

            @block.scalar
            def _(act):
                def block_act(b, slot):
                    for u in range(PER_BLOCK):
                        act.wait_ge(pre_ready, b * PER_BLOCK + u + 1)
                        if deep and u == 0:
                            step = nc.scalar.activation(first[:, :], hid_ps[:, 0:HALF], func, bias=b_in[:, 0:1])
                        else:
                            half = u - 1 if deep else u
                            step = nc.scalar.activation(
                                hidden[slot][0:HID, half * HALF:(half + 1) * HALF], hid_ps[0:HID, 0:HALF], func,
                                bias=(b_mid if deep else b_in)[:, 0:1])
                        step.then_inc(hidden_ready, 1)

                def scale_rows(g, s):
                    act.wait_ge(gathered[s], g * (16 * TILES) + 16 * TILES)
                    act.wait_ge(loaded[s], g * 48 + 48)
                    act.wait_ge(w_used, g * SLOTS + s + 1)
                    for t in range(TILES):
                        last = nc.scalar.activation(scaled_pair[s % 2][:, t, MUL:], rows[s][:, t, :], ACT.Copy,
                                                    scale=sh[s][:, t, 0:1])
                    last.then_inc(rows_scaled, 1)

                turns = Turns(act, k)
                act.wait_ge(params, PARAMS)
                block_act(0, 0)
                block_act(1, 1)
                with turns.flat() as g:
                    for s in range(SLOTS):
                        if not deep:
                            scale_rows(g, s)
                        block_act(g * SLOTS + s + 2, (s + 2) % SLOTS)

            @block.vector
            def _(dve):
                for s in range(SLOTS):
                    dve.memset(hidden[s][HID:, :], 0.0).then_inc(ones, 1)
                dve.memset(w_out[HID:, :], 0.0).then_inc(ones, 1)
                dve.memset(w_in[:, :], 0.0).then_inc(ones, 1)
                dve.memset(w_mid[:, :, :], 0.0).then_inc(ones, 1)
                dve.wait_ge(ones, ZEROED)
                for s in range(SLOTS):
                    dve.memset(hidden[s][HID:HID + 1, :], 1.0).then_inc(ones, 1)
                dve.wait_ge(params, PARAMS)
                dots = w_out[0:HID + 1, 0:2 * MUL * MUL].rearrange("h (o q i) -> h o q i", q=2, i=MUL)[:, :, 0, :]
                dve.tensor_scalar(dots, dots, float(1 / np.sqrt(3.0)), None, ALU.mult).then_inc(ones, 1)
                win = Windows(dve, k, iota, base_f, base, stepped, (P, 2))
                dve.sem_inc(summed, 1)
                dve.sem_inc(w_used, 2)
                dve.memset(win_ps[:, 0:2 * WINDOW], 0.0).then_inc(zeroed, 1)
                dve.wait_ge(zeroed, 1)
                turns = Turns(dve, k)

                def add_window(count, at):
                    dve.wait_ge(summed, count)
                    dst = k["acc"][:, :, bass.ds(at, WINDOW)]
                    dve.tensor_tensor(dst, dst, win_ps[:, 0:2 * WINDOW].rearrange("p (c w) -> p c w", c=2),
                                      ALU.add).then_inc(summed, 1)

                with dve.Fori(0, turns.passes, 1) as p:
                    with dve.Fori(0, TURNS, 1) as i:
                        g = p * TURNS + i
                        before = win.bases(i * SLOTS - 1)
                        for s in range(SLOTS):
                            n = g * SLOTS + s
                            x, h, scaled = rows[s], sh[s], scaled_pair[s % 2]
                            harm = h[:, :, 1:4][:, :, None, :].broadcast_to([P, TILES, MUL, 3])
                            vecs = x[:, :, MUL:].rearrange("p t (i m) -> p t i m", m=3)
                            win.one_hot(onehot[s], i * SLOTS + s).then_inc(vec, 1)
                            dve.wait_ge(gathered[s], g * (16 * TILES) + 16 * TILES)
                            dve.wait_ge(loaded[s], g * 48 + 48)
                            dve.tensor_tensor(vsh[:, :, :, :], vecs, harm, ALU.mult).then_inc(vec, 1)
                            if deep:
                                dve.tensor_tensor(scaled[:, :, MUL:], x[:, :, :],
                                                  h[:, :, 0:1].broadcast_to([P, TILES, FEAT]), ALU.mult)\
                                    .then_inc(rows_scaled, 1)
                            dve.wait_ge(w_ready, n + 1)
                            w = banks[s % 2][:, 0:TILES * WPATHS].rearrange("p (t n) -> p t n", t=TILES)
                            w_s = w[:, :, 0:2 * MUL * MUL].rearrange("p t (o i) -> p t o i", o=MUL)
                            w_sv = w[:, :, 2 * MUL * MUL:3 * MUL * MUL].rearrange("p t (o i) -> p t o i", o=MUL)
                            w_vv = w[:, :, 3 * MUL * MUL:].rearrange("p t (o i) -> p t o i", o=MUL)
                            dve.tensor_tensor(s_v[:, :, :, :], w_sv,
                                              x[:, :, None, 0:MUL].broadcast_to([P, TILES, MUL, MUL]), ALU.mult)
                            dve.wait_ge(vec, n * VEC + 2)
                            dve.tensor_reduce(scaled[:, :, 0:MUL], vsh[:, :, :, :], AX, ALU.add).then_inc(vec, 1)
                            dve.wait_ge(rows_scaled, n + 1)
                            for m in range(3):
                                v_m = scaled[:, :, 2 * MUL:].rearrange("p t (i m) -> p t m i", m=3)[:, :, m]
                                last = dve.tensor_tensor(
                                    v_v[:, :, m * MUL:(m + 1) * MUL, :], w_vv,
                                    v_m[:, :, None, :].broadcast_to([P, TILES, MUL, MUL]), ALU.mult)
                            last.then_inc(vec, 1)
                            dve.wait_ge(vec, n * VEC + 3)
                            dve.tensor_tensor(to_s[:, :, :, :], w_s,
                                              scaled[:, :, None, 0:2 * MUL].broadcast_to([P, TILES, MUL, 2 * MUL]),
                                              ALU.mult).then_inc(w_used, 1)
                            dve.wait_ge(spread, n + 1)
                            add_window(n + p + 1, before[s])
                            dve.wait_ge(w_used, n + 3)
                            dve.tensor_reduce(sums[:, :, :], s_v[:, :, :, :], AX, ALU.add).then_inc(vec, 1)
                            dve.tensor_tensor(prod[s][:, :, 0:TO_S].rearrange("p t (o i) -> p t o i", o=MUL),
                                              to_s[:, :, :, 0:MUL], to_s[:, :, :, MUL:], ALU.add)
                            dve.tensor_tensor(
                                prod[s][:, :, TO_S:TO_S + V_V].rearrange("p t (o i) -> p t o i", i=MUL // 2),
                                v_v[:, :, :, 0:MUL // 2], v_v[:, :, :, MUL // 2:], ALU.add)
                            dve.wait_ge(vec, n * VEC + 5)
                            dve.tensor_tensor(prod[s][:, :, TO_S + V_V:].rearrange("p t (o m) -> p t o m", m=3),
                                              sums[:, :, :, None].broadcast_to([P, TILES, MUL, 3]), harm,
                                              ALU.mult).then_inc(msg_ready, 1)
                    last_base = win.bases(BLOCKS - 1, 1)[0]
                    dve.wait_ge(spread, (p + 1) * BLOCKS + 1)
                    add_window((p + 1) * BLOCKS + p + 1, last_base)
                    win.next_window(p)


def one(src, b, to="b p t -> p (b t)"):
    return src[bass.ds(b, 1)].rearrange(to)


def coupled_edges(nc, a, k, table):
    with ExitStack() as ctx:
        sb = lambda n, shape, dt=F32: ctx.enter_context(nc.sbuf_tensor(f"coupled_{n}", shape, dt))
        sem = lambda n: ctx.enter_context(nc.semaphore(f"coupled_{n}"))
        ring = lambda n, shape, dt=F32: [sb(f"{n}{s}", shape, dt) for s in range(SLOTS)]
        idx, sh = ring("idx", [P, TILES], I32), ring("sh", [P, TILES, HARM])
        rows, onehot = ring("rows", [P, TILES, FEAT]), ring("onehot", [P, TILES, WINDOW])
        prod = ring("prod", [P, TILES, 2 * OCH])
        iota, base_f, base = sb("iota", [P, WINDOW]), sb("base_f", [1, BLOCKS + SLOTS]), sb("base", [1, BLOCKS + SLOTS], I32)
        win_ps = [ctx.enter_context(nc.psum_tensor(f"coupled_win{b}", [P, 512], F32)) for b in range(2)]
        loaded, gathered = [sem(f"loaded{s}") for s in range(SLOTS)], [sem(f"gathered{s}") for s in range(SLOTS)]
        msg_ready, spread, summed, stepped, ones = sem("msg_ready"), sem("spread"), sem("summed"), sem("stepped"), sem("ones")
        started, ended = sem("started"), sem("ended")

        with nc.Block() as block:
            @block.sync
            def _(sp):
                load_blocks(sp, k, [
                    ([x[:, :] for x in idx], lambda b: one(a["src_blocks"], b)),
                    ([x[:, :, :].rearrange("p t c -> p (t c)") for x in sh],
                     lambda b: one(a["sh9"], b, "b p t c -> p (b t c)")),
                ], msg_ready, loaded, ended)

            @block.gpsimd
            def _(pool):
                gather_rows(pool, k, table, idx, rows, loaded, 32, gathered, started)

            @block.tensor
            def _(pe):
                turns = Turns(pe, k)
                pe.wait_ge(ones, 2 * SLOTS)
                with turns.flat() as g:
                    for s in range(SLOTS):
                        n = g * SLOTS + s
                        if s == 0:
                            pe.wait_ge(summed, n + 1)
                        else:
                            pe.wait_ge(summed, n)
                        pe.wait_ge(msg_ready, n + 1)
                        for c in range(2):
                            for t in range(TILES):
                                mm = pe.matmul(win_ps[s % 2][0:OCH, c * WINDOW:(c + 1) * WINDOW],
                                               prod[s][:, t, c * OCH:(c + 1) * OCH], onehot[s][:, t, :],
                                               start=(t == 0), stop=(t == TILES - 1))
                        mm.then_inc(spread, 1)

            @block.vector
            def _(dve):
                for s in range(SLOTS):
                    dve.memset(prod[s][:, :, OUTER:OUTER + 1], 1.0).then_inc(ones, 1)
                    dve.memset(prod[s][:, :, OUTER + 1:], 0.0).then_inc(ones, 1)
                win = Windows(dve, k, iota, base_f, base, stepped, (P, 2))
                dve.sem_inc(summed, 1)
                turns = Turns(dve, k)

                def add_window(n, s, at):
                    dve.wait_ge(summed, n + 1)
                    dve.wait_ge(spread, n + 1)
                    dst = k["acc"][0:OCH, :, bass.ds(at, WINDOW)]
                    dve.tensor_tensor(dst, dst, win_ps[s % 2][0:OCH, 0:2 * WINDOW].rearrange("p (c w) -> p c w", c=2),
                                      ALU.add).then_inc(summed, 1)

                with dve.Fori(0, turns.passes, 1) as p:
                    with dve.Fori(0, TURNS, 1) as i:
                        g = p * TURNS + i
                        bases = win.bases(i * SLOTS)
                        for s in range(SLOTS):
                            n = g * SLOTS + s
                            x, h = rows[s], sh[s]
                            win.one_hot(onehot[s], i * SLOTS + s)
                            dve.wait_ge(gathered[s], g * (16 * TILES) + 16 * TILES)
                            dve.wait_ge(loaded[s], g * 32 + 32)
                            dve.tensor_tensor(
                                prod[s][:, :, 0:4 * FEAT].rearrange("p t (c f) -> p t c f", c=4),
                                h[:, :, 0:4][:, :, :, None].broadcast_to([P, TILES, 4, FEAT]),
                                x[:, :, None, :].broadcast_to([P, TILES, 4, FEAT]), ALU.mult)
                            dve.tensor_tensor(
                                prod[s][:, :, 4 * FEAT:OUTER].rearrange("p t (c f) -> p t c f", c=5),
                                h[:, :, 4:9][:, :, :, None].broadcast_to([P, TILES, 5, 3 * MUL]),
                                x[:, :, None, MUL:].broadcast_to([P, TILES, 5, 3 * MUL]), ALU.mult)\
                                .then_inc(msg_ready, 1)
                            if s > 0:
                                add_window(n - 1, s - 1, bases[s - 1])
                        add_window(g * SLOTS + (SLOTS - 1), SLOTS - 1, bases[SLOTS - 1])
                    win.next_window(p)


def conv_edges(nc, a, k, name, table):
    with ExitStack() as ctx:
        sb = lambda n, shape, dt=F32: ctx.enter_context(nc.sbuf_tensor(f"{name}_{n}", shape, dt))
        sem = lambda n: ctx.enter_context(nc.semaphore(f"{name}_{n}"))
        ring = lambda n, shape, dt=F32: [sb(f"{n}{s}", shape, dt) for s in range(SLOTS)]
        idx = ring("idx", [P, TILES], I32)
        rows, onehot = ring("rows", [P, TILES, FEAT]), ring("onehot", [P, TILES, WINDOW])
        iota, base_f, base = sb("iota", [P, WINDOW]), sb("base_f", [1, BLOCKS + SLOTS]), sb("base", [1, BLOCKS + SLOTS], I32)
        win_ps = [ctx.enter_context(nc.psum_tensor(f"{name}_win{b}", [P, 512], F32)) for b in range(2)]
        loaded, gathered = [sem(f"loaded{s}") for s in range(SLOTS)], [sem(f"gathered{s}") for s in range(SLOTS)]
        msg_ready, spread, summed, stepped = sem("msg_ready"), sem("spread"), sem("summed"), sem("stepped")
        started, ended = sem("started"), sem("ended")

        with nc.Block() as block:
            @block.sync
            def _(sp):
                load_blocks(sp, k, [([x[:, :] for x in idx], lambda b: one(a["src_blocks"], b))],
                            spread, loaded, ended)

            @block.gpsimd
            def _(pool):
                gather_rows(pool, k, table, idx, rows, loaded, 16, gathered, started)

            @block.tensor
            def _(pe):
                turns = Turns(pe, k)
                with turns.flat() as g:
                    for s in range(SLOTS):
                        n = g * SLOTS + s
                        if s == 0:
                            pe.wait_ge(summed, n + 1)
                        else:
                            pe.wait_ge(summed, n)
                        pe.wait_ge(msg_ready, n + 1)
                        pe.wait_ge(gathered[s], g * (16 * TILES) + 16 * TILES)
                        for t in range(TILES):
                            mm = pe.matmul(win_ps[s % 2][0:FEAT, 0:WINDOW], rows[s][:, t, :], onehot[s][:, t, :],
                                           start=(t == 0), stop=(t == TILES - 1))
                        mm.then_inc(spread, 1)

            @block.vector
            def _(dve):
                win = Windows(dve, k, iota, base_f, base, stepped, (FEAT, 1))
                dve.sem_inc(summed, 1)
                turns = Turns(dve, k)

                def add_window(n, s, at):
                    dve.wait_ge(summed, n + 1)
                    dve.wait_ge(spread, n + 1)
                    dst = k["acc"][0:FEAT, 0, bass.ds(at, WINDOW)]
                    dve.tensor_tensor(dst, dst, win_ps[s % 2][0:FEAT, 0:WINDOW], ALU.add).then_inc(summed, 1)

                with dve.Fori(0, turns.passes, 1) as p:
                    with dve.Fori(0, TURNS, 1) as i:
                        g = p * TURNS + i
                        bases = win.bases(i * SLOTS)
                        for s in range(SLOTS):
                            n = g * SLOTS + s
                            win.one_hot(onehot[s], i * SLOTS + s).then_inc(msg_ready, 1)
                            if s > 0:
                                add_window(n - 1, s - 1, bases[s - 1])
                        add_window(g * SLOTS + (SLOTS - 1), SLOTS - 1, bases[SLOTS - 1])
                    win.next_window(p)


def node_phase(nc, name):
    ctx = ExitStack()
    sb = lambda n, shape, dt=F32: ctx.enter_context(nc.sbuf_tensor(f"{name}_{n}", shape, dt))
    sem = lambda n: ctx.enter_context(nc.semaphore(f"{name}_{n}"))
    psum = lambda n, shape: ctx.enter_context(nc.psum_tensor(f"{name}_{n}_ps", shape, F32))
    return ctx, sb, sem, psum


LEAD = 2


def groups(engine):
    with engine.Fori(0, GROUPS // 2, 1) as turn:
        for slot in range(2):
            yield turn * 2 + slot, slot


def of_group(t, g):
    return t[:, bass.ds(g * GROUP, GROUP)]


def table_rows(t, g):
    return t.rearrange("(p j) f -> p j f", j=NODE_TILES)[:, bass.ds(g * GROUP, GROUP), :]


def acc_columns(k, rows, part, g):
    return k["acc"][0:rows, part, 0:NODES].rearrange("r (p j) -> r j p", j=NODE_TILES)[:, bass.ds(g * GROUP, GROUP), :]


def store_groups(sp, t, table, done, steps, stored):
    for g, _ in groups(sp):
        sp.wait_ge(done, (g + 1 + LEAD) * steps)
        sp.dma_start(table_rows(table, g), of_group(t, g)).then_inc(stored, 16)
    sp.wait_ge(stored, 16 * GROUPS)


class Steps:

    def __init__(self, dve, done, per_group, g):
        self.dve, self.done, self.base, self.n = dve, done, (g + LEAD) * per_group, 0

    def __call__(self, instruction):
        instruction.then_inc(self.done, 1)
        self.n += 1
        return self.n

    def wait(self, n):
        self.dve.wait_ge(self.done, self.base + n)


def normalise(step, dve, b, xn, root_ready, g):
    over = lambda t: t[:, :, None].broadcast_to([NT, GROUP, FEAT])
    step.wait(step(dve.tensor_reduce(b["total"][:, :], b["y"][:, :, :], AX, ALU.add)))
    step.wait(step(dve.scalar_tensor_tensor(b["y"][:, :, :], over(b["total"]), -1.0 / FEAT, b["y"][:, :, :],
                                            ALU.mult, ALU.add)))
    step.wait(step(dve.tensor_tensor(b["sq"][:, :, :], b["y"][:, :, :], b["y"][:, :, :], ALU.mult)))
    step(dve.tensor_reduce(b["var"][:, :], b["sq"][:, :, :], AX, ALU.add))
    dve.wait_ge(root_ready, g + 1)
    step.wait(step(dve.reciprocal(b["rstd"][:, :], b["root"][:, :])))
    step(dve.tensor_tensor(xn, b["y"][:, :, :], over(b["rstd"]), ALU.mult))


def root_of_variance(nc, k, b):
    return nc.scalar.activation(b["root"][:, :], b["var"][:, :], ACT.Sqrt, scale=1.0 / FEAT, bias=k["eps"][0:NT, 0:1])


def norm_buffers(sb):
    b = {n: sb(n, [NT, GROUP, FEAT]) for n in ("y", "sq")}
    return b | {n: sb(n, [NT, GROUP]) for n in ("total", "var", "root", "rstd")}


def pair(make, name, shape):
    return [make(f"{name}{s}", shape) for s in range(2)]


def next_group(g):
    return (g + 1) % GROUPS


def weighted_nodes(nc, a, k, name, table, self_w, agg_scale, self_scale):
    ctx, sb, sem, psum = node_phase(nc, f"{name}_nodes")
    with ctx:
        x, xt = pair(sb, "x", [NT, GROUP, FEAT]), pair(sb, "xt", [FEAT, GROUP, NT])
        sums = pair(sb, "sums", [P, 2, GROUP, NT])
        own, ends = sb("own", [FEAT, FEAT]), sb("ends", [P, 2, FEAT])
        b = norm_buffers(sb)
        xt_ps, y_ps = pair(psum, "xt", [FEAT, 3 * 512]), pair(psum, "y", [NT, 512])
        params, scaled, turned, mixed = sem("params"), sem("scaled"), sem("turned"), sem("mixed")
        copied, done, root_ready, stored = sem("copied"), sem("done"), sem("root_ready"), sem("stored")
        STEPS, COPIES, VAR = 7, 4, 5
        with nc.Block() as block:
            @block.sync
            def _(sp):
                sp.dma_start(own[:, :], a[self_w]).then_inc(params, 16)
                sp.dma_start(ends[:, :, :], a["sum_columns"].rearrange("c p f -> p c f")).then_inc(params, 16)
                store_groups(sp, k["x"], table, done, STEPS, stored)

            @block.tensor
            def _(pe):
                pe.sem_inc(mixed, LEAD)
                pe.wait_ge(scaled, 2)
                for g, s in groups(pe):
                    pe.wait_ge(copied, g * COPIES + 1)
                    for q in range(GROUP):
                        mm = pe.transpose(xt_ps[s][:, q * P:q * P + NT], x[s][:, q, :], k["ident"][0:NT, 0:NT])
                    mm.then_inc(turned, 1)
                    pe.wait_ge(copied, g * COPIES + COPIES)
                    pe.wait_ge(done, g * STEPS + 1)
                    for q in range(GROUP):
                        y = y_ps[s][:, q * FEAT:(q + 1) * FEAT]
                        for c in range(2):
                            pe.matmul(y, sums[s][:, c, q, :], ends[:, c, :], start=(c == 0), stop=False)
                        mm = pe.matmul(y, xt[s][:, q, :], own[:, :], start=False, stop=True)
                    mm.then_inc(mixed, 1)

            @block.scalar
            def _(act):
                def copies(g, s):
                    nc.scalar.activation(x[s][:, :, :], of_group(k["x"], g), ACT.Copy).then_inc(copied, 1)
                    for c in range(2):
                        nc.scalar.activation(sums[s][:, c], acc_columns(k, P, c, g), ACT.Copy).then_inc(copied, 1)

                copies(0, 0)
                for g, s in groups(act):
                    act.wait_ge(turned, g + 1)
                    nc.scalar.activation(xt[s][:, :, :], tiles_of(xt_ps[s], FEAT), ACT.Copy).then_inc(copied, 1)
                    act.wait_ge(mixed, g - 1 + 1 + LEAD)
                    copies(next_group(g), 1 - s)
                    act.wait_ge(done, (g + LEAD) * STEPS + VAR)
                    root_of_variance(nc, k, b).then_inc(root_ready, 1)

            @block.vector
            def _(dve):
                dve.sem_inc(done, LEAD * STEPS)
                dve.wait_ge(params, 32)
                dve.tensor_scalar(own[:, :], own[:, :], float(self_scale), None, ALU.mult).then_inc(scaled, 1)
                dve.tensor_scalar(ends[:, :, :], ends[:, :, :], float(agg_scale), None, ALU.mult).then_inc(scaled, 1)
                for g, s in groups(dve):
                    step = Steps(dve, done, STEPS, g)
                    step.wait(0)
                    dve.wait_ge(mixed, g + 1 + LEAD)
                    y = y_ps[s][:, 0:GROUP * FEAT].rearrange("p (q f) -> p q f", q=GROUP)
                    step.wait(step(dve.tensor_tensor(b["y"][:, :, :], y, of_group(k["x"], g), ALU.add)))
                    normalise(step, dve, b, of_group(k["x"], g), root_ready, g)


def tiles_of(ps, rows):
    return ps[0:rows, 0:GROUP * P].rearrange("r (q p) -> r q p", p=P)[:, :, 0:NT]


def coupled_nodes(nc, a, k, u_table):
    ctx, sb, sem, psum = node_phase(nc, "coupled_nodes")
    with ctx:
        sums = pair(sb, "sums", [OCH, 2, GROUP, NT])
        mix, coef = sb("mix", [OCH, 2, FEAT + 1]), sb("coef", [OCH, 2, FEAT + 1])
        deg, root_d = sb("deg", [NT, GROUP]), sb("root_d", [NT, GROUP])
        b = norm_buffers(sb)
        y_ps = pair(psum, "y", [NT, 512])
        params, mix_ready, mixed, copied = sem("params"), sem("mix_ready"), sem("mixed"), sem("copied")
        done, root_ready, rootd_ready, stored = sem("done"), sem("root_ready"), sem("rootd_ready"), sem("stored")
        STEPS, COPIES, DEG, VAR = 10, 2, 2, 6
        with nc.Block() as block:
            @block.sync
            def _(sp):
                sp.dma_start(mix[:, :, :], a["L1_mix"].rearrange("c p f -> p c f")).then_inc(params, 16)
                sp.dma_start(coef[:, :, :], a["L1_coef"].rearrange("c p f -> p c f")).then_inc(params, 16)
                store_groups(sp, k["u"], u_table, done, STEPS, stored)

            @block.tensor
            def _(pe):
                pe.sem_inc(mixed, LEAD)
                pe.wait_ge(mix_ready, 1)
                for g, s in groups(pe):
                    pe.wait_ge(copied, g * COPIES + COPIES)
                    pe.wait_ge(done, g * STEPS + DEG)
                    for q in range(GROUP):
                        for c in range(2):
                            mm = pe.matmul(y_ps[s][:, q * (FEAT + 1):(q + 1) * (FEAT + 1)], sums[s][:, c, q, :],
                                           mix[:, c, :], start=(c == 0), stop=(c == 1))
                    mm.then_inc(mixed, 1)

            @block.scalar
            def _(act):
                def copies(g, s):
                    for c in range(2):
                        nc.scalar.activation(sums[s][:, c], acc_columns(k, OCH, c, g), ACT.Copy).then_inc(copied, 1)

                copies(0, 0)
                for g, s in groups(act):
                    act.wait_ge(mixed, g - 1 + 1 + LEAD)
                    copies(next_group(g), 1 - s)
                    act.wait_ge(done, (g + LEAD) * STEPS + DEG)
                    nc.scalar.activation(root_d[:, :], deg[:, :], ACT.Sqrt).then_inc(rootd_ready, 1)
                    act.wait_ge(done, (g + LEAD) * STEPS + VAR)
                    root_of_variance(nc, k, b).then_inc(root_ready, 1)

            @block.vector
            def _(dve):
                dve.sem_inc(done, LEAD * STEPS)
                dve.wait_ge(params, 32)
                dve.tensor_tensor(mix[:, :, :], mix[:, :, :], coef[:, :, :], ALU.mult).then_inc(mix_ready, 1)
                for g, s in groups(dve):
                    step = Steps(dve, done, STEPS, g)
                    step.wait(0)
                    dve.wait_ge(mixed, g + 1 + LEAD)
                    y = y_ps[s][:, 0:GROUP * (FEAT + 1)].rearrange("p (q f) -> p q f", q=GROUP)
                    x, dinv = of_group(k["x"], g), of_group(k["dinv"], g)
                    step(dve.tensor_tensor(b["y"][:, :, :], y[:, :, 0:FEAT], x, ALU.add))
                    step.wait(step(dve.tensor_scalar(deg[:, :], y[:, :, FEAT], 1.0, None, ALU.add)))
                    normalise(step, dve, b, x, root_ready, g)
                    dve.wait_ge(rootd_ready, g + 1)
                    step.wait(step(dve.reciprocal(dinv, root_d[:, :])))
                    step(dve.tensor_tensor(of_group(k["u"], g), x, dinv[:, :, None].broadcast_to([NT, GROUP, FEAT]), ALU.mult))


def conv1_nodes(nc, a, k, u_table):
    ctx, sb, sem, psum = node_phase(nc, "conv1_nodes")
    with ctx:
        sums, z = pair(sb, "sums", [FEAT, GROUP, NT]), sb("z", [NT, GROUP, FEAT])
        zt, h = sb("zt", [FEAT, GROUP, NT]), sb("h", [HID, GROUP, NT])
        w1, b1, w2 = sb("w1", [FEAT, HID]), sb("b1", [HID, 1]), sb("w2", [HID, FEAT])
        agg_ps, o_ps = psum("agg", [NT, 512]), psum("o", [NT, 512])
        zt_ps, h_ps = psum("zt", [FEAT, 3 * 512]), psum("h", [HID, 3 * 512])
        params, copied, turned, done, stored = (sem(n) for n in ("params", "copied", "turned", "done", "stored"))
        STEPS, TURNED, COPIES = 3, 4, 3
        with nc.Block() as block:
            @block.sync
            def _(sp):
                sp.dma_start(w1[:, :], a["L2_gnn_W1"]).then_inc(params, 16)
                sp.dma_start(b1[:, :], a["L2_gnn_b1"].rearrange("(h o) -> h o", o=1)).then_inc(params, 16)
                sp.dma_start(w2[:, :], a["L2_gnn_W2"]).then_inc(params, 16)
                store_groups(sp, k["u"], u_table, done, STEPS, stored)

            @block.tensor
            def _(pe):
                pe.sem_inc(turned, LEAD * TURNED)
                pe.wait_ge(params, 48)
                for g, s in groups(pe):
                    pe.wait_ge(copied, g * COPIES + 1)
                    for q in range(GROUP):
                        mm = pe.matmul(agg_ps[:, q * FEAT:(q + 1) * FEAT], sums[s][:, q, :],
                                       k["ident"][0:FEAT, 0:FEAT], start=True, stop=True)
                    mm.then_inc(turned, 1)
                    pe.wait_ge(done, (g + LEAD) * STEPS + 2)
                    for q in range(GROUP):
                        mm = pe.transpose(zt_ps[:, q * P:q * P + NT], z[:, q, :], k["ident"][0:NT, 0:NT])
                    mm.then_inc(turned, 1)
                    pe.wait_ge(copied, g * COPIES + 2)
                    for q in range(0, GROUP, 4):
                        some = slice(q, min(q + 4, GROUP))
                        mm = pe.matmul(tiles_of(h_ps, HID)[:, some, :], w1[:, :], zt[:, some, :], start=True, stop=True)
                    mm.then_inc(turned, 1)
                    pe.wait_ge(copied, g * COPIES + 3)
                    for q in range(GROUP):
                        mm = pe.matmul(o_ps[:, q * FEAT:(q + 1) * FEAT], h[:, q, :], w2[:, :], start=True, stop=True)
                    mm.then_inc(turned, 1)

            @block.scalar
            def _(act):
                def copies(g, s):
                    return nc.scalar.activation(sums[s][:, :, :], acc_columns(k, FEAT, 0, g), ACT.Copy)

                copies(0, 0).then_inc(copied, 1)
                act.wait_ge(params, 48)
                for g, s in groups(act):
                    act.wait_ge(turned, (g + LEAD) * TURNED + 2)
                    nc.scalar.activation(zt[:, :, :], tiles_of(zt_ps, FEAT), ACT.Copy).then_inc(copied, 1)
                    act.wait_ge(turned, (g + LEAD) * TURNED + 3)
                    nc.scalar.activation(h[:, :, :], tiles_of(h_ps, HID), ACT.Relu, bias=b1[:, 0:1]).then_inc(copied, 1)
                    copies(next_group(g), 1 - s).then_inc(copied, 1)

            @block.vector
            def _(dve):
                dve.sem_inc(done, LEAD * STEPS)
                for g, s in groups(dve):
                    step = Steps(dve, done, STEPS, g)
                    step.wait(0)
                    u, dinv = of_group(k["u"], g), of_group(k["dinv"], g)[:, :, None].broadcast_to([NT, GROUP, FEAT])
                    as_rows = lambda ps: ps[:, 0:GROUP * FEAT].rearrange("p (q f) -> p q f", q=GROUP)
                    dve.wait_ge(turned, (g + LEAD) * TURNED + 1)
                    step.wait(step(dve.tensor_tensor(z[:, :, :], as_rows(agg_ps), u, ALU.add)))
                    step(dve.tensor_tensor(z[:, :, :], z[:, :, :], dinv, ALU.mult))
                    dve.wait_ge(turned, (g + LEAD) * TURNED + 4)
                    step(dve.tensor_tensor(u, as_rows(o_ps), dinv, ALU.mult))


def conv2_nodes(nc, a, k, table):
    ctx, sb, sem, psum = node_phase(nc, "conv2_nodes")
    with ctx:
        sums, z, bias = pair(sb, "sums", [FEAT, GROUP, NT]), sb("z", [NT, GROUP, FEAT]), sb("bias", [NT, FEAT])
        b = norm_buffers(sb)
        agg_ps = pair(psum, "agg", [NT, 512])
        params, copied, turned, done, root_ready, stored = (
            sem(n) for n in ("params", "copied", "turned", "done", "root_ready", "stored"))
        STEPS, VAR = 10, 8
        with nc.Block() as block:
            @block.sync
            def _(sp):
                sp.dma_start(bias[:, :], a["L2_gnn_b2"].rearrange("(o n) -> o n", o=1).broadcast_to([NT, FEAT]))\
                  .then_inc(params, 16)
                store_groups(sp, k["x"], table, done, STEPS, stored)

            @block.tensor
            def _(pe):
                pe.sem_inc(turned, LEAD)
                for g, s in groups(pe):
                    pe.wait_ge(copied, g + 1)
                    pe.wait_ge(done, g * STEPS + 1)
                    for q in range(GROUP):
                        mm = pe.matmul(agg_ps[s][:, q * FEAT:(q + 1) * FEAT], sums[s][:, q, :],
                                       k["ident"][0:FEAT, 0:FEAT], start=True, stop=True)
                    mm.then_inc(turned, 1)

            @block.scalar
            def _(act):
                def copies(g, s):
                    return nc.scalar.activation(sums[s][:, :, :], acc_columns(k, FEAT, 0, g), ACT.Copy)

                copies(0, 0).then_inc(copied, 1)
                for g, s in groups(act):
                    act.wait_ge(turned, g - 1 + 1 + LEAD)
                    copies(next_group(g), 1 - s).then_inc(copied, 1)
                    act.wait_ge(done, (g + LEAD) * STEPS + VAR)
                    root_of_variance(nc, k, b).then_inc(root_ready, 1)

            @block.vector
            def _(dve):
                dve.sem_inc(done, LEAD * STEPS)
                dve.wait_ge(params, 16)
                for g, s in groups(dve):
                    step = Steps(dve, done, STEPS, g)
                    step.wait(0)
                    wide = [NT, GROUP, FEAT]
                    x, u, dinv = (of_group(k[n], g) for n in ("x", "u", "dinv"))
                    dve.wait_ge(turned, g + 1 + LEAD)
                    agg = agg_ps[s][:, 0:GROUP * FEAT].rearrange("p (q f) -> p q f", q=GROUP)
                    step.wait(step(dve.tensor_tensor(z[:, :, :], agg, u, ALU.add)))
                    step.wait(step(dve.tensor_tensor(z[:, :, :], z[:, :, :], dinv[:, :, None].broadcast_to(wide), ALU.mult)))
                    step.wait(step(dve.tensor_tensor(z[:, :, :], z[:, :, :], bias[:, None, :].broadcast_to(wide), ALU.add)))
                    step.wait(step(dve.scalar_tensor_tensor(b["y"][:, :, :], z[:, :, :], 0.0, x, ALU.max, ALU.add)))
                    normalise(step, dve, b, x, root_ready, g)


def kernel(**inputs):
    import concourse.bacc as bacc
    from concourse.bass_utils import run_bass_kernel_spmd

    v = {n: np.asarray(x) for n, x in inputs.items()}
    coef, mix = coupling_layout(v["L1_gnn_W"])
    dst = np.concatenate([v["dst"], np.full(BLOCKS * BLOCK - EDGES, -1, v["dst"].dtype)])
    arrays = {
        "x": v["x"], "dst": v["dst"],
        "dst_lanes": np.ascontiguousarray(dst.reshape(BLOCKS * TILES, P).T),
        "src_blocks": edge_order(v["src"]),
        "sh4": edge_order(v["edge_attr_4"]),
        "sh9": edge_order(np.concatenate([v["edge_weight1"], v["edge_attr_3"], v["edge_attr_5"]], 1)),
        "ef32": edge_major(v["edge_attr_32"]), "ef8": half_rows(edge_major(v["edge_attr_8"])),
        "L0_self": irrep_blocks(v["L0_gnn_si_w0"], v["L0_gnn_si_w1"]),
        "L3_self": irrep_blocks(v["L3_gnn_Ws"], v["L3_gnn_Wv"]),
        "sum_columns": message_sums(),
        "L1_mix": mix, "L1_coef": coef,
        "L0_gnn_W2": path_columns(v["L0_gnn_W2"], (3, 0, 1, 2)),
        "L0_gnn_b2": path_columns(v["L0_gnn_b2"][None], (3, 0, 1, 2))[0],
        "L3_gnn_W3": path_columns(v["L3_gnn_W3"], (1, 0, 2, 3)),
        "L3_gnn_b3": path_columns(v["L3_gnn_b3"][None], (1, 0, 2, 3))[0],
    }
    for n in ("L0_gnn_W1", "L0_gnn_b1", "L2_gnn_W1", "L2_gnn_b1", "L2_gnn_W2", "L2_gnn_b2",
              "L3_gnn_W1", "L3_gnn_b1", "L3_gnn_W2", "L3_gnn_b2"):
        arrays[n] = v[n]
    nc = bacc.Bacc("TRN2", target_bir_lowering=False, num_devices=1)
    aps = {n: nc.dram_tensor(f"in_{n}", x.shape, mybir.dt.from_np(x.dtype), kind="ExternalInput").ap()
           for n, x in arrays.items()}
    out = nc.dram_tensor("out", [NODES, FEAT], F32, kind="ExternalOutput").ap()
    build(nc, aps, out)
    r = run_bass_kernel_spmd(nc, [{f"in_{n}": x for n, x in arrays.items()}], core_ids=[0])
    return r.results[0]["out"]
```
